# Optimizing a Trainium2 kernel written in Bass

```python
import numpy as np
import jax
import jax.numpy as jnp

def _softmax(x, axis=-1):
    return jax.nn.softmax(x, axis=axis)

def _gelu(x):
    return jax.nn.gelu(x, approximate=True)

def _silu(x):
    return jax.nn.silu(x)

def _sigmoid(x):
    return jax.nn.sigmoid(x)

def _layernorm(x, axis=-1, eps=1e-05):
    m = jnp.mean(x, axis=axis, keepdims=True)
    v = jnp.var(x, axis=axis, keepdims=True)
    return (x - m) / jnp.sqrt(v + eps)

def _scatter_add(tgt, idx, src, axis=0):
    return tgt.at[idx].add(src)

def _segment_sum(src, seg, n):
    return jax.ops.segment_sum(src, seg, n)
kernel_name = 'mk_perceiver_d2_seqx_r4_20472c'

def setup_inputs(seed: int=0):
    np.random.seed(seed)
    _w = jnp.asarray

    def _rec_inputs():
        import jax
        import jax.numpy as jnp
        _rk = jax.random.key(seed)
        x = -0.0002928 + 1 * jax.random.normal(jax.random.fold_in(_rk, 1), (8, 64, 256), jnp.float32)
        _lenS = 64 - jax.random.randint(jax.random.fold_in(_rk, 7), (8,), 0, max(1, 64 // 4) + 1, jnp.int32)
        _lenS2 = 1024 - jax.random.randint(jax.random.fold_in(_rk, 8), (8,), 0, max(1, 1024 // 4) + 1, jnp.int32)
        _ctx_1024P = jax.random.normal(jax.random.fold_in(_rk, 11), (8, 16, 256), jnp.float32)
        _ctx_1024c = jax.random.dirichlet(jax.random.fold_in(_rk, 511), 0.3 * jnp.ones((16,), jnp.float32), (8, 1024))
        _ctx_1024t = jnp.einsum('bsk,bkd->bsd', _ctx_1024c, _ctx_1024P)
        _ctx_1024t = _ctx_1024t * jax.lax.rsqrt(jnp.mean(jnp.square(_ctx_1024t)) + 1e-12) * 0.953939
        ctx_1024 = -1.39393e-06 + 0.999914 * (_ctx_1024t + 0.3 * jax.random.normal(jax.random.fold_in(_rk, 611), (8, 1024, 256), jnp.float32))
        _validS = jnp.arange(64)[None, :] < _lenS[:, None]
        _validS2 = jnp.arange(1024)[None, :] < _lenS2[:, None]
        _causal = jnp.tril(jnp.ones((64, 64), dtype=bool))
        mask_BxSxS2_ik1 = jnp.where(jnp.broadcast_to(_validS2[:, None, :], (8, 64, 1024)), 1, 0).astype(jnp.int32)
        return (x, ctx_1024, mask_BxSxS2_ik1)
    x, ctx_1024, mask_BxSxS2_ik1 = _rec_inputs()

    def _L0_xattn_setup():
        import jax, jax.numpy as jnp
        import numpy as np
        D_MODEL = 256
        N_HEADS = 16
        D_K = D_MODEL // N_HEADS

        def _xavier(key, shape):
            fan_in, fan_out = (shape[1], shape[0])
            a = float(np.sqrt(6.0 / (fan_in + fan_out)))
            return jax.random.uniform(key, shape, jnp.float32, -a, a)
        key = jax.random.key(seed)
        ks = jax.random.split(key, 7)
        B, S = (2, 512)
        return {'query': jax.random.normal(ks[0], (B, S, D_MODEL), jnp.float32), 'key': jax.random.normal(ks[1], (B, S, D_MODEL), jnp.float32), 'value': jax.random.normal(ks[2], (B, S, D_MODEL), jnp.float32), 'w_q': _xavier(ks[3], (D_MODEL, D_MODEL)), 'w_k': _xavier(ks[4], (D_MODEL, D_MODEL)), 'w_v': _xavier(ks[5], (D_MODEL, D_MODEL)), 'w_o': _xavier(ks[6], (D_MODEL, D_MODEL)), 'b_q': jnp.zeros((D_MODEL,), jnp.float32), 'b_k': jnp.zeros((D_MODEL,), jnp.float32), 'b_v': jnp.zeros((D_MODEL,), jnp.float32), 'b_o': jnp.zeros((D_MODEL,), jnp.float32)}
    _L0_xattn_all = _L0_xattn_setup()
    _L0_xattn_in = {k: v for k, v in _L0_xattn_all.items() if k in ('w_q', 'w_k', 'w_v', 'w_o', 'b_q', 'b_k', 'b_v', 'b_o')}
    del _L0_xattn_all

    def _L0_attn_setup():
        import jax, jax.numpy as jnp
        import numpy as np
        SEQ_LEN, BATCH, H, N = (1024, 8, 256, 16)

        def _to_c(t):
            return t[..., 0] + 1j * t[..., 1]

        def _s4_kernel(log_dt, inv_w_real, w_imaginary, B, P, C, L):
            dt = jnp.exp(log_dt)
            w = (-jnp.exp(inv_w_real) + 1j * w_imaginary) * dt
            Bc = _to_c(B)
            Cc = _to_c(C)
            Pc = _to_c(P)
            Qc = jnp.conj(Pc)
            Bcat = jnp.concatenate([Bc[None], Pc], axis=0)
            Ccat = jnp.concatenate([Cc[None], Qc], axis=0)
            v = Bcat[:, None] * Ccat[None]
            M = L // 2 + 1
            omega = jnp.exp(-2j * jnp.pi / L * jnp.arange(M)).astype(jnp.complex64)
            z = 2 * (1 - omega) / (1 + omega)
            cauchy = 1.0 / (z[None, None, :] - w[:, :, None])
            r = jnp.einsum('abhn,hnm->abhm', v, cauchy)
            r = r * dt[None, None]
            k_f = r[:1, :1] - r[:1, 1:] * r[1:, :1] / (1 + r[1:, 1:])
            k_f = k_f * 2 / (1 + omega)
            k = jnp.fft.irfft(k_f, n=L, axis=-1)[..., :L]
            return k[0, 0]
        key = jax.random.key(seed)
        ks = jax.random.split(key, 8)
        H_, N_ = (H, N)
        x = jax.random.normal(ks[0], (SEQ_LEN, BATCH, H_), dtype=jnp.float32)
        log_dt = jax.random.normal(ks[1], (H_, 1), dtype=jnp.float32) * 0.5 - 4.6
        inv_w_real = jax.random.normal(ks[2], (H_, N_), dtype=jnp.float32)
        w_imaginary = jax.random.normal(ks[3], (H_, N_), dtype=jnp.float32)
        B = jax.random.normal(ks[4], (H_, N_, 2), dtype=jnp.float32)
        P = jax.random.normal(ks[5], (1, H_, N_, 2), dtype=jnp.float32)
        C = jax.random.normal(ks[6], (H_, N_, 2), dtype=jnp.float32)
        D = jax.random.normal(ks[7], (H_,), dtype=jnp.float32)
        return {'x': x, 'log_dt': log_dt, 'inv_w_real': inv_w_real, 'w_imaginary': w_imaginary, 'B': B, 'P': P, 'C': C, 'D': D}
    _L0_attn_all = _L0_attn_setup()
    _L0_attn_in = {k: v for k, v in _L0_attn_all.items() if k in ('log_dt', 'inv_w_real', 'w_imaginary', 'B', 'P', 'C', 'D')}
    del _L0_attn_all

    def _L0_ffn_setup():
        import jax, jax.numpy as jnp
        import numpy as np
        B, L, D = (4, 128, 256)
        E, TOP_K = (16, 4)
        F = 4 * D
        key = jax.random.key(seed)
        ks = jax.random.split(key, 6)
        scale = 0.02
        return {'x': jax.random.normal(ks[0], (B, L, D), jnp.float32), 'keys': jax.random.normal(ks[1], (E, D), jnp.float32), 'w1': jax.random.normal(ks[2], (E, F, D), jnp.float32) * scale, 'b1': jnp.zeros((E, F), jnp.float32), 'w2': jax.random.normal(ks[3], (E, D, F), jnp.float32) * scale, 'b2': jnp.zeros((E, D), jnp.float32), 'rw': jax.random.normal(ks[4], (E, D), jnp.float32) * scale, 'rb': jnp.zeros((E,), jnp.float32)}
    _L0_ffn_all = _L0_ffn_setup()
    _L0_ffn_in = {k: v for k, v in _L0_ffn_all.items() if k in ('keys', 'w1', 'b1', 'w2', 'b2', 'rw', 'rb')}
    del _L0_ffn_all

    def _L1_xattn_setup():
        import jax, jax.numpy as jnp
        import numpy as np
        NEG = -9000000000000000.0
        EPS = 1e-05
        key = jax.random.key(seed)
        k1, k2, k3, k4 = jax.random.split(key, 4)
        B, S, D = (4, 512, 256)
        q = jax.random.normal(k1, (B, S, D), dtype=jnp.float32)
        k = jax.random.normal(k2, (B, S, D), dtype=jnp.float32)
        v = jax.random.normal(k3, (B, S, D), dtype=jnp.float32)
        mask = jax.random.randint(k4, (B, S, S), 0, 2, dtype=jnp.int32)
        gamma = jnp.ones((D,), dtype=jnp.float32)
        beta = jnp.zeros((D,), dtype=jnp.float32)
        return {'q': q, 'k': k, 'v': v, 'mask': mask, 'gamma': gamma, 'beta': beta}
    _L1_xattn_all = _L1_xattn_setup()
    _L1_xattn_in = {k: v for k, v in _L1_xattn_all.items() if k in ('gamma', 'beta')}
    del _L1_xattn_all

    def _L1_attn_setup():
        import jax, jax.numpy as jnp
        import numpy as np
        D_INPUT, D_MODEL, D_STATE, D_DISCR, KER = (256, 512, 16, 128, 4)

        def _mamba_fwd(seq, W_in, W_out, W_sB, W_sC, W_sD1, W_sD2, conv_w, conv_b, A_param, D_param):
            b, l, _ = seq.shape
            ab = seq @ W_in.T
            a, g = jnp.split(ab, 2, axis=-1)
            x = jnp.swapaxes(a, 1, 2)
            y = jax.lax.conv_general_dilated(x, conv_w, window_strides=(1,), padding=[(KER - 1, 0)], dimension_numbers=('NCH', 'OIH', 'NCH'), feature_group_count=D_MODEL)
            y = y + conv_b[None, :, None]
            a = jax.nn.silu(jnp.swapaxes(y, 1, 2))
            B = a @ W_sB.T
            C = a @ W_sC.T
            s_delta = jax.nn.softplus(D_param + a @ W_sD1.T @ W_sD2.T)
            expA = jnp.exp(-A_param)
            A_bar = expA[None, None] * s_delta[..., None]
            X_bar = B[:, :, None, :] * s_delta[..., None] * a[..., None]
            A_t = jnp.moveaxis(A_bar, 1, 0)
            X_t = jnp.moveaxis(X_bar, 1, 0)
            h0 = jnp.zeros((b, D_MODEL, D_STATE), dtype=seq.dtype)

            def step(h, ax):
                At, Xt = ax
                h = At * h + Xt
                return (h, h)
            _, hid = jax.lax.scan(step, h0, (A_t, X_t))
            out_ssm = jnp.einsum('lbds,lbs->lbd', hid, jnp.moveaxis(C, 1, 0))
            out_ssm = jnp.moveaxis(out_ssm, 0, 1) + D_param * a
            out = out_ssm * jax.nn.silu(g) @ W_out.T
            return out
        key = jax.random.key(seed)
        ks = jax.random.split(key, 10)
        sc = lambda fan_in: 1.0 / np.sqrt(fan_in)
        seq = jax.random.normal(ks[0], (2, 256, D_INPUT), dtype=jnp.float32)
        W_in = jax.random.uniform(ks[1], (2 * D_MODEL, D_INPUT), jnp.float32, -sc(D_INPUT), sc(D_INPUT))
        W_out = jax.random.uniform(ks[2], (D_INPUT, D_MODEL), jnp.float32, -sc(D_MODEL), sc(D_MODEL))
        W_sB = jax.random.uniform(ks[3], (D_STATE, D_MODEL), jnp.float32, -sc(D_MODEL), sc(D_MODEL))
        W_sC = jax.random.uniform(ks[4], (D_STATE, D_MODEL), jnp.float32, -sc(D_MODEL), sc(D_MODEL))
        W_sD1 = jax.random.uniform(ks[5], (D_DISCR, D_MODEL), jnp.float32, -sc(D_MODEL), sc(D_MODEL))
        W_sD2 = jax.random.uniform(ks[6], (D_MODEL, D_DISCR), jnp.float32, -sc(D_DISCR), sc(D_DISCR))
        conv_w = jax.random.uniform(ks[7], (D_MODEL, 1, KER), jnp.float32, -sc(KER), sc(KER))
        conv_b = jax.random.uniform(ks[8], (D_MODEL,), jnp.float32, -sc(KER), sc(KER))
        A_param = jnp.tile(jnp.arange(1, D_STATE + 1, dtype=jnp.float32), (D_MODEL, 1))
        D_param = jnp.ones((D_MODEL,), dtype=jnp.float32)
        return dict(seq=seq, W_in=W_in, W_out=W_out, W_sB=W_sB, W_sC=W_sC, W_sD1=W_sD1, W_sD2=W_sD2, conv_w=conv_w, conv_b=conv_b, A_param=A_param, D_param=D_param)
    _L1_attn_all = _L1_attn_setup()
    _L1_attn_in = {k: v for k, v in _L1_attn_all.items() if k in ('W_in', 'W_out', 'W_sB', 'W_sC', 'W_sD1', 'W_sD2', 'conv_w', 'conv_b', 'A_param', 'D_param')}
    del _L1_attn_all

    def _L1_ffn_setup():
        import jax, jax.numpy as jnp
        import numpy as np
        DIM = 256
        INTER = 128
        E = 8
        TOP_K = 2
        ROUTE_SCALE = 1.0
        key = jax.random.key(seed)
        ks = jax.random.split(key, 8)
        s_d = 1.0 / np.sqrt(DIM)
        s_f = 1.0 / np.sqrt(INTER)
        x = jax.random.normal(ks[0], (2, 512, DIM), dtype=jnp.float32)
        gate_w = jax.random.uniform(ks[1], (E, DIM), jnp.float32, -s_d, s_d)
        wg = jax.random.uniform(ks[2], (E, INTER, DIM), jnp.float32, -s_d, s_d)
        wu = jax.random.uniform(ks[3], (E, INTER, DIM), jnp.float32, -s_d, s_d)
        wd = jax.random.uniform(ks[4], (E, DIM, INTER), jnp.float32, -s_f, s_f)
        sg = jax.random.uniform(ks[5], (INTER, DIM), jnp.float32, -s_d, s_d)
        su = jax.random.uniform(ks[6], (INTER, DIM), jnp.float32, -s_d, s_d)
        sd = jax.random.uniform(ks[7], (DIM, INTER), jnp.float32, -s_f, s_f)
        return {'x': x, 'gate_w': gate_w, 'wg': wg, 'wu': wu, 'wd': wd, 'sg': sg, 'su': su, 'sd': sd}
    _L1_ffn_all = _L1_ffn_setup()
    _L1_ffn_in = {k: v for k, v in _L1_ffn_all.items() if k in ('gate_w', 'wg', 'wu', 'wd', 'sg', 'su', 'sd')}
    del _L1_ffn_all
    return {'x': x, 'ctx_1024': ctx_1024, 'mask_BxSxS2_ik1': mask_BxSxS2_ik1, 'L0_xattn_w_q': _L0_xattn_in['w_q'], 'L0_xattn_w_k': _L0_xattn_in['w_k'], 'L0_xattn_w_v': _L0_xattn_in['w_v'], 'L0_xattn_w_o': _L0_xattn_in['w_o'], 'L0_xattn_b_q': _L0_xattn_in['b_q'], 'L0_xattn_b_k': _L0_xattn_in['b_k'], 'L0_xattn_b_v': _L0_xattn_in['b_v'], 'L0_xattn_b_o': _L0_xattn_in['b_o'], 'L0_attn_log_dt': _L0_attn_in['log_dt'], 'L0_attn_inv_w_real': _L0_attn_in['inv_w_real'], 'L0_attn_w_imaginary': _L0_attn_in['w_imaginary'], 'L0_attn_B': _L0_attn_in['B'], 'L0_attn_P': _L0_attn_in['P'], 'L0_attn_C': _L0_attn_in['C'], 'L0_attn_D': _L0_attn_in['D'], 'L0_ffn_keys': _L0_ffn_in['keys'], 'L0_ffn_w1': _L0_ffn_in['w1'], 'L0_ffn_b1': _L0_ffn_in['b1'], 'L0_ffn_w2': _L0_ffn_in['w2'], 'L0_ffn_b2': _L0_ffn_in['b2'], 'L0_ffn_rw': _L0_ffn_in['rw'], 'L0_ffn_rb': _L0_ffn_in['rb'], 'L1_xattn_gamma': _L1_xattn_in['gamma'], 'L1_xattn_beta': _L1_xattn_in['beta'], 'L1_attn_W_in': _L1_attn_in['W_in'], 'L1_attn_W_out': _L1_attn_in['W_out'], 'L1_attn_W_sB': _L1_attn_in['W_sB'], 'L1_attn_W_sC': _L1_attn_in['W_sC'], 'L1_attn_W_sD1': _L1_attn_in['W_sD1'], 'L1_attn_W_sD2': _L1_attn_in['W_sD2'], 'L1_attn_conv_w': _L1_attn_in['conv_w'], 'L1_attn_conv_b': _L1_attn_in['conv_b'], 'L1_attn_A_param': _L1_attn_in['A_param'], 'L1_attn_D_param': _L1_attn_in['D_param'], 'L1_ffn_gate_w': _L1_ffn_in['gate_w'], 'L1_ffn_wg': _L1_ffn_in['wg'], 'L1_ffn_wu': _L1_ffn_in['wu'], 'L1_ffn_wd': _L1_ffn_in['wd'], 'L1_ffn_sg': _L1_ffn_in['sg'], 'L1_ffn_su': _L1_ffn_in['su'], 'L1_ffn_sd': _L1_ffn_in['sd']}

def reference(x, ctx_1024, mask_BxSxS2_ik1, L0_xattn_w_q, L0_xattn_w_k, L0_xattn_w_v, L0_xattn_w_o, L0_xattn_b_q, L0_xattn_b_k, L0_xattn_b_v, L0_xattn_b_o, L0_attn_log_dt, L0_attn_inv_w_real, L0_attn_w_imaginary, L0_attn_B, L0_attn_P, L0_attn_C, L0_attn_D, L0_ffn_keys, L0_ffn_w1, L0_ffn_b1, L0_ffn_w2, L0_ffn_b2, L0_ffn_rw, L0_ffn_rb, L1_xattn_gamma, L1_xattn_beta, L1_attn_W_in, L1_attn_W_out, L1_attn_W_sB, L1_attn_W_sC, L1_attn_W_sD1, L1_attn_W_sD2, L1_attn_conv_w, L1_attn_conv_b, L1_attn_A_param, L1_attn_D_param, L1_ffn_gate_w, L1_ffn_wg, L1_ffn_wu, L1_ffn_wd, L1_ffn_sg, L1_ffn_su, L1_ffn_sd):
    import jax
    import jax.numpy as jnp

    def _L0_xattn_ref(query, key, value, w_q, w_k, w_v, w_o, b_q, b_k, b_v, b_o):
        import jax, jax.numpy as jnp
        import numpy as np
        D_MODEL = 256
        N_HEADS = 16
        D_K = D_MODEL // N_HEADS

        def _xavier(key, shape):
            fan_in, fan_out = (shape[1], shape[0])
            a = float(np.sqrt(6.0 / (fan_in + fan_out)))
            return jax.random.uniform(key, shape, jnp.float32, -a, a)
        B = query.shape[0]
        scale = jnp.sqrt(jnp.asarray(D_K, query.dtype))

        def split_heads(x):
            return x.reshape(B, -1, N_HEADS, D_K).transpose(0, 2, 1, 3)
        q = split_heads(query @ w_q.T + b_q)
        k = split_heads(key @ w_k.T + b_k)
        v = split_heads(value @ w_v.T + b_v)
        scores = jnp.einsum('bhqd,bhkd->bhqk', q, k) / scale
        attn = jax.nn.softmax(scores, axis=-1)
        ctx = jnp.einsum('bhqk,bhkd->bhqd', attn, v)
        ctx = ctx.transpose(0, 2, 1, 3).reshape(B, -1, D_MODEL)
        out = ctx @ w_o.T + b_o
        return out

    def _L0_attn_ref(x, log_dt, inv_w_real, w_imaginary, B, P, C, D):
        import jax, jax.numpy as jnp
        import numpy as np
        SEQ_LEN, BATCH, H, N = (1024, 8, 256, 16)

        def _to_c(t):
            return t[..., 0] + 1j * t[..., 1]

        def _s4_kernel(log_dt, inv_w_real, w_imaginary, B, P, C, L):
            dt = jnp.exp(log_dt)
            w = (-jnp.exp(inv_w_real) + 1j * w_imaginary) * dt
            Bc = _to_c(B)
            Cc = _to_c(C)
            Pc = _to_c(P)
            Qc = jnp.conj(Pc)
            Bcat = jnp.concatenate([Bc[None], Pc], axis=0)
            Ccat = jnp.concatenate([Cc[None], Qc], axis=0)
            v = Bcat[:, None] * Ccat[None]
            M = L // 2 + 1
            omega = jnp.exp(-2j * jnp.pi / L * jnp.arange(M)).astype(jnp.complex64)
            z = 2 * (1 - omega) / (1 + omega)
            cauchy = 1.0 / (z[None, None, :] - w[:, :, None])
            r = jnp.einsum('abhn,hnm->abhm', v, cauchy)
            r = r * dt[None, None]
            k_f = r[:1, :1] - r[:1, 1:] * r[1:, :1] / (1 + r[1:, 1:])
            k_f = k_f * 2 / (1 + omega)
            k = jnp.fft.irfft(k_f, n=L, axis=-1)[..., :L]
            return k[0, 0]
        L = x.shape[0]
        residual = x * D
        xc = jnp.transpose(x, (1, 2, 0))
        k = _s4_kernel(log_dt, inv_w_real, w_imaginary, B, P, C, L)
        n = 2 * L
        k_f = jnp.fft.rfft(k, n=n, axis=-1)
        x_f = jnp.fft.rfft(xc, n=n, axis=-1)
        out = jnp.fft.irfft(x_f * k_f, n=n, axis=-1)[..., :L]
        out = jax.nn.silu(jnp.transpose(out, (2, 0, 1)) + residual)
        return out

    def _L0_ffn_ref(x, keys, w1, b1, w2, b2, rw, rb):
        import jax, jax.numpy as jnp
        import numpy as np
        B, L, D = (4, 128, 256)
        E, TOP_K = (16, 4)
        F = 4 * D
        diff = x[:, :, None, :] - keys
        dist2 = jnp.sum(diff * diff, axis=-1)
        logits = -dist2 + jnp.einsum('bld,ed->ble', x, rw) + rb
        topv, topi = jax.lax.top_k(logits, TOP_K)
        w = jax.nn.softmax(topv, axis=-1)
        hidden = jax.nn.gelu(jnp.einsum('bld,efd->blef', x, w1) + b1, approximate=False)
        exp_out = jnp.einsum('blef,edf->bled', hidden, w2) + b2
        sel = jnp.take_along_axis(exp_out, topi[..., None], axis=2)
        fused = jnp.sum(w[..., None] * sel, axis=2)
        return fused

    def _L1_xattn_ref(q, k, v, mask, gamma, beta):
        import jax, jax.numpy as jnp
        import numpy as np
        NEG = -9000000000000000.0
        EPS = 1e-05
        d_k = q.shape[-1]
        logits = jnp.einsum('bsd,btd->bst', q, k) / jnp.sqrt(jnp.asarray(d_k, q.dtype))
        logits = jnp.where(mask == 0, jnp.asarray(NEG, logits.dtype), logits)
        attn = jax.nn.softmax(logits, axis=-1)
        x = jnp.einsum('bst,btd->bsd', attn, v)
        mu = jnp.mean(x, axis=-1, keepdims=True)
        var = jnp.mean(jnp.square(x - mu), axis=-1, keepdims=True)
        xhat = (x - mu) * jax.lax.rsqrt(var + EPS)
        return xhat * gamma + beta

    def _L1_attn_ref(seq, W_in, W_out, W_sB, W_sC, W_sD1, W_sD2, conv_w, conv_b, A_param, D_param):
        import jax, jax.numpy as jnp
        import numpy as np
        D_INPUT, D_MODEL, D_STATE, D_DISCR, KER = (256, 512, 16, 128, 4)

        def _mamba_fwd(seq, W_in, W_out, W_sB, W_sC, W_sD1, W_sD2, conv_w, conv_b, A_param, D_param):
            b, l, _ = seq.shape
            ab = seq @ W_in.T
            a, g = jnp.split(ab, 2, axis=-1)
            x = jnp.swapaxes(a, 1, 2)
            y = jax.lax.conv_general_dilated(x, conv_w, window_strides=(1,), padding=[(KER - 1, 0)], dimension_numbers=('NCH', 'OIH', 'NCH'), feature_group_count=D_MODEL)
            y = y + conv_b[None, :, None]
            a = jax.nn.silu(jnp.swapaxes(y, 1, 2))
            B = a @ W_sB.T
            C = a @ W_sC.T
            s_delta = jax.nn.softplus(D_param + a @ W_sD1.T @ W_sD2.T)
            expA = jnp.exp(-A_param)
            A_bar = expA[None, None] * s_delta[..., None]
            X_bar = B[:, :, None, :] * s_delta[..., None] * a[..., None]
            A_t = jnp.moveaxis(A_bar, 1, 0)
            X_t = jnp.moveaxis(X_bar, 1, 0)
            h0 = jnp.zeros((b, D_MODEL, D_STATE), dtype=seq.dtype)

            def step(h, ax):
                At, Xt = ax
                h = At * h + Xt
                return (h, h)
            _, hid = jax.lax.scan(step, h0, (A_t, X_t))
            out_ssm = jnp.einsum('lbds,lbs->lbd', hid, jnp.moveaxis(C, 1, 0))
            out_ssm = jnp.moveaxis(out_ssm, 0, 1) + D_param * a
            out = out_ssm * jax.nn.silu(g) @ W_out.T
            return out
        return _mamba_fwd(seq, W_in, W_out, W_sB, W_sC, W_sD1, W_sD2, conv_w, conv_b, A_param, D_param)

    def _L1_ffn_ref(x, gate_w, wg, wu, wd, sg, su, sd):
        import jax, jax.numpy as jnp
        import numpy as np
        DIM = 256
        INTER = 128
        E = 8
        TOP_K = 2
        ROUTE_SCALE = 1.0
        B, S, D = x.shape
        xf = x.reshape(-1, D)
        N = xf.shape[0]
        scores = jax.nn.softmax(xf @ gate_w.T, axis=-1)
        _, idx = jax.lax.top_k(scores, TOP_K)
        weights = jnp.take_along_axis(scores, idx, axis=-1) * ROUTE_SCALE
        cw = jnp.zeros((N, E), dtype=xf.dtype)
        cw = cw.at[jnp.arange(N)[:, None], idx].add(weights)
        g = jnp.einsum('nd,efd->nef', xf, wg)
        u = jnp.einsum('nd,efd->nef', xf, wu)
        h = jax.nn.silu(g) * u
        y = jnp.einsum('nef,edf->ned', h, wd)
        routed = jnp.einsum('ned,ne->nd', y, cw)
        shared = jax.nn.silu(xf @ sg.T) * (xf @ su.T) @ sd.T
        return (routed + shared).reshape(B, S, D)
    x = x + _L0_xattn_ref(_layernorm(x, axis=-1), ctx_1024, ctx_1024, L0_xattn_w_q, L0_xattn_w_k, L0_xattn_w_v, L0_xattn_w_o, L0_xattn_b_q, L0_xattn_b_k, L0_xattn_b_v, L0_xattn_b_o)
    x = x + _L0_attn_ref(_layernorm(x, axis=-1), L0_attn_log_dt, L0_attn_inv_w_real, L0_attn_w_imaginary, L0_attn_B, L0_attn_P, L0_attn_C, L0_attn_D)
    x = x + _L0_ffn_ref(_layernorm(x, axis=-1), L0_ffn_keys, L0_ffn_w1, L0_ffn_b1, L0_ffn_w2, L0_ffn_b2, L0_ffn_rw, L0_ffn_rb)
    x = x + _L1_xattn_ref(_layernorm(x, axis=-1), ctx_1024, ctx_1024, mask_BxSxS2_ik1, L1_xattn_gamma, L1_xattn_beta)
    x = x + _L1_attn_ref(_layernorm(x, axis=-1), L1_attn_W_in, L1_attn_W_out, L1_attn_W_sB, L1_attn_W_sC, L1_attn_W_sD1, L1_attn_W_sD2, L1_attn_conv_w, L1_attn_conv_b, L1_attn_A_param, L1_attn_D_param)
    x = x + _L1_ffn_ref(_layernorm(x, axis=-1), L1_ffn_gate_w, L1_ffn_wg, L1_ffn_wu, L1_ffn_wd, L1_ffn_sg, L1_ffn_su, L1_ffn_sd)
    return x

_drawn_inputs = setup_inputs


def setup_inputs(seed=0):
    import zlib

    import numpy as np

    out = dict(_drawn_inputs(seed))
    spreads = {'L0_xattn_b_q': (0.0, 0.1),
     'L0_xattn_b_k': (0.0, 0.1),
     'L0_xattn_b_v': (0.0, 0.1),
     'L0_xattn_b_o': (0.0, 0.1),
     'L0_ffn_b1': (0.0, 0.1),
     'L0_ffn_b2': (0.0, 0.1),
     'L0_ffn_rb': (0.0, 0.1),
     'L1_xattn_gamma': (1.0, 0.2),
     'L1_xattn_beta': (0.0, 0.1),
     'L1_attn_D_param': (1.0, 0.2)}
    factors = {}
    for name, (base, spread) in spreads.items():
        noise = np.random.default_rng([zlib.crc32(name.encode()), seed]).standard_normal(out[name].shape)
        drawn = base * np.exp(spread * noise) if base else spread * noise
        out[name] = jnp.asarray(drawn.astype(out[name].dtype))
    for name, factor in factors.items():
        out[name] = (out[name] * factor).astype(out[name].dtype)
    return out
```

```python
from contextlib import ExitStack

import concourse.bass as bass
import numpy as np
from concourse import mybir

F32 = mybir.dt.float32
F32R = mybir.dt.float32r
I32 = mybir.dt.int32
ACT = mybir.ActivationFunctionType
ALU = mybir.AluOpType
AX = mybir.AxisListType

P = 128
B, S, D = 8, 64, 256
KEYS = 1024
TOK = B * S
TC = TOK // P
DC = D // P
KC = KEYS // P
HEADS, DH = 16, 16
HPC = HEADS // DC
PAIRS = HPC // 2
EPS = 1e-5
NSTATE, MODES = 16, 5
E0, TOP0, F0 = 16, 4, 1024
FC = F0 // P
E1, TOP1 = 9, 2
ROUTED1 = E1 - 1
DI, DISCR, KER = 512, 128, 4
CC = DI // P
NEG = -9000000000000000.0
EW = 2 * DC * F0
QW = EW // 4
UNITS = FC
GS = 2
GROUPS = NSTATE // GS
FB = 3
LAYERS = 6
STAGE_AT, PHASE_AT, PLAN_END = 51 * 1024, 83 * 1024, 207 * 1024


def columns(widths):
    at, out = 0, {}
    for name, width in widths:
        out[name] = (at, at + width)
        at += width
    return out, at


FIRST, FIRST_W = columns([("wq", DC * D), ("bq", DC), ("wk", DC * D), ("bk", DC), ("wv", DC * D), ("bv", DC)])
TABLE, TABLE_W = columns([
    ("ident", P), ("head", HPC), ("quad", 4), ("pick", PAIRS * P), ("query", S), ("before0", E0 * E0),
    ("before1", ROUTED1 * ROUTED1), ("ar", MODES), ("ai", MODES), ("cr", MODES), ("ci", MODES),
    ("alpha", B * MODES), ("beta", B * MODES), ("ones", P), ("minus_half", TC), ("minus_one", DC * NSTATE * MODES)])
LATER, LATER_W = columns([
    ("wo", DC * D), ("log_dt", DC), ("inv_w", DC * NSTATE), ("w_im", DC * NSTATE), ("B", DC * NSTATE * 2),
    ("P", DC * NSTATE * 2), ("C", DC * NSTATE * 2), ("D", DC), ("keys", DC * E0), ("rw", DC * E0),
    ("b1", E0 * FC), ("w_in", DC * 2 * DI), ("w_sbc", CC * 2 * NSTATE), ("w_sd1", CC * DISCR), ("w_sd2", DI),
    ("conv_w", CC * KER), ("conv_b", CC), ("a_param", CC * NSTATE), ("d_param", CC), ("w_out", CC * D),
    ("gate_w", DC * ROUTED1)])
ROWS, ROWS_W = columns([("bo", D), ("gamma", D), ("beta", D), ("rb", E0)])


def part(tile, layout, name):
    a, b = layout[name]
    return tile[:, a:b]


class Order:

    def __init__(self, eng, sem):
        self.eng, self.sem, self.count = eng, sem, 0

    def mark(self, ins):
        self.count += 1
        ins.then_inc(self.sem, 1)

    def settle(self):
        self.eng.wait_ge(self.sem, self.count)

    def step(self, ins):
        self.mark(ins)
        self.settle()


def over(ap, n, axis):
    ap = ap.unsqueeze(axis)
    shape = list(ap.shape)
    shape[axis] = n
    return ap.broadcast_to(shape)


def build(nc, d, out):
    ctx = ExitStack()
    with ctx:
        names = set()

        def sem(name):
            assert name not in names
            names.add(name)
            return ctx.enter_context(nc.semaphore(name))

        base = -(-nc.sbuf_base // 64) * 64
        place = {"common": base, "stage": base + STAGE_AT, "phase": base + PHASE_AT}
        ends = {"common": place["stage"], "stage": place["phase"], "phase": base + PLAN_END}

        def sb(region, name, shape, dt=F32):
            width = int(np.prod(shape[1:])) * 4
            at = place[region]
            place[region] = at + -(-width // 64) * 64
            assert place[region] <= ends[region], (name, region, place[region] - ends[region])
            return nc.alloc_sbuf_tensor_at(name, shape, dt, offset=at)

        first = sb("common", "first", [P, FIRST_W])
        table = sb("common", "table", [P, TABLE_W])
        later = sb("common", "later", [P, LATER_W])
        rows = sb("common", "rows", [P, ROWS_W])
        b2 = sb("common", "b2", [E0, D])
        X = sb("common", "X", [P, TC, D])
        xn = sb("common", "xn", [P, TC, D])
        xnT = sb("common", "xnT", [P, DC, TOK])
        stats = sb("common", "stats", [P, TC, 6])
        moments = sb("common", "moments", [P, TC, 2])
        vareps = sb("common", "vareps", [P, TC])
        rstd = sb("common", "rstd", [P, TC])
        taps = sb("common", "taps", [P, B, DC])
        key_sum = sb("common", "key_sum", [P, DC, E0])
        key_sq = sb("common", "key_sq", [P, DC, E0])
        exp_a = sb("common", "exp_a", [P, CC * NSTATE])

        ident = part(table, TABLE, "ident")
        ones = part(table, TABLE, "ones")

        raw = [sb("stage", f"raw{k}", [P, EW]) for k in range(2)]

        top = place["phase"]
        ctxT = [sb("phase", f"ctxT{k}", [P, DC, KEYS]) for k in range(2)]
        kT = [sb("phase", f"kT{k}", [P, DC, KEYS]) for k in range(2)]
        V = [sb("phase", f"V{k}", [P, KC, D]) for k in range(2)]
        probs = [sb("phase", f"probs{k}", [P, KEYS]) for k in range(2)]
        probsT = [sb("phase", f"probsT{k}", [P, KC, PAIRS, P]) for k in range(DC)]
        qT = sb("phase", "qT", [P, DC, TOK])
        Qh = [[sb("phase", f"Qh{k}{c}", [P, HPC, S]) for c in range(DC)] for k in range(2)]
        negmax_raw = [sb("phase", f"negmax_raw{k}", [P, 1]) for k in range(2)]
        negmax = [sb("phase", f"negmax{k}", [P, 1]) for k in range(2)]
        sums = sb("phase", "sums", [P, B, HEADS // 2])
        inv_sums = sb("phase", "inv_sums", [P, B, HEADS // 2])
        spread = [sb("phase", f"spread{k}", [P, B, S]) for k in range(2)]
        own = sb("phase", "own", [P, 4, S])
        attnT = sb("phase", "attnT", [P, DC, TOK])
        s4 = {n: sb("phase", "s4_" + n, [P, DC * NSTATE]) for n in ("wr", "wi", "ew")}
        s4v = sb("phase", "s4_v", [P, 7, DC * NSTATE])
        s4t = sb("phase", "s4_t", [P, DC * NSTATE])
        s4g = [sb("phase", f"s4_g{k}", [P, MODES, DC * NSTATE]) for k in range(6)]
        s4p = sb("phase", "s4_p", [P, 8, MODES * DC, NSTATE])
        s4s = sb("phase", "s4_s", [P, 14, MODES, DC])
        s4dt = sb("phase", "s4_dt", [P, DC])
        s4l = [sb("phase", f"s4_l{k}", [P, B, DC, MODES]) for k in range(2)]

        place["phase"] = top
        conv = [sb("phase", f"conv{k}", [P, DC, TOK]) for k in range(2)]
        w_hi = [sb("phase", f"w_hi{k}", [P, EW], F32R) for k in range(2)]
        w_lo = [sb("phase", f"w_lo{k}", [P, EW], F32R) for k in range(2)]
        x_hi = sb("phase", "x_hi", [P, DC, TOK], F32R)
        x_lo = sb("phase", "x_lo", [P, DC, TOK], F32R)
        h_full = [sb("phase", f"h_full{k}", [P, TOK]) for k in range(2)]
        h_hi = [sb("phase", f"h_hi{k}", [P, TOK], F32R) for k in range(4)]
        h_lo = [sb("phase", f"h_lo{k}", [P, TOK], F32R) for k in range(4)]
        logits = sb("phase", "logits", [P, TC, E0])
        squares = sb("phase", "squares", [P, D])
        sumsq = sb("phase", "sumsq", [P, TC])
        above = sb("phase", "above", [P, TC, E0, E0])
        tied = sb("phase", "tied", [P, TC, E0, E0])
        rank = sb("phase", "rank", [P, TC, E0])
        best = sb("phase", "best", [P, TC])
        gate = sb("phase", "gate", [P, TC, E0])
        gateT = sb("phase", "gateT", [E0, TC, P])

        place["phase"] = top
        place["stage"] = base + STAGE_AT
        ctxT2 = [sb(("stage", "phase")[k], f"ctxT2{k}", [P, 2, DC, KEYS]) for k in range(2)]
        ctxN2 = [sb(("stage", "phase")[k], f"ctxN2{k}", [P, 2, KC, D]) for k in range(2)]
        mask = [sb("phase", f"mask{k}", [P, KEYS], I32) for k in range(2)]
        maskneg = [sb("phase", f"maskneg{k}", [P, KEYS]) for k in range(2)]
        masked = [sb("phase", f"masked{k}", [P, KEYS]) for k in range(2)]
        probs2 = [sb("phase", f"probs2{k}", [P, KEYS]) for k in range(2)]
        probsT2 = sb("phase", "probsT2", [P, KC, P])
        stat2 = sb("phase", "stat2", [P, TC, 4])
        mixed = sb("phase", "mixed", [P, D])

        place["phase"] = top
        place["stage"] = base + STAGE_AT
        Bbc = sb("phase", "Bbc", [P, NSTATE, TOK])
        Cbc = sb("phase", "Cbc", [P, NSTATE, TOK])
        a_pad = sb("phase", "a_pad", [P, CC, B, S + KER - 1])
        aT = sb("phase", "aT", [P, CC, TOK])
        gT = sb("phase", "gT", [P, CC, TOK])
        delta = sb("phase", "delta", [P, CC, TOK])
        drive = sb("phase", "drive", [P, CC, TOK])
        hidden = [sb("phase", f"hidden{k}", [P, GS, TOK]) for k in range(2)]
        acc = sb("phase", "acc", [P, TOK])
        bcT = sb("stage", "bcT", [P, TOK])
        lowT = sb("stage", "lowT", [P, TOK])
        soft = [sb("stage", f"soft{k}", [P, TOK]) for k in range(2)]
        decay = [sb("stage", f"decay{k}", [P, GS, TOK]) for k in range(2)]
        inject = [sb("stage", f"inject{k}", [P, GS, TOK]) for k in range(2)]
        shown = [sb("stage", f"shown{k}", [P, GS, TOK]) for k in range(2)]

        wf = [sb("phase", f"wf{k}", [P, 3 * D]) for k in range(FB)]
        place["phase"] = top
        act_f = [sb("phase", f"act_f{k}", [P, TOK]) for k in range(FB)]
        hid_f = [sb("phase", f"hid_f{k}", [P, TOK]) for k in range(FB)]
        logits1 = sb("phase", "logits1", [P, TC, ROUTED1])
        above1 = sb("phase", "above1", [P, TC, ROUTED1, ROUTED1])
        tied1 = sb("phase", "tied1", [P, TC, ROUTED1, ROUTED1])
        rank1 = sb("phase", "rank1", [P, TC, ROUTED1])
        best1 = sb("phase", "best1", [P, TC])
        gate1 = sb("phase", "gate1", [P, TC, E1])

        banks = ctx.enter_context(nc.psum_tensor("banks", [P, 8, 512], F32))

        def pb(i):
            return banks[:, i, :] if isinstance(i, int) else banks[:, bass.ds(i, 1), :].rearrange("p a n -> p (a n)")

        def two(i):
            return banks[:, 2 * i:2 * i + 2, :].rearrange("p a n -> p (a n)")

        loaded = {n: sem("loaded_" + n) for n in ("x", "first", "table", "later", "rows", "b2")}
        ctx_loaded = [sem(f"ctx_loaded{k}") for k in range(2)]
        raw_loaded = [sem(f"raw_loaded{k}") for k in range(2)]
        stored = sem("stored")
        dve_step, pool_step, act_step = sem("dve_step"), sem("pool_step"), sem("act_step")
        var_ready, rstd_ready, xn_ready = sem("var_ready"), sem("rstd_ready"), sem("xn_ready")
        xt_done, xt0_ready, xt1_ready = sem("xt_done"), sem("xt0_ready"), sem("xt1_ready")
        q_done, q_ready, heads_ready = sem("q_done"), sem("q_ready"), sem("heads_ready")
        proj_done, k_ready, v_ready = sem("proj_done"), sem("k_ready"), sem("v_ready")
        scores_done, raw_max, max_ready, exp_done = sem("scores_done"), sem("raw_max"), sem("max_ready"), sem("exp_done")
        t_done, pt0_ready, pt1_ready = sem("t_done"), sem("pt0_ready"), sem("pt1_ready")
        pv_done, masked_ready, attn_ready = sem("pv_done"), sem("masked_ready"), sem("attn_ready")
        spread_ready, inv_done, attn_scaled = sem("spread_ready"), sem("inv_done"), sem("attn_scaled")
        out_done, x_updated = sem("out_done"), sem("x_updated")
        s4_exp, taps_ready = sem("s4_exp"), sem("taps_ready")
        conv_ready, silu_ready, back_done = sem("conv_ready"), sem("silu_ready"), sem("back_done")

        hi_done, lo_done, xs_ready = sem("hi_done"), sem("lo_done"), sem("xs_ready")
        keys_ready, logits_done, ssq_ready = sem("keys_ready"), sem("logits_done"), sem("ssq_ready")
        centred, gate_exp, gate_ready = sem("centred"), sem("gate_exp"), sem("gate_ready")
        gate_turned, gateT_ready, bias_done, bias_added = (sem(n) for n in ("gate_turned", "gateT_ready", "bias_done", "bias_added"))
        up_done, gelu_done, h_hi_ready, h_ready = sem("up_done"), sem("gelu_done"), sem("h_hi_ready"), sem("h_ready")
        down_done, combined = sem("down_done"), sem("combined")
        ctxT2_loaded = [sem(f"ctxT2_loaded{k}") for k in range(2)]
        ctxN2_loaded = [sem(f"ctxN2_loaded{k}") for k in range(2)]
        mask_loaded = [sem(f"mask_loaded{k}") for k in range(2)]
        maskneg_ready, scores2_done, max2_ready, exp2_done = (
            sem(n) for n in ("maskneg_ready", "scores2_done", "max2_ready", "exp2_done"))
        turned2, left2_ready, right2_ready, mixed_done = (sem(n) for n in ("turned2", "left2_ready", "right2_ready", "mixed_done"))
        mixed_taken = sem("mixed_taken")
        expa_ready, pads_ready, ag_done, a_ready, g_ready = (sem(n) for n in ("expa_ready", "pads_ready", "ag_done", "a_ready", "g_ready"))
        conv1_ready, a_silu, bc_done, bc_ready = (sem(n) for n in ("conv1_ready", "a_silu", "bc_done", "bc_ready"))
        low_done, low_ready, step_done, abs_ready, soft_ready, drive_ready = (
            sem(n) for n in ("low_done", "low_ready", "step_done", "abs_ready", "soft_ready", "drive_ready"))
        soft_taken, relu_ready, inject_free = sem("soft_taken"), sem("relu_ready"), sem("inject_free")
        Bbc_done, Bbc_ready, Cbc_done, Cbc_ready = (sem(n) for n in ("Bbc_done", "Bbc_ready", "Cbc_done", "Cbc_ready"))
        decay_ready, inject_ready, scanned, shown_ready, shown_used, y_ready, gated_ready = (
            sem(n) for n in ("decay_ready", "inject_ready", "scanned", "shown_ready", "shown_used", "y_ready", "gated_ready"))
        out1_done = sem("out1_done")
        wf_loaded = [sem(f"wf_loaded{k}") for k in range(FB)]
        logits1_done, centred1, gate1_exp, gate1_ready = (sem(n) for n in ("logits1_done", "centred1", "gate1_exp", "gate1_ready"))
        gu_done, silu1_ready, hid_ready, down1_done, combined1 = (
            sem(n) for n in ("gu_done", "silu1_ready", "hid_ready", "down1_done", "combined1"))

        block = ctx.enter_context(nc.Block())

        @block.sync
        def _(sp):
            sp.dma_start(X[:], d["x"].rearrange("(c p) n -> p c n", p=P)).then_inc(loaded["x"], 16)
            sp.dma_start(first[:], d["first"]).then_inc(loaded["first"], 16)
            sp.dma_start(table[:], d["table"]).then_inc(loaded["table"], 16)
            for k in range(2):
                sp.dma_start(ctxT[k][:], d["ctxT"][k]).then_inc(ctx_loaded[k], 16)
            sp.dma_start(later[:], d["later"]).then_inc(loaded["later"], 16)
            sp.dma_start(rows[:], d["rows"]).then_inc(loaded["rows"], 16)
            sp.dma_start(b2[:], d["b2"]).then_inc(loaded["b2"], 16)
            for k in range(2):
                sp.dma_start(raw[k][:], d["w0"][k]).then_inc(raw_loaded[k], 16)
            with sp.Fori(0, B // 2 - 1) as n:
                for k in range(2):
                    sp.wait_ge(proj_done, 16 * n + 8 * (k + 1))
                    sp.dma_start(ctxT[k][:], d["ctxT"][bass.ds(2 * n + (2 + k), 1)].rearrange("a p c n -> p (a c) n"))\
                        .then_inc(ctx_loaded[k], 16)
            with sp.Fori(0, E0 // 2 - 1) as n:
                for k in range(2):
                    sp.wait_ge(lo_done, 8 * n + 4 * (k + 1))
                    sp.dma_start(raw[k][:], d["w0"][bass.ds(2 * n + (2 + k), 1)].rearrange("a p n -> p (a n)"))\
                        .then_inc(raw_loaded[k], 16)
            sp.wait_ge(lo_done, 4 * E0)
            for p in range(TC):
                k = p % 2
                if p == 1:
                    sp.wait_ge(x_updated, 3)
                    for m in range(2):
                        sp.dma_start(mask[m][:], d["mask"][m * P:(m + 1) * P]).then_inc(mask_loaded[m], 16)
                if p >= 2:
                    sp.wait_ge(maskneg_ready, p - 1)
                    sp.dma_start(mask[k][:], d["mask"][p * P:(p + 1) * P]).then_inc(mask_loaded[k], 16)
                    sp.wait_ge(scores2_done, p - 1)
                sp.dma_start(ctxT2[k][:], d["ctxT"][2 * p:2 * p + 2].rearrange("b p c n -> p b c n"))\
                    .then_inc(ctxT2_loaded[k], 16)
                if p >= 2:
                    sp.wait_ge(mixed_done, p - 1)
                sp.dma_start(ctxN2[k][:], d["ctxN"][2 * p:2 * p + 2].rearrange("b p k n -> p b k n"))\
                    .then_inc(ctxN2_loaded[k], 16)
            for k in range(FB):
                sp.dma_start(wf[k][:], d["w1"][k]).then_inc(wf_loaded[k], 16)
            with sp.Fori(0, E1 // FB - 1) as n:
                for k in range(FB):
                    sp.wait_ge(down1_done, FB * n + (k + 1))
                    sp.dma_start(wf[k][:], d["w1"][bass.ds(FB * n + (FB + k), 1)].rearrange("a p n -> p (a n)"))\
                        .then_inc(wf_loaded[k], 16)
            sp.wait_ge(x_updated, LAYERS)
            sp.dma_start(out.rearrange("(c p) n -> p c n", p=P), X[:]).then_inc(stored, 16)
            sp.wait_ge(stored, 16)

        @block.gpsimd
        def _(pool):
            order = Order(pool, pool_step)

            def rstd_of(k):
                pool.wait_ge(var_ready, k)
                nc.gpsimd.tensor_tensor(rstd[:], vareps[:], part(table, TABLE, "minus_half"), ALU.pow)\
                    .then_inc(rstd_ready, 1)

            def split_heads(k, b):
                for c in range(DC):
                    tok = bass.ds(b * S, S)
                    last = nc.gpsimd.tensor_tensor(
                        Qh[k][c][:], over(qT[:, c, tok], HPC, 1), over(part(table, TABLE, "head"), S, 2), ALU.mult)
                last.then_inc(heads_ready, 1)

            def filter_taps():
                N, MN = DC * NSTATE, [P, MODES, DC * NSTATE]
                mul, add, sub = ALU.mult, ALU.add, ALU.subtract

                def tt(o, a, b, op):
                    order.step(nc.gpsimd.tensor_tensor(o, a, b, op))

                def modes(name):
                    return over(part(table, TABLE, name), N, 2)

                def poles(ap):
                    return over(ap, MODES, 1)

                def by_state(ap):
                    return over(ap, NSTATE, 2)

                pool.wait_ge(s4_exp, 2)
                pool.wait_ge(loaded["later"], 16)
                w3 = {n: s4[n][:].rearrange("p (c n) -> p c n", c=DC) for n in s4}
                im3 = part(later, LATER, "w_im").rearrange("p (c n) -> p c n", c=DC)
                tt(w3["wr"], w3["ew"], by_state(s4dt[:]), mul)
                tt(w3["wi"], im3, by_state(s4dt[:]), mul)
                wr, wi = poles(s4["wr"][:]), poles(s4["wi"][:])
                g = [x[:] for x in s4g]
                tt(g[0], wr, modes("cr"), mul)
                tt(g[1], wi, modes("ci"), mul)
                tt(g[0], g[0], g[1], add)
                tt(g[0], g[0], modes("ar"), add)
                tt(g[1], wr, modes("ci"), mul)
                tt(g[2], wi, modes("cr"), mul)
                tt(g[1], g[1], g[2], sub)
                tt(g[1], g[1], modes("ai"), add)
                tt(g[2], g[0], g[0], mul)
                tt(g[3], g[1], g[1], mul)
                tt(g[2], g[2], g[3], add)
                tt(g[2], g[2], part(table, TABLE, "minus_one").rearrange("p (m n) -> p m n", m=MODES), ALU.pow)
                tt(g[3], g[0], g[2], mul)
                tt(g[4], g[1], g[2], mul)
                gr, gi = g[3], g[4]
                pair = {n: part(later, LATER, n).rearrange("p (n two) -> p n two", two=2) for n in ("B", "C", "P")}
                re = {n: pair[n][:, :, 0] for n in pair}
                im = {n: pair[n][:, :, 1] for n in pair}
                t = s4t[:]

                def both(o, a, b, e, f, op):
                    tt(o, a, b, mul)
                    tt(t, e, f, mul)
                    tt(o, o, t, op)

                both(s4v[:, 0], re["B"], re["C"], im["B"], im["C"], sub)
                both(s4v[:, 1], re["B"], im["C"], im["B"], re["C"], add)
                both(s4v[:, 2], re["B"], re["P"], im["B"], im["P"], add)
                both(s4v[:, 3], im["B"], re["P"], re["B"], im["P"], sub)
                both(s4v[:, 4], re["P"], re["C"], im["P"], im["C"], sub)
                both(s4v[:, 5], re["P"], im["C"], im["P"], re["C"], add)
                both(s4v[:, 6], re["P"], re["P"], im["P"], im["P"], add)
                prod = [s4p[:, k].rearrange("p (m c) n -> p m (c n)", m=MODES) for k in range(8)]
                for k in range(3):
                    vr, vi = poles(s4v[:, 2 * k]), poles(s4v[:, 2 * k + 1])
                    tt(prod[2 * k], vr, gr, mul)
                    tt(g[5], vi, gi, mul)
                    tt(prod[2 * k], prod[2 * k], g[5], add)
                    tt(prod[2 * k + 1], vi, gr, mul)
                    tt(g[5], vr, gi, mul)
                    tt(prod[2 * k + 1], prod[2 * k + 1], g[5], sub)
                tt(prod[6], poles(s4v[:, 6]), gr, mul)
                tt(prod[7], poles(s4v[:, 6]), gi, mul)
                flat = s4p[:].rearrange("p k m n -> p (k m) n")
                n = NSTATE // 2
                while n:
                    tt(flat[:, :, 0:n], flat[:, :, 0:n], flat[:, :, n:2 * n], add)
                    n //= 2
                Z = [s4s[:, k] for k in range(14)]
                for k in range(8):
                    tt(Z[k], s4p[:, k, :, 0].rearrange("p (m c) -> p m c", m=MODES), over(s4dt[:], MODES, 1), mul)
                cr, ci = (over(part(table, TABLE, n), DC, 2) for n in ("cr", "ci"))
                dr, di, tr, ti, u0, u1 = Z[8:14]
                tt(dr, cr, Z[6], mul)
                tt(u0, ci, Z[7], mul)
                tt(dr, dr, u0, add)
                order.step(nc.gpsimd.tensor_scalar_add(dr, dr, 1.0))
                tt(di, ci, Z[6], mul)
                tt(u0, cr, Z[7], mul)
                tt(di, di, u0, sub)
                tt(u0, Z[2], Z[4], mul)
                tt(u1, Z[3], Z[5], mul)
                tt(u0, u0, u1, sub)
                tt(u1, Z[2], Z[5], mul)
                tt(tr, Z[3], Z[4], mul)
                tt(u1, u1, tr, add)
                tt(tr, cr, u0, mul)
                tt(ti, ci, u1, mul)
                tt(tr, tr, ti, sub)
                tt(ti, cr, u1, mul)
                tt(u0, ci, u0, mul)
                tt(ti, ti, u0, add)
                tt(u0, dr, dr, mul)
                tt(u1, di, di, mul)
                tt(u0, u0, u1, add)
                one = part(table, TABLE, "minus_one")[:, 0:MODES * DC].rearrange("p (m c) -> p m c", m=MODES)
                tt(u0, u0, one, ALU.pow)
                tt(u1, tr, dr, mul)
                tt(Z[2], ti, di, mul)
                tt(u1, u1, Z[2], add)
                tt(u1, u1, u0, mul)
                tt(Z[0], Z[0], u1, sub)
                tt(u1, ti, dr, mul)
                tt(Z[2], tr, di, mul)
                tt(u1, u1, Z[2], sub)
                tt(u1, u1, u0, mul)
                tt(Z[1], Z[1], u1, sub)
                for name, k in (("alpha", 0), ("beta", 1)):
                    for c in range(DC):
                        tt(s4l[k][:, :, c, :], over(Z[k][:, :, c], B, 1),
                           part(table, TABLE, name).rearrange("p (l m) -> p l m", l=B), mul)
                tt(s4l[0][:], s4l[0][:], s4l[1][:], add)
                for m in range(1, MODES):
                    tt(s4l[0][:, :, :, 0], s4l[0][:, :, :, 0], s4l[0][:, :, :, m], add)
                order.step(nc.gpsimd.tensor_copy(taps[:], s4l[0][:, :, :, 0]))
                nc.gpsimd.tensor_tensor(taps[:, 0, :], taps[:, 0, :], part(later, LATER, "D"), add).then_inc(taps_ready, 1)

            pool.wait_ge(loaded["table"], 16)
            rstd_of(1)
            pool.wait_ge(q_ready, DC)
            for b in range(2):
                split_heads(b, b)
            filter_taps()
            with pool.Fori(0, B // 2 - 1) as n:
                for k in range(2):
                    pool.wait_ge(scores_done, 16 * n + 8 * (k + 1))
                    split_heads(k, 2 * n + (2 + k))
            pool.wait_ge(attn_ready, 2 * B + 1)
            for c in range(DC):
                for j in range(PAIRS):
                    k = PAIRS * c + j
                    if k >= 2:
                        pool.wait_ge(inv_done, k - 1)
                    nc.gpsimd.tensor_tensor(spread[k % 2][:], over(inv_sums[:, :, k], S, 2),
                                            over(part(table, TABLE, "query"), B, 1), ALU.mult).then_inc(spread_ready, 1)
            rstd_of(2)

            keys3 = part(later, LATER, "keys").rearrange("p (c e) -> p c e", c=DC)
            rw3 = part(later, LATER, "rw").rearrange("p (c e) -> p c e", c=DC)
            order.step(nc.gpsimd.tensor_tensor(key_sum[:], keys3, keys3, ALU.add))
            nc.gpsimd.tensor_tensor(key_sum[:], key_sum[:], rw3, ALU.add).then_inc(keys_ready, 1)
            order.step(nc.gpsimd.tensor_tensor(key_sq[:], keys3, keys3, ALU.mult))
            nc.gpsimd.tensor_scalar(key_sq[:], key_sq[:], -1.0, 0.0, ALU.mult, ALU.add).then_inc(keys_ready, 1)

            def split_low(e, k):
                for q in range(4):
                    cols = slice(q * QW, (q + 1) * QW)
                    pool.wait_ge(hi_done, 4 * e + (q + 1))
                    nc.gpsimd.tensor_tensor(w_lo[k][:, cols], raw[k][:, cols], w_hi[k][:, cols].bitcast(F32), ALU.subtract)\
                        .then_inc(lo_done, 1)

            split_low(0, 0)
            rstd_of(3)
            split_low(1, 1)
            with pool.Fori(0, E0 // 2 - 1) as n:
                for k in range(2):
                    split_low(2 * n + (2 + k), k)

            def mask_term(p):
                k = p % 2
                pool.wait_ge(mask_loaded[k], 16 * (p // 2 + 1))
                if p >= 2:
                    pool.wait_ge(max2_ready, p - 1)
                nc.gpsimd.tensor_scalar(maskneg[k][:], mask[k][:], 0, NEG * 16, ALU.is_equal, ALU.mult)\
                    .then_inc(maskneg_ready, 1)

            def rstd_of_pair(p):
                pool.wait_ge(var_ready, 4 + p + 1)
                nc.gpsimd.tensor_tensor(stat2[:, p, 3:4], stat2[:, p, 2:3], part(table, TABLE, "minus_half")[:, 0:1], ALU.pow)\
                    .then_inc(rstd_ready, 1)

            mask_term(0)
            rstd_of(4)
            mask_term(1)
            for p in range(TC):
                if p + 2 < TC:
                    mask_term(p + 2)
                rstd_of_pair(p)

            pool.wait_ge(x_updated, 4)
            nc.gpsimd.memset(a_pad[:, :, :, 0:KER - 1], 0.0).then_inc(pads_ready, 1)
            nc.gpsimd.memset(bcT[:], 0.0).then_inc(pads_ready, 1)
            for k in range(2):
                last = nc.gpsimd.memset(decay[k][:].rearrange("p g (b s) -> p (g b) s", s=S)[:, :, 0:1], 0.0)
            last.then_inc(pads_ready, 1)
            rstd_of(5 + TC)

            def injected(m, first_chunk):
                for g in range(GROUPS):
                    if first_chunk:
                        pool.wait_ge(Bbc_ready, GS * (g + 1))
                    pool.wait_ge(drive_ready, 1 if first_chunk else CC)
                    if g >= 2 or not first_chunk:
                        pool.wait_ge(scanned, GROUPS * m + (g - 1))
                        pool.sem_inc(inject_free, 1)
                    nc.gpsimd.tensor_tensor(inject[g % 2][:], Bbc[:, GS * g:GS * (g + 1), :],
                                            over(drive_of(m), GS, 1), ALU.mult).then_inc(inject_ready, 1)

            def drive_of(m):
                return drive[:].rearrange("p c n -> p (c n)")[:, bass.ds(m * TOK, TOK)]

            injected(0, True)
            with pool.Fori(1, CC) as m:
                injected(m, False)
            rstd_of(6 + TC)

        @block.scalar
        def _(act):
            def transposed(k):
                act.wait_ge(xt_done, 2 * k - 1)
                nc.scalar.activation(xnT[:, 0, :], pb(0), ACT.Copy).then_inc(xt0_ready, 1)

            transposed(1)
            act.wait_ge(loaded["first"], 16)
            for c in range(DC):
                act.wait_ge(q_done, c + 1)
                bias = part(first, FIRST, "bq")[:, c:c + 1]
                nc.scalar.activation(qT[:, c, :], pb(2 + c), ACT.Identity, bias=bias).then_inc(q_ready, 1)

            def key_piece(b, k):
                act.wait_ge(proj_done, 8 * b + (k + 1))
                c, half = divmod(k, 2)
                nc.scalar.activation(kT_of(b)[:, c, half * 512:(half + 1) * 512], pb(4), ACT.Identity,
                                     bias=part(first, FIRST, "bk")[:, c:c + 1]).then_inc(k_ready, 1)

            parity = [0]

            def kT_of(b):
                return kT[parity[0]]

            def batch(b, par, last):
                for i in range(8):
                    act.wait_ge(max_ready, 8 * b + (i + 1))
                    if i < 2:
                        if not (isinstance(b, int) and b == 0):
                            act.wait_ge(t_done, 16 * (b - 1) + 2 * (i + 7))
                    else:
                        act.wait_ge(t_done, 16 * b + 2 * (i - 1))
                    nc.scalar.activation(probs[i % 2][:], two(i % 2), ACT.Exp,
                                         bias=negmax[i % 2][:], scale=0.25,
                                         accum_out=sums[:, bass.ds(b, 1), i]).then_inc(exp_done, 1)
                    if i < 4 and not last:
                        parity[0] = 1 - par
                        key_piece(b + 1, i)
                    if i >= 1:
                        second_half(b, i - 1)
                    elif not (isinstance(b, int) and b == 0):
                        second_half(b - 1, 7)

            def second_half(b, i):
                c, j = divmod(i, PAIRS)
                act.wait_ge(t_done, 16 * b + 2 * i + 2)
                nc.scalar.activation(probsT[c][:, KC // 2:KC, j, :], pb(6).rearrange("p (k n) -> p k n", n=P),
                                     ACT.Copy).then_inc(pt1_ready, 1)

            parity[0] = 0
            for k in range(4):
                key_piece(0, k)
            act.wait_ge(loaded["later"], 16)
            nc.scalar.activation(s4dt[:], part(later, LATER, "log_dt"), ACT.Exp).then_inc(s4_exp, 1)
            nc.scalar.activation(s4["ew"][:], part(later, LATER, "inv_w"), ACT.Exp).then_inc(s4_exp, 1)
            batch(0, 0, False)
            with act.Fori(0, B // 2 - 1) as n:
                for k in range(2):
                    batch(2 * n + (1 + k), 1 - k, False)
            batch(B - 1, 1, True)
            second_half(B - 1, 7)
            transposed(2)
            for c in range(DC):
                act.wait_ge(conv_ready, c + 1)
                nc.scalar.activation(conv[1][:, c, :], conv[0][:, c, :], ACT.Silu).then_inc(silu_ready, 1)

            def split_high(e, half_e, k, q):
                if q == 0:
                    act.wait_ge(raw_loaded[k], 16 * half_e + 16)
                    if not (isinstance(e, int) and e < 2):
                        act.wait_ge(down_done, UNITS * (e - 1))
                cols = slice(q * QW, (q + 1) * QW)
                nc.scalar.activation(w_hi[k][:, cols], raw[k][:, cols], ACT.Copy).then_inc(hi_done, 1)

            def gelu(e, u):
                act.wait_ge(up_done, UNITS * e + (u + 1))
                if not (isinstance(e, int) and e == 0 and u < 2):
                    act.wait_ge(h_hi_ready, UNITS * e + (u - 1))
                    act.wait_ge(h_ready, UNITS * e + (u - 1))
                nc.scalar.activation(h_full[u % 2][:], pb(u % 2), ACT.Gelu,
                                     bias=part(later, LATER, "b1")[:, bass.ds(UNITS * e + u, 1)]).then_inc(gelu_done, 1)

            def pair_of_experts(n, is_first, is_last):
                for k in range(2):
                    e = 2 * n + k
                    for u in range(UNITS):
                        gelu(e, u)
                        if 2 <= u < 6 and not (is_last and k) and not (is_first and not k):
                            split_high(e + 1, n + k, 1 - k, u - 2)
                        if is_first and k == 0 and u == 5:
                            act.wait_ge(centred, 1)
                            nc.scalar.activation(gate[:], logits[:], ACT.Exp).then_inc(gate_exp, 1)
                        if is_first and k == 1 and u == 3:
                            act.wait_ge(gate_turned, 1)
                            nc.scalar.activation(gateT[:], pb(3)[0:E0, :].rearrange("e (t n) -> e t n", t=TC), ACT.Copy)\
                                .then_inc(gateT_ready, 1)

            act.wait_ge(x_updated, 1)
            for e in range(2):
                for q in range(4):
                    split_high(e, 0, e, q)
            transposed(3)
            act.wait_ge(xt1_ready, 3)
            act.wait_ge(xt0_ready, 3)
            nc.scalar.activation(x_hi[:], xnT[:], ACT.Copy).then_inc(xs_ready, 1)
            for t in range(TC):
                if t:
                    act.wait_ge(ssq_ready, t)
                nc.scalar.activation(squares[:], xn[:, t, :], ACT.Square, accum_out=sumsq[:, t:t + 1]).then_inc(ssq_ready, 1)
            pair_of_experts(0, True, False)
            with act.Fori(1, E0 // 2 - 1) as n:
                pair_of_experts(n, False, False)
            pair_of_experts(E0 // 2 - 1, False, True)

            transposed(4)

            def weights2(p):
                k = p % 2
                act.wait_ge(max2_ready, p + 1)
                if p >= 2:
                    act.wait_ge(turned2, 2 * (p - 1))
                nc.scalar.activation(probs2[k][:], masked[k][:], ACT.Exp, bias=stat2[:, p, 0:1], scale=1.0 / 16,
                                     accum_out=stat2[:, p, 1:2]).then_inc(exp2_done, 1)

            def right_half(p):
                act.wait_ge(turned2, 2 * p + 2)
                if p:
                    act.wait_ge(mixed_done, p)
                nc.scalar.activation(probsT2[:, KC // 2:KC, :], pb(5).rearrange("p (k n) -> p k n", n=P), ACT.Copy)\
                    .then_inc(right2_ready, 1)

            weights2(0)
            for p in range(TC):
                if p + 1 < TC:
                    weights2(p + 1)
                right_half(p)

            act.wait_ge(loaded["later"], 16)
            nc.scalar.activation(exp_a[:], part(later, LATER, "a_param"), ACT.Exp, scale=-1.0).then_inc(expa_ready, 1)
            transposed(5)
            act.wait_ge(pads_ready, 3)
            for m in range(CC):
                act.wait_ge(ag_done, m + 1)
                nc.scalar.activation(a_pad[:, m, :, KER - 1:], pb(2 + m).rearrange("p (b s) -> p b s", b=B), ACT.Copy)\
                    .then_inc(a_ready, 1)
            for m in range(CC):
                act.wait_ge(conv1_ready, m + 1)
                nc.scalar.activation(aT[:, m, :], hidden[0][:, m % 2, :], ACT.Silu,
                                     bias=part(later, LATER, "conv_b")[:, m:m + 1]).then_inc(a_silu, 1)
                act.wait_ge(ag_done, CC + m + 1)
                nc.scalar.activation(gT[:, m, :], pb(2 + m), ACT.Silu).then_inc(g_ready, 1)
            act.wait_ge(low_done, 1)
            nc.scalar.activation(lowT[:], pb(7), ACT.Copy).then_inc(low_ready, 1)
            for m in range(CC):
                act.wait_ge(relu_ready, m + 1)
                if m >= 2:
                    act.wait_ge(soft_taken, m - 1)
                nc.scalar.activation(soft[m % 2][:], pb(2 + m), ACT.Abs, bias=part(later, LATER, "d_param")[:, m:m + 1])\
                    .then_inc(abs_ready, 1)
                act.wait_ge(abs_ready, m + 1)
                nc.scalar.activation(soft[m % 2][:], soft[m % 2][:], ACT.Exp, scale=-1.0).then_inc(act_step, 1)
                act.wait_ge(act_step, m + 1)
                nc.scalar.activation(soft[m % 2][:], soft[m % 2][:], ACT.Ln, bias=ones[:, 0:1]).then_inc(soft_ready, 1)

            def decays(m, first_chunk):
                for g in range(GROUPS):
                    if first_chunk:
                        for s in range(GS):
                            act.wait_ge(Bbc_done, GS * g + s + 1)
                            nc.scalar.activation(Bbc[:, GS * g + s, :], pb(s), ACT.Copy).then_inc(Bbc_ready, 1)
                    if g == 0:
                        act.wait_ge(drive_ready, m + 1)
                    if g >= 2 or not first_chunk:
                        act.wait_ge(scanned, GROUPS * m + (g - 1))
                    row = delta[:, m, :] if first_chunk else delta[:, bass.ds(m, 1), :].rearrange("p c n -> p (c n)")
                    for s in range(GS):
                        last = nc.scalar.activation(
                            decay[g % 2][:, s, :].rearrange("p (b s) -> p b s", b=B)[:, :, 1:S],
                            row.rearrange("p (b s) -> p b s", b=B)[:, :, 1:S], ACT.Copy,
                            scale=exp_a[:, bass.ds(NSTATE * m + (GS * g + s), 1)])
                    last.then_inc(decay_ready, 1)

            act.wait_ge(expa_ready, 1)
            decays(0, True)
            with act.Fori(1, CC) as m:
                decays(m, False)

            transposed(6)
            act.wait_ge(centred1, 1)
            nc.scalar.activation(logits1[:], logits1[:], ACT.Exp).then_inc(gate1_exp, 1)

            def silu1(n):
                for k in range(FB):
                    act.wait_ge(gu_done, FB * n + (k + 1))
                    if not isinstance(n, int):
                        act.wait_ge(hid_ready, FB * n + (k - 2))
                    nc.scalar.activation(act_f[k][:], pb(2 * k), ACT.Silu).then_inc(silu1_ready, 1)

            silu1(0)
            with act.Fori(1, E1 // FB) as n:
                silu1(n)

        @block.vector
        def _(dve):
            order = Order(dve, dve_step)

            def layer_norm(k):
                for t in range(TC):
                    last = nc.vector.bn_stats(stats[:, t, :], X[:, t, :])
                order.step(last)
                for t in range(TC):
                    last = nc.vector.bn_aggr(moments[:, t, :], stats[:, t, :])
                order.step(last)
                nc.vector.tensor_scalar_add(vareps[:], moments[:, :, 1], EPS).then_inc(var_ready, 1)
                dve.wait_ge(rstd_ready, k)
                for t in range(TC):
                    last = nc.vector.tensor_scalar(xn[:, t, :], X[:, t, :], moments[:, t, 0:1], rstd[:, t:t + 1],
                                                   ALU.subtract, ALU.mult)
                last.then_inc(xn_ready, 1)

            def transposed(k):
                dve.wait_ge(xt_done, 2 * k)
                nc.vector.tensor_copy(xnT[:, 1, :], pb(1)).then_inc(xt1_ready, 1)

            dve.wait_ge(loaded["x"], 16)
            layer_norm(1)
            transposed(1)

            def value_piece(b, par, k):
                dve.wait_ge(proj_done, 8 * b + (k + 1))
                v = k - 4
                if not (isinstance(b, int) and b < 2):
                    dve.wait_ge(pv_done, 2 * (b - 1))
                nc.vector.tensor_copy(V[par][:, 2 * v:2 * v + 2, :], pb(4).rearrange("p (k n) -> p k n", k=2))\
                    .then_inc(v_ready, 1)

            def first_half(b, i):
                c, j = divmod(i, PAIRS)
                dve.wait_ge(t_done, 16 * b + 2 * i + 1)
                nc.vector.tensor_copy(probsT[c][:, 0:KC // 2, j, :], pb(5).rearrange("p (k n) -> p k n", n=P))\
                    .then_inc(pt0_ready, 1)

            def gather(b, c):
                dve.wait_ge(pv_done, 2 * b + (c + 1))
                if not (isinstance(b, int) and b == 0 and c == 0):
                    dve.wait_ge(attn_ready, 2 * b + c)
                nc.vector.tensor_tensor(own[:], pb(7)[:, 0:256].rearrange("p (h s) -> p h s", h=4),
                                        over(part(table, TABLE, "quad"), S, 2), ALU.mult).then_inc(masked_ready, 1)
                dve.wait_ge(masked_ready, 2 * b + (c + 1))
                nc.vector.tensor_reduce(attnT[:, c, bass.ds(b * S, S)], own[:].rearrange("p h s -> p s h"),
                                        AX.X, ALU.add).then_inc(attn_ready, 1)

            def batch(b, par, last):
                for i in range(8):
                    dve.wait_ge(scores_done, 8 * b + (i + 1))
                    nc.vector.tensor_reduce(negmax_raw[i % 2][:], two(i % 2),
                                            AX.X, ALU.max, negate=True).then_inc(raw_max, 1)
                    dve.wait_ge(raw_max, 8 * b + (i + 1))
                    nc.vector.tensor_scalar(negmax[i % 2][:], negmax_raw[i % 2][:], 0.25, None, ALU.mult)\
                        .then_inc(max_ready, 1)
                    if i == 6:
                        gather(b, 0)
                    if i == 2 and not (isinstance(b, int) and b == 0):
                        gather(b - 1, 1)
                    if i >= 4 and not last:
                        value_piece(b + 1, 1 - par, i)
                    if i >= 1:
                        first_half(b, i - 1)
                    elif not (isinstance(b, int) and b == 0):
                        first_half(b - 1, 7)

            for k in range(4, 8):
                value_piece(0, 0, k)
            batch(0, 0, False)
            with dve.Fori(0, B // 2 - 1) as n:
                for k in range(2):
                    batch(2 * n + (1 + k), 1 - k, False)
            batch(B - 1, 1, True)
            first_half(B - 1, 7)
            gather(B - 1, 1)
            dve.wait_ge(exp_done, 8 * B)
            nc.vector.reciprocal(inv_sums[:], sums[:]).then_inc(attn_ready, 1)
            dve.wait_ge(loaded["rows"], 16)
            bo = part(rows, ROWS, "bo")
            order.step(nc.vector.tensor_tensor(X[:], X[:], over(bo, TC, 1), ALU.add))
            for c in range(DC):
                dve.wait_ge(inv_done, PAIRS * (c + 1))
                order.step(nc.vector.tensor_tensor(attnT[:, c, :], attnT[:, c, :], pb(c), ALU.mult))
                nc.vector.tensor_scalar(attnT[:, c, :], attnT[:, c, :], part(first, FIRST, "bv")[:, c:c + 1], None, ALU.add)\
                    .then_inc(attn_scaled, 1)
            for h in range(2):
                dve.wait_ge(out_done, h + 1)
                last = nc.vector.tensor_tensor(X[:, 2 * h:2 * h + 2, :], X[:, 2 * h:2 * h + 2, :],
                                               pb(2 + h).rearrange("p (t n) -> p t n", t=2), ALU.add)
            last.then_inc(x_updated, 1)
            dve.wait_ge(x_updated, 1)
            layer_norm(2)
            transposed(2)
            dve.wait_ge(taps_ready, 1)
            dve.wait_ge(xt0_ready, 2)
            dve.wait_ge(xt1_ready, 2)
            for c in range(DC):
                order.step(nc.vector.tensor_scalar(conv[0][:, c, :], xnT[:, c, :], taps[:, 0, c:c + 1], None, ALU.mult))
                for l in range(1, B):
                    later_cols = conv[0][:, c, l * S:TOK]
                    ins = nc.vector.scalar_tensor_tensor(later_cols, xnT[:, c, 0:TOK - l * S], taps[:, l, c:c + 1],
                                                         later_cols, ALU.mult, ALU.add)
                    if l < B - 1:
                        order.step(ins)
                    else:
                        ins.then_inc(conv_ready, 1)
            for h in range(2):
                dve.wait_ge(back_done, h + 1)
                last = nc.vector.tensor_tensor(X[:, 2 * h:2 * h + 2, :], X[:, 2 * h:2 * h + 2, :],
                                               pb(2 + h).rearrange("p (t n) -> p t n", t=2), ALU.add)
            last.then_inc(x_updated, 1)

            def top(values, n, before, count, greater, equal, place_of):
                one, other = over(values, n, 3), over(values, n, 2)
                order.step(nc.vector.tensor_tensor(greater, other, one, ALU.is_gt))
                order.step(nc.vector.tensor_tensor(equal, other, one, ALU.is_equal))
                lower = over(part(table, TABLE, before), TC, 1)
                flat = equal.rearrange("p t a b -> p t (a b)")
                order.step(nc.vector.tensor_tensor(flat, flat, lower, ALU.mult))
                order.step(nc.vector.tensor_tensor(greater, greater, equal, ALU.add))
                order.step(nc.vector.tensor_reduce(place_of, greater, AX.X, ALU.add))
                order.step(nc.vector.tensor_scalar(place_of, place_of, float(count), None, ALU.is_lt))

            def router():
                dve.wait_ge(logits_done, 1)
                dve.wait_ge(ssq_ready, TC)
                rb = part(rows, ROWS, "rb")
                for t in range(TC):
                    last = nc.vector.scalar_tensor_tensor(logits[:, t, :], pb(2)[:, t * E0:(t + 1) * E0], sumsq[:, t:t + 1], rb,
                                                          ALU.subtract, ALU.add)
                order.step(last)
                top(logits[:], E0, "before0", TOP0, above[:], tied[:], rank[:])
                order.step(nc.vector.tensor_reduce(best[:], logits[:], AX.X, ALU.max))
                nc.vector.tensor_tensor(logits[:], logits[:], over(best[:], E0, 2), ALU.subtract).then_inc(centred, 1)

            def router_end():
                dve.wait_ge(gate_exp, 1)
                order.step(nc.vector.tensor_tensor(gate[:], gate[:], rank[:], ALU.mult))
                order.step(nc.vector.tensor_reduce(best[:], gate[:], AX.X, ALU.add))
                order.step(nc.vector.reciprocal(best[:], best[:]))
                nc.vector.tensor_tensor(gate[:], gate[:], over(best[:], E0, 2), ALU.mult).then_inc(gate_ready, 1)
                dve.wait_ge(gate_ready, 1)

            def split_hidden(e, u):
                dve.wait_ge(gelu_done, UNITS * e + (u + 1))
                if not (isinstance(e, int) and e == 0 and u < 4):
                    dve.wait_ge(down_done, UNITS * e + (u - 3))
                nc.vector.tensor_copy(h_hi[u % 4][:], h_full[u % 2][:]).then_inc(h_hi_ready, 1)
                dve.wait_ge(h_hi_ready, UNITS * e + (u + 1))
                nc.vector.tensor_tensor(h_lo[u % 4][:], h_full[u % 2][:], h_hi[u % 4][:].bitcast(F32), ALU.subtract)\
                    .then_inc(h_ready, 1)

            def combine(e, k, is_first):
                dve.wait_ge(down_done, UNITS * (e + 1))
                if not is_first:
                    dve.wait_ge(combined, e)
                for t in range(TC):
                    y = pb(4 + 2 * k + t // 2)[:, (t % 2) * D:(t % 2 + 1) * D]
                    last = nc.vector.scalar_tensor_tensor(X[:, t, :], y, gate[:, t, bass.ds(e, 1)], X[:, t, :],
                                                          ALU.mult, ALU.add)
                last.then_inc(combined, 1)

            def pair_of_experts(n, is_first):
                for k in range(2):
                    e = 2 * n + k
                    for u in range(UNITS):
                        split_hidden(e, u)
                        if is_first and k == 0 and u == 3:
                            router()
                        if is_first and k == 0 and u == 6:
                            router_end()
                        if u == 3 and not (is_first and k == 0):
                            combine(e - 1, 1 - k, is_first and k == 1)
                        if is_first and k == 1 and u == 6:
                            dve.wait_ge(bias_done, 1)
                            dve.wait_ge(combined, 1)
                            order.step(nc.vector.tensor_tensor(
                                X[:], X[:], banks[:, 2:4, :].rearrange("p a (t n) -> p (a t) n", n=D), ALU.add))

            dve.wait_ge(x_updated, 2)
            layer_norm(3)
            transposed(3)
            dve.wait_ge(xt1_ready, 3)
            dve.wait_ge(xs_ready, 1)
            nc.vector.tensor_tensor(x_lo[:], xnT[:], x_hi[:].bitcast(F32), ALU.subtract).then_inc(xs_ready, 1)
            pair_of_experts(0, True)
            with dve.Fori(1, E0 // 2) as n:
                pair_of_experts(n, False)
            combine(E0 - 1, 1, False)
            dve.wait_ge(combined, E0)
            dve.sem_inc(x_updated, 1)

            dve.wait_ge(x_updated, 3)
            layer_norm(4)
            transposed(4)

            def greatest(p):
                k = p % 2
                dve.wait_ge(scores2_done, p + 1)
                dve.wait_ge(maskneg_ready, p + 1)
                if p >= 2:
                    dve.wait_ge(exp2_done, p - 1)
                order.step(nc.vector.tensor_tensor(masked[k][:], two(k), maskneg[k][:], ALU.add))
                order.step(nc.vector.tensor_reduce(stat2[:, p, 0:1], masked[k][:], AX.X, ALU.max))
                nc.vector.tensor_scalar(stat2[:, p, 0:1], stat2[:, p, 0:1], -1.0 / 16, None, ALU.mult).then_inc(max2_ready, 1)

            def left_half(p):
                dve.wait_ge(turned2, 2 * p + 1)
                if p:
                    dve.wait_ge(mixed_done, p)
                nc.vector.tensor_copy(probsT2[:, 0:KC // 2, :], pb(4).rearrange("p (k n) -> p k n", n=P)).then_inc(left2_ready, 1)

            def normalise(p):
                dve.wait_ge(exp2_done, p + 1)
                order.step(nc.vector.reciprocal(stat2[:, p, 1:2], stat2[:, p, 1:2]))
                dve.wait_ge(mixed_done, p + 1)
                nc.vector.tensor_scalar(mixed[:], pb(6)[:, 0:D], stat2[:, p, 1:2], None, ALU.mult).then_inc(mixed_taken, 1)
                dve.wait_ge(mixed_taken, p + 1)
                order.step(nc.vector.bn_stats(stats[:, p, :], mixed[:]))
                order.step(nc.vector.bn_aggr(moments[:, p, :], stats[:, p, :]))
                nc.vector.tensor_scalar_add(stat2[:, p, 2:3], moments[:, p, 1:2], EPS).then_inc(var_ready, 1)
                dve.wait_ge(rstd_ready, 4 + p + 1)
                order.step(nc.vector.tensor_scalar(mixed[:], mixed[:], moments[:, p, 0:1], stat2[:, p, 3:4],
                                                   ALU.subtract, ALU.mult))
                order.step(nc.vector.tensor_tensor(mixed[:], mixed[:], part(rows, ROWS, "gamma"), ALU.mult))
                order.step(nc.vector.tensor_tensor(mixed[:], mixed[:], part(rows, ROWS, "beta"), ALU.add))
                order.mark(nc.vector.tensor_tensor(X[:, p, :], X[:, p, :], mixed[:], ALU.add))

            greatest(0)
            for p in range(TC):
                if p + 1 < TC:
                    greatest(p + 1)
                left_half(p)
                normalise(p)
            order.settle()
            dve.sem_inc(x_updated, 1)

            dve.wait_ge(x_updated, 4)
            layer_norm(5 + TC)
            transposed(5)
            conv_w = part(later, LATER, "conv_w").rearrange("p (c k) -> p c k", c=CC)
            for m in range(CC):
                dve.wait_ge(a_ready, m + 1)
                if m >= 2:
                    dve.wait_ge(a_silu, m - 1)
                y = hidden[0][:, m % 2, :].rearrange("p (b s) -> p b s", b=B)
                order.step(nc.vector.tensor_scalar(y, a_pad[:, m, :, 0:S], conv_w[:, m, 0:1], None, ALU.mult))
                for k in range(1, KER):
                    ins = nc.vector.scalar_tensor_tensor(y, a_pad[:, m, :, k:k + S], conv_w[:, m, k:k + 1], y, ALU.mult, ALU.add)
                    if k < KER - 1:
                        order.step(ins)
                    else:
                        ins.then_inc(conv1_ready, 1)
            d_param = part(later, LATER, "d_param")
            dve.wait_ge(bc_done, 1)
            nc.vector.tensor_copy(bcT[0:2 * NSTATE, :], pb(6)[0:2 * NSTATE, :]).then_inc(bc_ready, 1)

            def step_parts(m):
                dve.wait_ge(step_done, m + 1)
                bias = d_param[:, m:m + 1]
                nc.vector.tensor_scalar(delta[:, m, :], pb(2 + m), bias, 0.0, ALU.add, ALU.max).then_inc(relu_ready, 1)

            def step_end(m):
                dve.wait_ge(soft_ready, m + 1)
                dve.wait_ge(relu_ready, m + 1)
                nc.vector.tensor_tensor(delta[:, m, :], delta[:, m, :], soft[m % 2][:], ALU.add).then_inc(soft_taken, 1)
                dve.wait_ge(soft_taken, m + 1)
                dve.wait_ge(a_silu, m + 1)
                nc.vector.tensor_tensor(drive[:, m, :], delta[:, m, :], aT[:, m, :], ALU.mult).then_inc(drive_ready, 1)

            step_parts(0)
            for m in range(CC):
                if m + 1 < CC:
                    step_parts(m + 1)
                step_end(m)

            def chunk(tile, m):
                return tile[:, m, :] if isinstance(m, int) else tile[:, bass.ds(m, 1), :].rearrange("p c n -> p (c n)")

            def gated(m):
                dve.wait_ge(y_ready, m + 1)
                if not isinstance(m, int):
                    dve.wait_ge(gated_ready, 2 * m)
                elif m:
                    dve.wait_ge(gated_ready, 2 * m)
                nc.vector.scalar_tensor_tensor(acc[:], chunk(aT, m), d_param[:, bass.ds(m, 1)], pb(m + 2),
                                               ALU.mult, ALU.add).then_inc(gated_ready, 1)
                dve.wait_ge(gated_ready, 2 * m + 1)
                nc.vector.tensor_tensor(chunk(gT, m), acc[:], chunk(gT, m), ALU.mult).then_inc(gated_ready, 1)

            def states(m, first_chunk):
                for g in range(GROUPS):
                    if first_chunk:
                        for s in range(GS):
                            dve.wait_ge(Cbc_done, GS * g + s + 1)
                            nc.vector.tensor_copy(Cbc[:, GS * g + s, :], pb(6 + s)).then_inc(Cbc_ready, 1)
                    dve.wait_ge(decay_ready, GROUPS * m + (g + 1))
                    dve.wait_ge(inject_ready, GROUPS * m + (g + 1))
                    if g >= 2 or not first_chunk:
                        dve.wait_ge(shown_ready, GROUPS * m + (g - 1))
                    nc.vector.tensor_tensor_scan(hidden[g % 2][:].rearrange("p g n -> p (g n)"),
                                                 decay[g % 2][:].rearrange("p g n -> p (g n)"),
                                                 inject[g % 2][:].rearrange("p g n -> p (g n)"),
                                                 0.0, ALU.mult, ALU.add).then_inc(scanned, 1)
                    dve.wait_ge(scanned, GROUPS * m + (g + 1))
                    if first_chunk:
                        dve.wait_ge(Cbc_ready, GS * (g + 1))
                    if g >= 2 or not first_chunk:
                        dve.wait_ge(shown_used, GROUPS * m + (g - 1))
                    nc.vector.tensor_tensor(shown[g % 2][:], hidden[g % 2][:], Cbc[:, GS * g:GS * (g + 1), :], ALU.mult)\
                        .then_inc(shown_ready, 1)
                    if g == 2 and not first_chunk:
                        gated(m - 1)

            dve.wait_ge(g_ready, CC)
            states(0, True)
            with dve.Fori(1, CC) as m:
                states(m, False)
            gated(CC - 1)
            for h in range(2):
                dve.wait_ge(out1_done, h + 1)
                last = nc.vector.tensor_tensor(X[:, 2 * h:2 * h + 2, :], X[:, 2 * h:2 * h + 2, :],
                                               pb(6 + h).rearrange("p (t n) -> p t n", t=2), ALU.add)
            last.then_inc(x_updated, 1)

            dve.wait_ge(x_updated, 5)
            layer_norm(6 + TC)
            transposed(6)
            dve.wait_ge(logits1_done, 1)
            raw_logits = pb(6)[:, 0:TC * ROUTED1].rearrange("p (t e) -> p t e", t=TC)
            order.step(nc.vector.tensor_reduce(best1[:], raw_logits, AX.X, ALU.max))
            nc.vector.tensor_tensor(logits1[:], raw_logits, over(best1[:], ROUTED1, 2), ALU.subtract).then_inc(centred1, 1)
            nc.vector.memset(gate1[:], 1.0).then_inc(gate1_ready, 1)

            def route():
                dve.wait_ge(gate1_exp, 1)
                order.step(nc.vector.tensor_reduce(best1[:], logits1[:], AX.X, ALU.add))
                order.step(nc.vector.reciprocal(best1[:], best1[:]))
                order.step(nc.vector.tensor_tensor(logits1[:], logits1[:], over(best1[:], ROUTED1, 2), ALU.mult))
                top(logits1[:], ROUTED1, "before1", TOP1, above1[:], tied1[:], rank1[:])
                dve.wait_ge(gate1_ready, 1)
                nc.vector.tensor_tensor(gate1[:, :, 0:ROUTED1], logits1[:], rank1[:], ALU.mult).then_inc(gate1_ready, 1)
                dve.wait_ge(gate1_ready, 2)

            def hidden1(n, k):
                dve.wait_ge(silu1_ready, FB * n + (k + 1))
                if not isinstance(n, int):
                    dve.wait_ge(down1_done, FB * n + (k - 2))
                nc.vector.tensor_tensor(hid_f[k][:], act_f[k][:], pb(2 * k + 1), ALU.mult).then_inc(hid_ready, 1)

            def combine1(n, k):
                dve.wait_ge(down1_done, FB * n + (k + 1))
                if not (isinstance(n, int) and k == 0):
                    dve.wait_ge(combined1, FB * n + k)
                for t in range(TC):
                    y = pb(6 + t // 2)[:, (t % 2) * D:(t % 2 + 1) * D]
                    last = nc.vector.scalar_tensor_tensor(X[:, t, :], y, gate1[:, t, bass.ds(FB * n + k, 1)], X[:, t, :],
                                                          ALU.mult, ALU.add)
                last.then_inc(combined1, 1)

            def three_experts(n):
                hidden1(n, 0)
                hidden1(n, 1)
                if isinstance(n, int):
                    route()
                combine1(n, 0)
                hidden1(n, 2)
                combine1(n, 1)
                combine1(n, 2)

            three_experts(0)
            with dve.Fori(1, E1 // FB) as n:
                three_experts(n)
            dve.wait_ge(combined1, E1)
            dve.sem_inc(x_updated, 1)

        @block.tensor
        def _(pe):
            def mm(o, lhsT, rhs, start, stop):
                return nc.tensor.matmul(o, lhsT, rhs, start=start, stop=stop)

            def weights(tile, layout, name, parts):
                return part(tile, layout, name).rearrange("p (c n) -> p c n", c=parts)

            def transpose_tokens(k):
                pe.wait_ge(xn_ready, k)
                for c in range(DC):
                    for t in range(TC):
                        last = nc.tensor.transpose(pb(c)[:, t * P:(t + 1) * P], xn[:, t, c * P:(c + 1) * P], ident)
                    last.then_inc(xt_done, 1)

            pe.wait_ge(loaded["table"], 16)
            transpose_tokens(1)
            pe.wait_ge(loaded["first"], 16)
            wq, wk, wv = (weights(first, FIRST, n, DC) for n in ("wq", "wk", "wv"))
            pe.wait_ge(xt0_ready, 1)
            pe.wait_ge(xt1_ready, 1)
            for c in range(DC):
                for i in range(DC):
                    last = mm(pb(2 + c), wq[:, i, c * P:(c + 1) * P], xnT[:, i, :], i == 0, i == DC - 1)
                last.then_inc(q_done, 1)

            def project(b, half_b, par, k):
                if k == 0:
                    pe.wait_ge(ctx_loaded[par], 16 * half_b + 16)
                    if not (isinstance(b, int) and b == 0):
                        pe.wait_ge(v_ready, 4 * b)
                elif k <= 4:
                    pe.wait_ge(k_ready, 4 * b + k)
                else:
                    pe.wait_ge(v_ready, 4 * b + (k - 4))
                if k < 4:
                    c, half = divmod(k, 2)
                    for i in range(DC):
                        last = mm(pb(4), wk[:, i, c * P:(c + 1) * P], ctxT[par][:, i, half * 512:(half + 1) * 512],
                                  i == 0, i == DC - 1)
                else:
                    for v in range(2):
                        kc = 2 * (k - 4) + v
                        for i in range(DC):
                            last = mm(pb(4)[:, v * D:(v + 1) * D], ctxT[par][:, i, kc * P:(kc + 1) * P], wv[:, i, :],
                                      i == 0, i == DC - 1)
                last.then_inc(proj_done, 1)

            def turn(b, i):
                pe.wait_ge(exp_done, 8 * b + (i + 1))
                for half in range(2):
                    if not (isinstance(b, int) and b == 0 and i == 0):
                        pe.wait_ge(pt1_ready if half else pt0_ready, 8 * b + i)
                    for k in range(KC // 2):
                        kc = half * (KC // 2) + k
                        last = nc.tensor.transpose(pb(5 + half)[:, k * P:(k + 1) * P],
                                                   probs[i % 2][:, kc * P:(kc + 1) * P], ident)
                    last.then_inc(t_done, 1)

            def weigh(b, par, c):
                pe.wait_ge(pt0_ready, 8 * b + PAIRS * (c + 1))
                pe.wait_ge(pt1_ready, 8 * b + PAIRS * (c + 1))
                pe.wait_ge(v_ready, 4 * b + 4)
                if not (isinstance(b, int) and b == 0 and c == 0):
                    pe.wait_ge(masked_ready, 2 * b + c)
                for kc in range(KC):
                    for g in range(2):
                        last = mm(pb(7)[64 * g:64 * g + 64, 0:256], V[par][:, kc, c * P + 64 * g:c * P + 64 * g + 64],
                                  probsT[c][:, kc, 2 * g:2 * g + 2, :], kc == 0, kc == KC - 1)
                last.then_inc(pv_done, 1)

            def batch(b, half_next, par, last):
                for i in range(8):
                    c, j = divmod(i, PAIRS)
                    if i == 0:
                        pe.wait_ge(heads_ready, b + 1)
                        pe.wait_ge(k_ready, 4 * b + 4)
                    if not (isinstance(b, int) and b == 0 and i < 2):
                        pe.wait_ge(exp_done, 8 * b + (i - 1))
                    for half in range(2):
                        done = mm(pb(2 * (i % 2) + half), Qh[par][c][:, 2 * j:2 * j + 2, :],
                                  kT[par][:, c, half * 512:(half + 1) * 512], True, True)
                    done.then_inc(scores_done, 1)
                    if not last:
                        project(b + 1, half_next, 1 - par, i)
                    if i >= 1:
                        turn(b, i - 1)
                    elif not (isinstance(b, int) and b == 0):
                        turn(b - 1, 7)
                    if i == 5:
                        weigh(b, par, 0)
                    if i == 1 and not (isinstance(b, int) and b == 0):
                        weigh(b - 1, 1 - par, 1)

            for k in range(8):
                project(0, 0, 0, k)
            batch(0, 0, 0, False)
            with pe.Fori(0, B // 2 - 1) as n:
                for k in range(2):
                    batch(2 * n + (1 + k), n + 1, 1 - k, False)
            batch(B - 1, 0, 1, True)
            turn(B - 1, 7)
            weigh(B - 1, 1, 1)
            pick = weights(table, TABLE, "pick", PAIRS)
            for c in range(DC):
                for j in range(PAIRS):
                    pe.wait_ge(spread_ready, PAIRS * c + j + 1)
                    mm(pb(c), pick[:, j, :], spread[j % 2][:].rearrange("p b s -> p (b s)"), j == 0, j == PAIRS - 1)\
                        .then_inc(inv_done, 1)
            pe.wait_ge(attn_scaled, DC)
            pe.wait_ge(loaded["later"], 16)
            wo = weights(later, LATER, "wo", DC)
            for t in range(TC):
                for c in range(DC):
                    last = mm(pb(2 + t // 2)[:, (t % 2) * D:(t % 2 + 1) * D], attnT[:, c, t * P:(t + 1) * P], wo[:, c, :],
                              c == 0, c == DC - 1)
                if t % 2:
                    last.then_inc(out_done, 1)
            transpose_tokens(2)
            for h in range(2):
                for t in (2 * h, 2 * h + 1):
                    for c in range(DC):
                        pe.wait_ge(silu_ready, c + 1)
                        last = nc.tensor.transpose(pb(2 + h)[:, (t % 2) * D + c * P:(t % 2) * D + (c + 1) * P],
                                                   conv[1][:, c, t * P:(t + 1) * P], ident)
                last.then_inc(back_done, 1)

            transpose_tokens(3)
            pe.wait_ge(xt0_ready, 3)
            pe.wait_ge(xt1_ready, 3)
            pe.wait_ge(keys_ready, 2)
            for t in range(TC):
                o = pb(2)[:, t * E0:(t + 1) * E0]
                for c in range(DC):
                    mm(o, xnT[:, c, t * P:(t + 1) * P], key_sum[:, c, :], c == 0, False)
                for c in range(DC):
                    last = mm(o, ones, key_sq[:, c, :], False, c == DC - 1)
            last.then_inc(logits_done, 1)
            pe.wait_ge(xs_ready, 2)

            def up(e, k, u):
                if u == 0:
                    pe.wait_ge(lo_done, 4 * e + 2)
                if not (isinstance(e, int) and e == 0 and u < 2):
                    pe.wait_ge(gelu_done, UNITS * e + (u - 1))
                passes = []
                for c in range(DC):
                    cols = slice(c * F0 + u * P, c * F0 + (u + 1) * P)
                    passes += [(w_hi[k][:, cols], x_hi[:, c, :]), (w_hi[k][:, cols], x_lo[:, c, :]),
                               (w_lo[k][:, cols], x_hi[:, c, :])]
                for i, (w, x) in enumerate(passes):
                    last = mm(pb(u % 2), w, x, i == 0, i == len(passes) - 1)
                last.then_inc(up_done, 1)

            def down(e, k, u):
                pe.wait_ge(h_ready, UNITS * e + (u + 1))
                if u == 0:
                    pe.wait_ge(lo_done, 4 * e + 4)
                    if not (isinstance(e, int) and e < 2):
                        pe.wait_ge(combined, e - 1)
                cols = slice(EW // 2 + u * D, EW // 2 + (u + 1) * D)
                for t in range(TC):
                    tok = slice(t * P, (t + 1) * P)
                    o = pb(4 + 2 * k + t // 2)[:, (t % 2) * D:(t % 2 + 1) * D]
                    passes = [(h_hi[u % 4][:, tok], w_hi[k][:, cols]), (h_hi[u % 4][:, tok], w_lo[k][:, cols]),
                              (h_lo[u % 4][:, tok], w_hi[k][:, cols])]
                    for i, (h, w) in enumerate(passes):
                        last = mm(o, h, w, u == 0 and i == 0 and t % 2 == 0, u == UNITS - 1 and i == 2 and t % 2 == 1)
                last.then_inc(down_done, 1)

            def pair_of_experts(n, is_first, is_last):
                for k in range(2):
                    e = 2 * n + k
                    for u in range(UNITS):
                        if u + 2 < UNITS:
                            up(e, k, u + 2)
                        elif not (is_last and k):
                            up(e + 1, 1 - k, u + 2 - UNITS)
                        down(e, k, u)
                        if is_first and k == 1 and u == 2:
                            pe.wait_ge(gate_ready, 1)
                            for t in range(TC):
                                last = nc.tensor.transpose(pb(3)[0:E0, t * P:(t + 1) * P], gate[:, t, :], ident)
                            last.then_inc(gate_turned, 1)
                        if is_first and k == 1 and u == 4:
                            pe.wait_ge(gateT_ready, 1)
                            pe.wait_ge(loaded["b2"], 16)
                            for t in range(TC):
                                last = mm(pb(2 + t // 2)[:, (t % 2) * D:(t % 2 + 1) * D], gateT[:, t, :], b2[:], True, True)
                            last.then_inc(bias_done, 1)

            up(0, 0, 0)
            up(0, 0, 1)
            pair_of_experts(0, True, False)
            with pe.Fori(1, E0 // 2 - 1) as n:
                pair_of_experts(n, False, False)
            pair_of_experts(E0 // 2 - 1, False, True)

            transpose_tokens(4)
            pe.wait_ge(xt0_ready, 4)
            pe.wait_ge(xt1_ready, 4)

            def score2(p):
                k = p % 2
                pe.wait_ge(ctxT2_loaded[k], 16 * (p // 2 + 1))
                if p >= 2:
                    pe.wait_ge(max2_ready, p - 1)
                for half in range(2):
                    for c in range(DC):
                        for b in range(2):
                            last = mm(pb(2 * k + half)[64 * b:64 * b + 64, :], xnT[:, c, p * P + S * b:p * P + S * (b + 1)],
                                      ctxT2[k][:, b, c, half * 512:(half + 1) * 512], c == 0, c == DC - 1)
                last.then_inc(scores2_done, 1)

            def turn2(p):
                pe.wait_ge(exp2_done, p + 1)
                for half in range(2):
                    if p:
                        pe.wait_ge(right2_ready if half else left2_ready, p)
                    for j in range(KC // 2):
                        kc = half * (KC // 2) + j
                        last = nc.tensor.transpose(pb(4 + half)[:, j * P:(j + 1) * P], probs2[p % 2][:, kc * P:(kc + 1) * P], ident)
                    last.then_inc(turned2, 1)

            def mix2(p):
                k = p % 2
                pe.wait_ge(ctxN2_loaded[k], 16 * (p // 2 + 1))
                pe.wait_ge(left2_ready, p + 1)
                pe.wait_ge(right2_ready, p + 1)
                if p:
                    pe.wait_ge(mixed_taken, p)
                for kc in range(KC):
                    for b in range(2):
                        last = mm(pb(6)[64 * b:64 * b + 64, 0:D], probsT2[:, kc, S * b:S * (b + 1)], ctxN2[k][:, b, kc, :],
                                  kc == 0, kc == KC - 1)
                last.then_inc(mixed_done, 1)

            score2(0)
            for p in range(TC):
                if p + 1 < TC:
                    score2(p + 1)
                turn2(p)
                mix2(p)

            transpose_tokens(5)
            pe.wait_ge(xt0_ready, 5)
            pe.wait_ge(xt1_ready, 5)
            w_in = weights(later, LATER, "w_in", DC)
            for g in range(2):
                for m in range(CC):
                    if g:
                        pe.wait_ge(a_ready, m + 1)
                    for c in range(DC):
                        last = mm(pb(2 + m), w_in[:, c, g * DI + m * P:g * DI + (m + 1) * P], xnT[:, c, :], c == 0, c == DC - 1)
                    last.then_inc(ag_done, 1)
            w_sd1, w_sbc = weights(later, LATER, "w_sd1", CC), weights(later, LATER, "w_sbc", CC)
            for o, w, done in ((pb(7), w_sd1, low_done), (pb(6)[0:2 * NSTATE, :], w_sbc, bc_done)):
                for m in range(CC):
                    pe.wait_ge(a_silu, m + 1)
                    last = mm(o, w[:, m, :], aT[:, m, :], m == 0, m == CC - 1)
                last.then_inc(done, 1)
            pe.wait_ge(low_ready, 1)
            w_sd2 = part(later, LATER, "w_sd2")
            for m in range(CC):
                pe.wait_ge(g_ready, m + 1)
                mm(pb(2 + m), w_sd2[:, m * P:(m + 1) * P], lowT[:], True, True).then_inc(step_done, 1)
            pe.wait_ge(bc_ready, 1)

            def broadcast(g):
                for row, at, done, ready in ((0, 0, Bbc_done, Bbc_ready), (NSTATE, 6, Cbc_done, Cbc_ready)):
                    for s in range(GS):
                        if g:
                            pe.wait_ge(ready, GS * (g - 1) + s + 1)
                        r = row + GS * g + s
                        mm(pb(at + s), ident[:, r:r + 1].broadcast_to([P, P]), bcT[:], True, True).then_inc(done, 1)

            def sum_states(m, g):
                pe.wait_ge(shown_ready, GROUPS * m + (g + 1))
                for s in range(GS):
                    last = mm(pb(m + 2), ident, shown[g % 2][:, s, :], g == 0 and s == 0, g == GROUPS - 1 and s == GS - 1)
                last.then_inc(shown_used, 1)
                if g == GROUPS - 1:
                    pe.wait_ge(shown_used, GROUPS * (m + 1))
                    pe.sem_inc(y_ready, 1)

            pe.wait_ge(abs_ready, CC)
            pe.wait_ge(drive_ready, CC)
            broadcast(0)
            broadcast(1)
            for g in range(GROUPS):
                if g + 2 < GROUPS:
                    broadcast(g + 2)
                sum_states(0, g)
            with pe.Fori(1, CC) as m:
                for g in range(GROUPS):
                    sum_states(m, g)
            w_out = weights(later, LATER, "w_out", CC)
            for t in range(TC):
                for m in range(CC):
                    pe.wait_ge(gated_ready, 2 * m + 2)
                    last = mm(pb(6 + t // 2)[:, (t % 2) * D:(t % 2 + 1) * D], gT[:, m, t * P:(t + 1) * P], w_out[:, m, :],
                              m == 0, m == CC - 1)
                if t % 2:
                    last.then_inc(out1_done, 1)

            transpose_tokens(6)
            pe.wait_ge(xt0_ready, 6)
            pe.wait_ge(xt1_ready, 6)
            gate_w = weights(later, LATER, "gate_w", DC)
            for t in range(TC):
                for c in range(DC):
                    last = mm(pb(6)[:, t * ROUTED1:(t + 1) * ROUTED1], xnT[:, c, t * P:(t + 1) * P], gate_w[:, c, :],
                              c == 0, c == DC - 1)
            last.then_inc(logits1_done, 1)

            def gate_up(n, k):
                pe.wait_ge(wf_loaded[k], 16 * n + 16)
                if not isinstance(n, int):
                    pe.wait_ge(hid_ready, FB * n + (k - 2))
                for g in range(2):
                    for c in range(DC):
                        last = mm(pb(2 * k + g), wf[k][:, (g * DC + c) * P:(g * DC + c + 1) * P], xnT[:, c, :], c == 0, c == DC - 1)
                last.then_inc(gu_done, 1)

            def down1(n, k):
                pe.wait_ge(hid_ready, FB * n + (k + 1))
                if isinstance(n, int) and k == 0:
                    pe.wait_ge(centred1, 1)
                else:
                    pe.wait_ge(combined1, FB * n + k)
                for t in range(TC):
                    last = mm(pb(6 + t // 2)[:, (t % 2) * D:(t % 2 + 1) * D], hid_f[k][:, t * P:(t + 1) * P],
                              wf[k][:, 2 * D:3 * D], True, True)
                last.then_inc(down1_done, 1)

            def three_experts(n):
                gate_up(n, 0)
                gate_up(n, 1)
                down1(n, 0)
                gate_up(n, 2)
                down1(n, 1)
                down1(n, 2)

            three_experts(0)
            with pe.Fori(1, E1 // FB) as n:
                three_experts(n)


def _tables():
    t = np.zeros((P, TABLE_W), np.float32)

    def put(name, value):
        a, b = TABLE[name]
        t[:, a:b] = np.asarray(value, np.float64).reshape(P, b - a) if np.ndim(value) > 1 else value

    p = np.arange(P)
    put("ident", np.eye(P))
    put("head", p[:, None] // DH == np.arange(HPC))
    put("quad", p[:, None] % 64 // DH == np.arange(4))
    put("pick", p[None, None, :] // DH == 2 * np.arange(PAIRS)[None, :, None] + p[:, None, None] // S)
    put("query", p[:, None] % S == np.arange(S))
    for name, n in (("before0", E0), ("before1", ROUTED1)):
        put(name, (np.arange(n)[None, :] < np.arange(n)[:, None]).ravel())
    omega = np.exp(-2j * np.pi * np.arange(MODES) / B)
    omega[MODES - 1] = -1.0
    put("ar", (2 * (1 - omega)).real)
    put("ai", (2 * (1 - omega)).imag)
    put("cr", (1 + omega).real)
    put("ci", (1 + omega).imag)
    often = np.array([1, 2, 2, 2, 1]) * 2 / B
    turn = 2 * np.pi * np.outer(np.arange(B), np.arange(MODES)) / B
    put("alpha", (often * np.cos(turn)).ravel())
    beta = -often * np.sin(turn)
    beta[:, [0, MODES - 1]] = 0
    put("beta", beta.ravel())
    put("ones", np.ones(P))
    put("minus_half", np.full(TC, -0.5))
    put("minus_one", np.full(DC * NSTATE * MODES, -1.0))
    return t


def _layouts(x, ctx_1024, mask_BxSxS2_ik1, **w):
    g = {k: np.asarray(v) for k, v in w.items()}

    def rows_in(m):
        m = m.reshape(m.shape[0] // P, P, -1)
        return np.ascontiguousarray(m.transpose(1, 0, 2)).reshape(P, -1)

    def weight(name):
        return rows_in(g[name].T)

    def side(layout, values):
        return np.ascontiguousarray(np.concatenate([values[n].reshape(P, -1) for n in layout], axis=1))

    out = {"x": np.asarray(x).reshape(TOK, D)}
    ctx = np.asarray(ctx_1024)
    out["ctxT"] = np.ascontiguousarray(ctx.transpose(0, 2, 1).reshape(B, DC, P, KEYS).transpose(0, 2, 1, 3))
    out["ctxN"] = np.ascontiguousarray(ctx.reshape(B, KC, P, D).transpose(0, 2, 1, 3))
    out["mask"] = np.asarray(mask_BxSxS2_ik1).reshape(TOK, KEYS)
    out["first"] = side(FIRST, {
        "wq": weight("L0_xattn_w_q"), "wk": weight("L0_xattn_w_k"), "wv": weight("L0_xattn_w_v"),
        "bq": rows_in(g["L0_xattn_b_q"]), "bk": rows_in(g["L0_xattn_b_k"]), "bv": rows_in(g["L0_xattn_b_v"])})
    out["table"] = _tables()
    b1 = g["L0_ffn_b1"].reshape(E0, FC, P).transpose(2, 0, 1)
    sbc = np.concatenate([g["L1_attn_W_sB"], g["L1_attn_W_sC"]], axis=0)
    out["later"] = side(LATER, {
        "wo": weight("L0_xattn_w_o"), "log_dt": rows_in(g["L0_attn_log_dt"]), "inv_w": rows_in(g["L0_attn_inv_w_real"]),
        "w_im": rows_in(g["L0_attn_w_imaginary"]), "B": rows_in(g["L0_attn_B"]), "P": rows_in(g["L0_attn_P"][0]),
        "C": rows_in(g["L0_attn_C"]), "D": rows_in(g["L0_attn_D"]), "keys": weight("L0_ffn_keys"),
        "rw": weight("L0_ffn_rw"), "b1": np.ascontiguousarray(b1), "w_in": weight("L1_attn_W_in"),
        "w_sbc": rows_in(sbc.T), "w_sd1": weight("L1_attn_W_sD1"), "w_sd2": weight("L1_attn_W_sD2"),
        "conv_w": rows_in(g["L1_attn_conv_w"]), "conv_b": rows_in(g["L1_attn_conv_b"]),
        "a_param": rows_in(g["L1_attn_A_param"]), "d_param": rows_in(g["L1_attn_D_param"]),
        "w_out": weight("L1_attn_W_out"), "gate_w": weight("L1_ffn_gate_w")})
    row = np.concatenate([g["L0_xattn_b_o"], g["L1_xattn_gamma"], g["L1_xattn_beta"], g["L0_ffn_rb"]])
    out["rows"] = np.ascontiguousarray(np.broadcast_to(row, (P, ROWS_W)))
    out["b2"] = g["L0_ffn_b2"]
    w1 = g["L0_ffn_w1"].transpose(0, 2, 1).reshape(E0, DC, P, F0).transpose(0, 2, 1, 3).reshape(E0, P, -1)
    w2 = g["L0_ffn_w2"].transpose(0, 2, 1).reshape(E0, FC, P, D).transpose(0, 2, 1, 3).reshape(E0, P, -1)
    out["w0"] = np.ascontiguousarray(np.concatenate([w1, w2], axis=2))
    up = np.stack([np.concatenate([g["L1_ffn_wg"], g["L1_ffn_sg"][None]]),
                   np.concatenate([g["L1_ffn_wu"], g["L1_ffn_su"][None]])], axis=1)
    up = up.transpose(0, 3, 1, 2).reshape(E1, DC, P, 2, P).transpose(0, 2, 3, 1, 4).reshape(E1, P, -1)
    down = np.concatenate([g["L1_ffn_wd"], g["L1_ffn_sd"][None]]).transpose(0, 2, 1)
    out["w1"] = np.ascontiguousarray(np.concatenate([up, down], axis=2))
    return out


def kernel(**inputs):
    import concourse.bacc as bacc
    from concourse.bass_utils import run_bass_kernel_spmd

    arrays = _layouts(**inputs)
    nc = bacc.Bacc("TRN2", target_bir_lowering=False, num_devices=1)
    drams = {n: nc.dram_tensor(f"in_{n}", a.shape, mybir.dt.from_np(a.dtype), kind="ExternalInput").ap()
             for n, a in arrays.items()}
    out = nc.dram_tensor("out", (TOK, D), F32, kind="ExternalOutput").ap()
    build(nc, drams, out)
    r = run_bass_kernel_spmd(nc, [{f"in_{n}": a for n, a in arrays.items()}], core_ids=[0])
    return r.results[0]["out"].reshape(B, S, D)
```

```python
from contextlib import ExitStack

import concourse.bass as bass
import numpy as np
from concourse import mybir

F32 = mybir.dt.float32
F32R = mybir.dt.float32r
I32 = mybir.dt.int32
ACT = mybir.ActivationFunctionType
ALU = mybir.AluOpType
AX = mybir.AxisListType

P = 128
B, S, D = 8, 64, 256
KEYS = 1024
TOK = B * S
TC = TOK // P
DC = D // P
KC = KEYS // P
HEADS, DH = 16, 16
HPC = HEADS // DC
PAIRS = HPC // 2
EPS = 1e-5
NSTATE, MODES = 16, 5
E0, TOP0, F0 = 16, 4, 1024
FC = F0 // P
E1, TOP1 = 9, 2
ROUTED1 = E1 - 1
DI, DISCR, KER = 512, 128, 4
CC = DI // P
NEG = -9000000000000000.0
EW = 2 * DC * F0
QW = EW // 4
UNITS = FC
GS = 2
GROUPS = NSTATE // GS
FB = 3
LAYERS = 6
Q_BANKS = (2, 3, 5, 6)
KEYS_AT, VALUES_AT, NEXT_KEYS_AT = (0, 2), (1, 3, 4, 6), (5, 7)
STACKS = D // 64
STAGE_AT, PHASE_AT, PLAN_END = 51 * 1024, 83 * 1024, 207 * 1024


def columns(widths):
    at, out = 0, {}
    for name, width in widths:
        out[name] = (at, at + width)
        at += width
    return out, at


FIRST, FIRST_W = columns([("wq", DC * 2 * D), ("bq", STACKS), ("wk", DC * D), ("bk", DC), ("wv", DC * D)])
TABLE, TABLE_W = columns([
    ("ident", P), ("quad", 4), ("pick", 2 * 64), ("before0", E0 * E0),
    ("before1", ROUTED1 * ROUTED1), ("ar", MODES), ("ai", MODES), ("cr", MODES), ("ci", MODES),
    ("alpha", B * MODES), ("beta", B * MODES), ("ones", P), ("minus_half", TC), ("minus_one", DC * MODES)])
LATER, LATER_W = columns([
    ("wo", DC * D), ("log_dt", DC), ("inv_w", DC * NSTATE), ("w_im", DC * NSTATE), ("B", DC * NSTATE * 2),
    ("P", DC * NSTATE * 2), ("C", DC * NSTATE * 2), ("D", DC), ("keys", DC * E0), ("rw", DC * E0),
    ("b1", E0 * FC), ("w_in", DC * 2 * DI), ("w_sbc", CC * 2 * NSTATE), ("w_sd1", CC * DISCR), ("w_sd2", DI),
    ("conv_w", CC * KER), ("conv_b", CC), ("a_param", CC * NSTATE), ("d_param", CC), ("w_out", CC * D),
    ("gate_w", DC * ROUTED1)])
ROWS, ROWS_W = columns([("bv", D), ("bo", D), ("gamma", D), ("beta", D), ("rb", E0)])


def part(tile, layout, name):
    a, b = layout[name]
    return tile[:, a:b]


class Order:

    def __init__(self, eng, sem):
        self.eng, self.sem, self.count = eng, sem, 0

    def mark(self, ins):
        self.count += 1
        ins.then_inc(self.sem, 1)

    def settle(self):
        self.eng.wait_ge(self.sem, self.count)

    def step(self, ins):
        self.mark(ins)
        self.settle()


def over(ap, n, axis):
    ap = ap.unsqueeze(axis)
    shape = list(ap.shape)
    shape[axis] = n
    return ap.broadcast_to(shape)


def build(nc, d, out):
    ctx = ExitStack()
    with ctx:
        names = set()

        def sem(name):
            assert name not in names
            names.add(name)
            return ctx.enter_context(nc.semaphore(name))

        base = -(-nc.sbuf_base // 64) * 64
        place = {"common": base, "stage": base + STAGE_AT, "phase": base + PHASE_AT}
        ends = {"common": place["stage"], "stage": place["phase"], "phase": base + PLAN_END}

        def sb(region, name, shape, dt=F32):
            width = int(np.prod(shape[1:])) * 4
            at = place[region]
            place[region] = at + -(-width // 64) * 64
            assert place[region] <= ends[region], (name, region, place[region] - ends[region])
            return nc.alloc_sbuf_tensor_at(name, shape, dt, offset=at)

        first = sb("common", "first", [P, FIRST_W])
        table = sb("common", "table", [P, TABLE_W])
        later = sb("common", "later", [P, LATER_W])
        rows = sb("common", "rows", [P, ROWS_W])
        b2 = sb("common", "b2", [E0, D])
        X = sb("common", "X", [P, TC, D])
        xn = sb("common", "xn", [P, TC, D])
        xnT = sb("common", "xnT", [P, DC, TOK])
        stats = sb("common", "stats", [P, TC, 6])
        moments = sb("common", "moments", [P, TC, 2])
        vareps = sb("common", "vareps", [P, TC])
        rstd = sb("common", "rstd", [P, TC])
        taps = sb("common", "taps", [P, B, DC])
        key_sum = sb("common", "key_sum", [P, DC, E0])
        key_sq = sb("common", "key_sq", [P, DC, E0])
        stat2 = sb("common", "stat2", [P, TC, 4])
        exp_a = sb("common", "exp_a", [P, CC * NSTATE])

        ident = part(table, TABLE, "ident")
        ones = part(table, TABLE, "ones")

        raw = [sb("stage", f"raw{k}", [P, EW]) for k in range(2)]

        place["stage"] = base + STAGE_AT
        ctx_hi, ctx_lo = [], []
        for k in range(2):
            ctx_hi.append(sb("stage", f"ctx_hi{k}", [P, DC, KEYS], F32R))
            ctx_lo.append(sb("stage", f"ctx_lo{k}", [P, DC, KEYS], F32R))
        top = place["phase"]
        ctx_raw = sb("phase", "ctx_raw", [P, DC, KEYS])
        w_kv = [[sb("phase", f"w_{n}_{part_of}", [P, DC, D], F32R) for part_of in ("hi", "lo")] for n in "kv"]
        k_stack = sb("phase", "k_stack", [P, STACKS, KEYS], F32R)
        V = sb("phase", "V", [P, KC, D])
        probs = [sb("phase", f"probs{k}", [P, KEYS]) for k in range(2)]
        probsT = [sb("phase", f"probsT{k}", [P, KC, PAIRS, P]) for k in range(DC)]
        q_part = [sb("phase", f"q_{n}", [P, STACKS, TOK], F32R) for n in ("hi", "lo")]
        q_stack = [sb("phase", f"q_stack_{n}", [P, STACKS, 4, S], F32R) for n in ("hi", "lo")]
        negmax_raw = [sb("phase", f"negmax_raw{k}", [P, 1]) for k in range(2)]
        negmax = [sb("phase", f"negmax{k}", [P, 1]) for k in range(2)]
        sums = [sb("phase", f"sums{k}", [P, PAIRS]) for k in range(DC)]
        inv_sums = [sb("phase", f"inv_sums{k}", [P, PAIRS]) for k in range(DC)]
        inv_diag = sb("phase", "inv_diag", [P, PAIRS, P])
        own = sb("phase", "own", [P, 4, S])
        attn = sb("phase", "attn", [P, DC, P])
        s4 = {n: sb("phase", "s4_" + n, [P, DC * NSTATE]) for n in ("wr", "wi", "ew")}
        s4v = sb("phase", "s4_v", [P, 7, DC * NSTATE])
        s4t = sb("phase", "s4_t", [P, DC * NSTATE])
        s4g = [sb("phase", f"s4_g{k}", [P, MODES, DC * NSTATE]) for k in range(6)]
        s4p = sb("phase", "s4_p", [P, 8, MODES * DC, NSTATE])
        s4s = sb("phase", "s4_s", [P, 14, MODES, DC])
        s4dt = sb("phase", "s4_dt", [P, DC])
        s4l = [sb("phase", f"s4_l{k}", [P, B, DC, MODES]) for k in range(2)]

        place["phase"] = top
        conv = [sb("phase", f"conv{k}", [P, DC, TOK]) for k in range(2)]
        w_hi, w_lo = [], []
        for k in range(2):
            w_hi.append(sb("phase", f"w_hi{k}", [P, EW], F32R))
            w_lo.append(sb("phase", f"w_lo{k}", [P, EW], F32R))
        x_hi = sb("phase", "x_hi", [P, DC, TOK], F32R)
        x_lo = sb("phase", "x_lo", [P, DC, TOK], F32R)
        h_full = [sb("phase", f"h_full{k}", [P, TOK]) for k in range(2)]
        h_hi = [sb("phase", f"h_hi{k}", [P, TOK], F32R) for k in range(4)]
        h_lo = [sb("phase", f"h_lo{k}", [P, TOK], F32R) for k in range(4)]
        logits = sb("phase", "logits", [P, TC, E0])
        squares = sb("phase", "squares", [P, D])
        sumsq = sb("phase", "sumsq", [P, TC])
        above = sb("phase", "above", [P, TC, E0, E0])
        tied = sb("phase", "tied", [P, TC, E0, E0])
        rank = sb("phase", "rank", [P, TC, E0])
        best = sb("phase", "best", [P, TC])
        gate = sb("phase", "gate", [P, TC, E0])
        gateT = sb("phase", "gateT", [E0, TC, P])

        place["phase"] = top
        place["stage"] = base + STAGE_AT
        mask = [sb("phase", f"mask{k}", [P, KEYS], I32) for k in range(2)]
        ctxT2, ctxN2 = [], []
        for p in range(TC):
            ctxT2.append(sb("phase" if p else "stage", f"ctxT2{p}", [P, 2, DC, KEYS]))
            ctxN2.append(sb("phase" if p else "stage", f"ctxN2{p}", [P, 2, KC, D]))
        probs2 = [sb("phase", f"probs2{k}", [P, KEYS]) for k in range(2)]
        probsT2 = sb("phase", "probsT2", [P, KC, P])
        mask += [sb("phase", f"mask{p}", [P, KEYS], I32) for p in range(2, TC)]

        place["phase"] = top
        place["stage"] = base + STAGE_AT
        Bbc = sb("phase", "Bbc", [P, NSTATE, TOK])
        Cbc = sb("phase", "Cbc", [P, NSTATE, TOK])
        a_pad = sb("phase", "a_pad", [P, CC, B, S + KER - 1])
        aT = sb("phase", "aT", [P, CC, TOK])
        gT = sb("phase", "gT", [P, CC, TOK])
        delta = sb("phase", "delta", [P, CC, TOK])
        drive = sb("phase", "drive", [P, CC, TOK])
        hidden = [sb("phase", f"hidden{k}", [P, GS, TOK]) for k in range(2)]
        gated_sum = sb("phase", "gated_sum", [P, TOK])
        bc_hi = sb("stage", "bc_hi", [P, TOK], F32R)
        bc_lo = sb("stage", "bc_lo", [P, TOK], F32R)
        one_hot = sb("stage", "one_hot", [P, P], F32R)
        lowT = sb("stage", "lowT", [P, TOK])
        acc = lowT
        decay = [sb("stage", f"decay{k}", [P, GS, TOK]) for k in range(2)]
        inject = [sb("stage", f"inject{k}", [P, GS, TOK]) for k in range(2)]
        shown = [sb("stage", f"shown{k}", [P, GS, TOK]) for k in range(2)]

        wf = [sb("phase", f"wf{k}", [P, 3 * D]) for k in range(FB)]
        place["phase"] = top
        act_f = [sb("phase", f"act_f{k}", [P, TOK]) for k in range(FB)]
        hid_f = [sb("phase", f"hid_f{k}", [P, TOK]) for k in range(FB)]
        logits1 = sb("phase", "logits1", [P, TC, ROUTED1])
        above1 = sb("phase", "above1", [P, TC, ROUTED1, ROUTED1])
        tied1 = sb("phase", "tied1", [P, TC, ROUTED1, ROUTED1])
        rank1 = sb("phase", "rank1", [P, TC, ROUTED1])
        best1 = sb("phase", "best1", [P, TC])
        gate1 = sb("phase", "gate1", [P, TC, E1])

        banks = ctx.enter_context(nc.psum_tensor("banks", [P, 8, 512], F32))

        def pb(i):
            return banks[:, i, :] if isinstance(i, int) else banks[:, bass.ds(i, 1), :].rearrange("p a n -> p (a n)")

        def two(i):
            return banks[:, 2 * i:2 * i + 2, :].rearrange("p a n -> p (a n)")

        loaded = {n: sem("loaded_" + n) for n in ("x", "first", "table", "later", "rows", "b2")}
        ctx_loaded = sem("ctx_loaded")
        raw_loaded = [sem(f"raw_loaded{k}") for k in range(2)]
        stored = sem("stored")
        dve_step, pool_step, act_step = sem("dve_step"), sem("pool_step"), sem("act_step")
        var_ready, rstd_ready, xn_ready = sem("var_ready"), sem("rstd_ready"), sem("xn_ready")
        xt_done, xt0_ready, xt1_ready = sem("xt_done"), sem("xt0_ready"), sem("xt1_ready")
        q_done, q_hi_ready, q_lo_ready, heads_ready = sem("q_done"), sem("q_hi_ready"), sem("q_lo_ready"), sem("heads_ready")
        w_hi_ready, w_lo_ready, ctx_hi_ready, ctx_lo_ready = (
            sem(n) for n in ("w_hi_ready", "w_lo_ready", "ctx_hi_ready", "ctx_lo_ready"))
        proj_done, k_hi_ready, piece_taken = sem("proj_done"), sem("k_hi_ready"), sem("piece_taken")
        scores_done, raw_max, max_ready, exp_done = sem("scores_done"), sem("raw_max"), sem("max_ready"), sem("exp_done")
        t_done, pt0_ready, pt1_ready = sem("t_done"), sem("pt0_ready"), sem("pt1_ready")
        quarter_done, masked_ready, attn_ready = sem("quarter_done"), sem("masked_ready"), sem("attn_ready")
        inverted, diag_ready, spread_taken, tile_added = (
            sem(n) for n in ("inverted", "diag_ready", "spread_taken", "tile_added"))
        out_done, x_updated = sem("out_done"), sem("x_updated")
        s4_norm = sem("s4_norm")
        s4_exp, taps_ready = sem("s4_exp"), sem("taps_ready")
        conv_ready, silu_ready, back_done = sem("conv_ready"), sem("silu_ready"), sem("back_done")

        hi_done, lo_done, xs_ready = sem("hi_done"), sem("lo_done"), sem("xs_ready")
        keys_ready, logits_done, ssq_ready = sem("keys_ready"), sem("logits_done"), sem("ssq_ready")
        centred, gate_exp, gate_ready = sem("centred"), sem("gate_exp"), sem("gate_ready")
        gate_turned, gateT_ready, bias_done, bias_added = (sem(n) for n in ("gate_turned", "gateT_ready", "bias_done", "bias_added"))
        up_done, gelu_done, h_hi_ready, h_ready = sem("up_done"), sem("gelu_done"), sem("h_hi_ready"), sem("h_ready")
        down_done, combined = sem("down_done"), sem("combined")
        ctxT2_loaded = [sem(f"ctxT2_loaded{p}") for p in range(TC)]
        ctxN2_loaded = [sem(f"ctxN2_loaded{p}") for p in range(TC)]
        mask_loaded = [sem(f"mask_loaded{p}") for p in range(TC)]
        maskneg_ready, scores2_done, max2_ready, exp2_done = (
            sem(n) for n in ("maskneg_ready", "scores2_done", "max2_ready", "exp2_done"))
        turned2, left2_ready, right2_ready, mixed_done = (sem(n) for n in ("turned2", "left2_ready", "right2_ready", "mixed_done"))
        mixed_taken = sem("mixed_taken")
        expa_ready, pads_ready, ag_done, a_ready, g_ready = (sem(n) for n in ("expa_ready", "pads_ready", "ag_done", "a_ready", "g_ready"))
        conv1_ready, a_silu, bc_done, bc_ready = (sem(n) for n in ("conv1_ready", "a_silu", "bc_done", "bc_ready"))
        low_done, low_ready, step_done, abs_ready, soft_ready, drive_ready = (
            sem(n) for n in ("low_done", "low_ready", "step_done", "abs_ready", "soft_ready", "drive_ready"))
        soft_taken, relu_ready, inject_free = sem("soft_taken"), sem("relu_ready"), sem("inject_free")
        Bbc_done, Bbc_ready, Cbc_done, Cbc_ready = (sem(n) for n in ("Bbc_done", "Bbc_ready", "Cbc_done", "Cbc_ready"))
        decay_ready, inject_ready, scanned, shown_ready, shown_used, y_ready, gated_ready = (
            sem(n) for n in ("decay_ready", "inject_ready", "scanned", "shown_ready", "shown_used", "y_ready", "gated_ready"))
        bc_hi_ready, one_hot_ready, first_tap, exp_soft, projected = (
            sem(n) for n in ("bc_hi_ready", "one_hot_ready", "first_tap", "exp_soft", "projected"))
        out1_done = sem("out1_done")
        wf_loaded = [sem(f"wf_loaded{k}") for k in range(FB)]
        logits1_done, centred1, gate1_exp, gate1_ready = (sem(n) for n in ("logits1_done", "centred1", "gate1_exp", "gate1_ready"))
        gu_done, silu1_ready, hid_ready, down1_done, combined1 = (
            sem(n) for n in ("gu_done", "silu1_ready", "hid_ready", "down1_done", "combined1"))

        def piece_at(b, step, last=False):
            return 8 * b + (3 + step - (last and step > NEXT_KEYS_AT[0]))

        block = ctx.enter_context(nc.Block())

        @block.sync
        def _(sp):
            sp.dma_start(X[:], d["x"].rearrange("(c p) n -> p c n", p=P)).then_inc(loaded["x"], 16)
            sp.dma_start(table[:], d["table"]).then_inc(loaded["table"], 16)
            sp.dma_start(first[:], d["first"]).then_inc(loaded["first"], 16)
            sp.dma_start(ctx_raw[:], d["ctxT"][0]).then_inc(ctx_loaded, 16)
            sp.dma_start(rows[:], d["rows"]).then_inc(loaded["rows"], 16)
            sp.dma_start(later[:], d["later"]).then_inc(loaded["later"], 16)
            sp.dma_start(b2[:], d["b2"]).then_inc(loaded["b2"], 16)
            with sp.Fori(0, B - 1) as n:
                sp.wait_ge(ctx_lo_ready, DC * n + DC)
                sp.dma_start(ctx_raw[:], d["ctxT"][bass.ds(n + 1, 1)].rearrange("a p c n -> p (a c) n")).then_inc(ctx_loaded, 16)
            for k, pieces in enumerate((piece_at(B - 2, VALUES_AT[-1]), 8 * B)):
                sp.wait_ge(proj_done, pieces)
                sp.dma_start(raw[k][:], d["w0"][k]).then_inc(raw_loaded[k], 16)
            sp.wait_ge(x_updated, 2)
            for m in range(2):
                sp.dma_start(mask[m][:], d["mask"][m * P:(m + 1) * P]).then_inc(mask_loaded[m], 16)
            with sp.Fori(0, E0 // 2 - 1) as n:
                for k in range(2):
                    sp.wait_ge(lo_done, 8 * n + 4 * (k + 1))
                    sp.dma_start(raw[k][:], d["w0"][bass.ds(2 * n + (2 + k), 1)].rearrange("a p n -> p (a n)"))\
                        .then_inc(raw_loaded[k], 16)
            for p in range(TC):
                if p == 0:
                    sp.wait_ge(lo_done, 4 * E0)
                elif p == 1:
                    sp.wait_ge(down_done, UNITS * (E0 - 1))
                elif p == 2:
                    sp.wait_ge(x_updated, 3)
                    for m in (2, 3):
                        sp.dma_start(mask[m][:], d["mask"][m * P:(m + 1) * P]).then_inc(mask_loaded[m], 16)
                sp.dma_start(ctxT2[p][:], d["ctxT"][2 * p:2 * p + 2].rearrange("b p c n -> p b c n"))\
                    .then_inc(ctxT2_loaded[p], 16)
                sp.dma_start(ctxN2[p][:], d["ctxN"][2 * p:2 * p + 2].rearrange("b p k n -> p b k n"))\
                    .then_inc(ctxN2_loaded[p], 16)
            sp.wait_ge(x_updated, 4)
            for k in range(FB):
                sp.dma_start(wf[k][:], d["w1"][k]).then_inc(wf_loaded[k], 16)
            with sp.Fori(0, E1 // FB - 1) as n:
                for k in range(FB):
                    sp.wait_ge(down1_done, FB * n + (k + 1))
                    sp.dma_start(wf[k][:], d["w1"][bass.ds(FB * n + (FB + k), 1)].rearrange("a p n -> p (a n)"))\
                        .then_inc(wf_loaded[k], 16)
            sp.wait_ge(x_updated, LAYERS)
            sp.dma_start(out.rearrange("(c p) n -> p c n", p=P), X[:]).then_inc(stored, 16)
            sp.wait_ge(stored, 16)

        @block.gpsimd
        def _(pool):
            order = Order(pool, pool_step)

            def rstd_of(k):
                pool.wait_ge(var_ready, k)
                nc.gpsimd.tensor_tensor(rstd[:], vareps[:], part(table, TABLE, "minus_half"), ALU.pow)\
                    .then_inc(rstd_ready, 1)

            def split_heads(b):
                for g in range(STACKS):
                    pool.wait_ge(q_lo_ready, g + 1)
                    if not (isinstance(b, int) and b == 0):
                        pool.wait_ge(scores_done, 8 * b + (2 * g - 6))
                    for q, to in zip(q_part, q_stack):
                        last = nc.gpsimd.tensor_tensor(
                            to[:, g], over(q[:, g, bass.ds(b * S, S)], 4, 1).bitcast(F32), over(part(table, TABLE, "quad"), S, 2),
                            ALU.mult)
                    last.then_inc(heads_ready, 1)

            def diagonals(b, c):
                pool.wait_ge(inverted, DC * b + (c + 1))
                if not (isinstance(b, int) and b == 0 and c == 0):
                    pool.wait_ge(quarter_done, 8 * b + (PAIRS * c - 3))
                nc.gpsimd.tensor_tensor(inv_diag[:], over(ident, PAIRS, 1), over(inv_sums[c][:], P, 2), ALU.mult)\
                    .then_inc(diag_ready, 1)

            def context_low(b, k):
                for c in range(DC):
                    pool.wait_ge(ctx_hi_ready, DC * b + (c + 1))
                    nc.gpsimd.tensor_tensor(ctx_lo[k][:, c, :], ctx_raw[:, c, :], ctx_hi[k][:, c, :].bitcast(F32), ALU.subtract)\
                        .then_inc(ctx_lo_ready, 1)

            def filter_taps():
                N, MN = DC * NSTATE, [P, MODES, DC * NSTATE]
                mul, add, sub = ALU.mult, ALU.add, ALU.subtract

                def tt(o, a, b, op):
                    order.step(nc.gpsimd.tensor_tensor(o, a, b, op))

                def modes(name):
                    return over(part(table, TABLE, name), N, 2)

                def poles(ap):
                    return over(ap, MODES, 1)

                def by_state(ap):
                    return over(ap, NSTATE, 2)

                pool.wait_ge(s4_exp, 2)
                pool.wait_ge(loaded["later"], 16)
                w3 = {n: s4[n][:].rearrange("p (c n) -> p c n", c=DC) for n in s4}
                im3 = part(later, LATER, "w_im").rearrange("p (c n) -> p c n", c=DC)
                tt(w3["wr"], w3["ew"], by_state(s4dt[:]), mul)
                tt(w3["wi"], im3, by_state(s4dt[:]), mul)
                wr, wi = poles(s4["wr"][:]), poles(s4["wi"][:])
                g = [x[:] for x in s4g]
                tt(g[0], wr, modes("cr"), mul)
                tt(g[1], wi, modes("ci"), mul)
                tt(g[0], g[0], g[1], add)
                tt(g[0], g[0], modes("ar"), add)
                tt(g[1], wr, modes("ci"), mul)
                tt(g[2], wi, modes("cr"), mul)
                tt(g[1], g[1], g[2], sub)
                tt(g[1], g[1], modes("ai"), add)
                tt(g[2], g[0], g[0], mul)
                tt(g[3], g[1], g[1], mul)
                tt(g[2], g[2], g[3], add)
                pool.sem_inc(s4_norm, 1)
                yield
                pool.wait_ge(s4_norm, 2)
                tt(g[3], g[0], g[2], mul)
                tt(g[4], g[1], g[2], mul)
                gr, gi = g[3], g[4]
                yield
                pair = {n: part(later, LATER, n).rearrange("p (n two) -> p n two", two=2) for n in ("B", "C", "P")}
                re = {n: pair[n][:, :, 0] for n in pair}
                im = {n: pair[n][:, :, 1] for n in pair}
                t = s4t[:]

                def both(o, a, b, e, f, op):
                    tt(o, a, b, mul)
                    tt(t, e, f, mul)
                    tt(o, o, t, op)

                both(s4v[:, 0], re["B"], re["C"], im["B"], im["C"], sub)
                both(s4v[:, 1], re["B"], im["C"], im["B"], re["C"], add)
                both(s4v[:, 2], re["B"], re["P"], im["B"], im["P"], add)
                both(s4v[:, 3], im["B"], re["P"], re["B"], im["P"], sub)
                both(s4v[:, 4], re["P"], re["C"], im["P"], im["C"], sub)
                both(s4v[:, 5], re["P"], im["C"], im["P"], re["C"], add)
                both(s4v[:, 6], re["P"], re["P"], im["P"], im["P"], add)
                yield
                prod = [s4p[:, k].rearrange("p (m c) n -> p m (c n)", m=MODES) for k in range(8)]
                for k in range(3):
                    if k:
                        yield
                    vr, vi = poles(s4v[:, 2 * k]), poles(s4v[:, 2 * k + 1])
                    tt(prod[2 * k], vr, gr, mul)
                    tt(g[5], vi, gi, mul)
                    tt(prod[2 * k], prod[2 * k], g[5], add)
                    tt(prod[2 * k + 1], vi, gr, mul)
                    tt(g[5], vr, gi, mul)
                    tt(prod[2 * k + 1], prod[2 * k + 1], g[5], sub)
                tt(prod[6], poles(s4v[:, 6]), gr, mul)
                tt(prod[7], poles(s4v[:, 6]), gi, mul)
                yield
                flat = s4p[:].rearrange("p k m n -> p (k m) n")
                n = NSTATE // 2
                while n:
                    tt(flat[:, :, 0:n], flat[:, :, 0:n], flat[:, :, n:2 * n], add)
                    n //= 2
                Z = [s4s[:, k] for k in range(14)]
                for k in range(8):
                    tt(Z[k], s4p[:, k, :, 0].rearrange("p (m c) -> p m c", m=MODES), over(s4dt[:], MODES, 1), mul)
                yield
                cr, ci = (over(part(table, TABLE, n), DC, 2) for n in ("cr", "ci"))
                dr, di, tr, ti, u0, u1 = Z[8:14]
                tt(dr, cr, Z[6], mul)
                tt(u0, ci, Z[7], mul)
                tt(dr, dr, u0, add)
                order.step(nc.gpsimd.tensor_scalar_add(dr, dr, 1.0))
                tt(di, ci, Z[6], mul)
                tt(u0, cr, Z[7], mul)
                tt(di, di, u0, sub)
                tt(u0, Z[2], Z[4], mul)
                tt(u1, Z[3], Z[5], mul)
                tt(u0, u0, u1, sub)
                tt(u1, Z[2], Z[5], mul)
                tt(tr, Z[3], Z[4], mul)
                tt(u1, u1, tr, add)
                tt(tr, cr, u0, mul)
                tt(ti, ci, u1, mul)
                tt(tr, tr, ti, sub)
                tt(ti, cr, u1, mul)
                tt(u0, ci, u0, mul)
                tt(ti, ti, u0, add)
                yield
                tt(u0, dr, dr, mul)
                tt(u1, di, di, mul)
                tt(u0, u0, u1, add)
                one = part(table, TABLE, "minus_one").rearrange("p (m c) -> p m c", m=MODES)
                tt(u0, u0, one, ALU.pow)
                tt(u1, tr, dr, mul)
                tt(Z[2], ti, di, mul)
                tt(u1, u1, Z[2], add)
                tt(u1, u1, u0, mul)
                tt(Z[0], Z[0], u1, sub)
                tt(u1, ti, dr, mul)
                tt(Z[2], tr, di, mul)
                tt(u1, u1, Z[2], sub)
                tt(u1, u1, u0, mul)
                tt(Z[1], Z[1], u1, sub)
                yield
                for name, k in (("alpha", 0), ("beta", 1)):
                    for c in range(DC):
                        tt(s4l[k][:, :, c, :], over(Z[k][:, :, c], B, 1),
                           part(table, TABLE, name).rearrange("p (l m) -> p l m", l=B), mul)
                tt(s4l[0][:], s4l[0][:], s4l[1][:], add)
                for m in range(1, MODES):
                    tt(s4l[0][:, :, :, 0], s4l[0][:, :, :, 0], s4l[0][:, :, :, m], add)
                order.step(nc.gpsimd.tensor_copy(taps[:], s4l[0][:, :, :, 0]))
                nc.gpsimd.tensor_tensor(taps[:, 0, :], taps[:, 0, :], part(later, LATER, "D"), add).then_inc(taps_ready, 1)

            pool.wait_ge(loaded["table"], 16)
            rstd_of(1)
            for j, n in enumerate(("wk", "wv")):
                pool.wait_ge(w_hi_ready, j + 1)
                nc.gpsimd.tensor_tensor(w_kv[j][1][:], part(first, FIRST, n).rearrange("p (c n) -> p c n", c=DC),
                                        w_kv[j][0][:].bitcast(F32), ALU.subtract).then_inc(w_lo_ready, 1)
            context_low(0, 0)
            split_heads(0)
            def split_low(e, k):
                for q in range(4):
                    cols = slice(q * QW, (q + 1) * QW)
                    pool.wait_ge(hi_done, 4 * e + (q + 1))
                    nc.gpsimd.tensor_tensor(w_lo[k][:, cols], raw[k][:, cols], w_hi[k][:, cols].bitcast(F32), ALU.subtract)\
                        .then_inc(lo_done, 1)

            taps_parts = filter_taps()
            next(taps_parts)
            context_low(1, 1)
            diagonals(0, 0)
            split_heads(1)
            diagonals(0, 1)
            next(taps_parts)
            context_low(2, 0)
            diagonals(1, 0)
            split_heads(2)
            with pool.Fori(1, B // 2 - 1) as n:
                for k in range(2):
                    diagonals(2 * n + (k - 1), 1)
                    context_low(2 * n + (k + 1), 1 - k)
                    diagonals(2 * n + k, 0)
                    split_heads(2 * n + (k + 1))
            diagonals(B - 3, 1)
            next(taps_parts)
            context_low(B - 1, 1)
            diagonals(B - 2, 0)
            split_heads(B - 1)
            next(taps_parts)
            diagonals(B - 2, 1)
            for _ in range(2):
                next(taps_parts)
            diagonals(B - 1, 0)
            for _ in range(2):
                next(taps_parts)
            diagonals(B - 1, 1)
            for _ in taps_parts:
                pass
            rstd_of(2)
            split_low(0, 0)
            rstd_of(3)

            keys3 = part(later, LATER, "keys").rearrange("p (c e) -> p c e", c=DC)
            rw3 = part(later, LATER, "rw").rearrange("p (c e) -> p c e", c=DC)
            order.step(nc.gpsimd.tensor_tensor(key_sum[:], keys3, keys3, ALU.add))
            nc.gpsimd.tensor_tensor(key_sum[:], key_sum[:], rw3, ALU.add).then_inc(keys_ready, 1)
            order.step(nc.gpsimd.tensor_tensor(key_sq[:], keys3, keys3, ALU.mult))
            nc.gpsimd.tensor_scalar(key_sq[:], key_sq[:], -1.0, 0.0, ALU.mult, ALU.add).then_inc(keys_ready, 1)

            split_low(1, 1)
            with pool.Fori(0, E0 // 2 - 1) as n:
                for k in range(2):
                    split_low(2 * n + (2 + k), k)

            def mask_term(p):
                pool.wait_ge(mask_loaded[p], 16)
                nc.gpsimd.tensor_scalar(mask[p][:].bitcast(F32), mask[p][:], 0, NEG * 16, ALU.is_equal, ALU.mult)\
                    .then_inc(maskneg_ready, 1)

            def rstd_of_pair(p):
                pool.wait_ge(var_ready, 4 + p + 1)
                nc.gpsimd.tensor_tensor(stat2[:, p, 3:4], stat2[:, p, 2:3], part(table, TABLE, "minus_half")[:, 0:1], ALU.pow)\
                    .then_inc(rstd_ready, 1)

            mask_term(0)
            mask_term(1)
            rstd_of(4)
            mask_term(2)
            mask_term(3)
            for p in range(TC):
                rstd_of_pair(p)

            pool.wait_ge(x_updated, 4)
            nc.gpsimd.memset(a_pad[:, :, :, 0:KER - 1], 0.0).then_inc(pads_ready, 1)
            nc.gpsimd.memset(bc_hi[:].bitcast(F32), 0.0).then_inc(pads_ready, 1)
            nc.gpsimd.memset(bc_lo[:].bitcast(F32), 0.0).then_inc(pads_ready, 1)
            for k in range(2):
                last = nc.gpsimd.memset(decay[k][:].rearrange("p g (b s) -> p (g b) s", s=S)[:, :, 0:1], 0.0)
            last.then_inc(pads_ready, 1)
            rstd_of(5 + TC)

            def injected(m, first_chunk):
                for g in range(GROUPS):
                    if first_chunk:
                        pool.wait_ge(Bbc_ready, GS * (g + 1))
                    pool.wait_ge(drive_ready, 1 if first_chunk else CC)
                    if g >= 2 or not first_chunk:
                        pool.wait_ge(scanned, GROUPS * m + (g - 1))
                        pool.sem_inc(inject_free, 1)
                    nc.gpsimd.tensor_tensor(inject[g % 2][:], Bbc[:, GS * g:GS * (g + 1), :],
                                            over(drive_of(m), GS, 1), ALU.mult).then_inc(inject_ready, 1)

            def drive_of(m):
                return drive[:].rearrange("p c n -> p (c n)")[:, bass.ds(m * TOK, TOK)]

            injected(0, True)
            with pool.Fori(1, CC) as m:
                injected(m, False)
            rstd_of(6 + TC)

        @block.scalar
        def _(act):
            def transposed(k):
                act.wait_ge(xt_done, 2 * k - 1)
                nc.scalar.activation(xnT[:, 0, :], pb(0), ACT.Copy).then_inc(xt0_ready, 1)

            def context_high(b, k):
                act.wait_ge(ctx_loaded, 16 * b + 16)
                for c in range(DC):
                    nc.scalar.activation(ctx_hi[k][:, c, :], ctx_raw[:, c, :], ACT.Copy).then_inc(ctx_hi_ready, 1)

            def key_piece(piece, c, half):
                act.wait_ge(proj_done, piece)
                for g in range(2):
                    at = slice(64 * g, 64 * g + 64)
                    nc.scalar.activation(k_stack[at, DC * c + g, half * 512:(half + 1) * 512], pb(4)[at, :], ACT.Identity,
                                         bias=part(first, FIRST, "bk")[at, c:c + 1]).then_inc(k_hi_ready, 1)

            def batch(b, par, last):
                for i in range(8):
                    if i in KEYS_AT:
                        key_piece(piece_at(b, i), 1, KEYS_AT.index(i))
                    if i in NEXT_KEYS_AT and not last:
                        key_piece(piece_at(b, i), 0, NEXT_KEYS_AT.index(i))
                    if i >= 1:
                        second_half(b, i - 1)
                    elif not (isinstance(b, int) and b == 0):
                        second_half(b - 1, 7)
                    act.wait_ge(max_ready, 8 * b + (i + 1))
                    if i >= 2 or not (isinstance(b, int) and b == 0):
                        act.wait_ge(t_done, 16 * b + 2 * (i - 1))
                    nc.scalar.activation(probs[i % 2][:], two(i % 2), ACT.Exp, bias=negmax[i % 2][:], scale=0.25,
                                         accum_out=sums[i // PAIRS][:, i % PAIRS:i % PAIRS + 1]).then_inc(exp_done, 1)
                    if i == 2 and not last:
                        context_high(b + 1, 1 - par)

            def second_half(b, i):
                c, j = divmod(i, PAIRS)
                act.wait_ge(t_done, 16 * b + 2 * i + 2)
                nc.scalar.activation(probsT[c][:, KC // 2:KC, j, :], pb(6).rearrange("p (k n) -> p k n", n=P),
                                     ACT.Copy).then_inc(pt1_ready, 1)

            act.wait_ge(loaded["first"], 16)
            for j, n in enumerate(("wk", "wv")):
                nc.scalar.activation(w_kv[j][0][:], part(first, FIRST, n).rearrange("p (c n) -> p c n", c=DC), ACT.Copy)\
                    .then_inc(w_hi_ready, 1)
            transposed(1)
            context_high(0, 0)
            for g in range(STACKS):
                act.wait_ge(q_done, g + 1)
                nc.scalar.activation(q_part[0][:, g, :], pb(Q_BANKS[g]), ACT.Identity, bias=part(first, FIRST, "bq")[:, g:g + 1])\
                    .then_inc(q_hi_ready, 1)
            for half in range(2):
                key_piece(half + 1, 0, half)
            act.wait_ge(loaded["later"], 16)
            nc.scalar.activation(s4dt[:], part(later, LATER, "log_dt"), ACT.Exp).then_inc(s4_exp, 1)
            nc.scalar.activation(s4["ew"][:], part(later, LATER, "inv_w"), ACT.Exp).then_inc(s4_exp, 1)
            batch(0, 0, False)
            with act.Fori(0, B // 2 - 1) as n:
                for k in range(2):
                    batch(2 * n + (1 + k), 1 - k, False)
            batch(B - 1, 1, True)
            second_half(B - 1, 7)
            def split_high(e, half_e, k, q):
                if q == 0:
                    act.wait_ge(raw_loaded[k], 16 * half_e + 16)
                    if not (isinstance(e, int) and e < 2):
                        act.wait_ge(down_done, UNITS * (e - 1))
                cols = slice(q * QW, (q + 1) * QW)
                nc.scalar.activation(w_hi[k][:, cols], raw[k][:, cols], ACT.Copy).then_inc(hi_done, 1)

            act.wait_ge(out_done, TC)
            for q in range(4):
                split_high(0, 0, 0, q)
            transposed(2)
            for c in range(DC):
                act.wait_ge(conv_ready, c + 1)
                nc.scalar.activation(conv[1][:, c, :], conv[0][:, c, :], ACT.Silu).then_inc(silu_ready, 1)

            def gelu(e, u):
                act.wait_ge(up_done, UNITS * e + (u + 1))
                if not (isinstance(e, int) and e == 0 and u < 2):
                    act.wait_ge(h_hi_ready, UNITS * e + (u - 1))
                    act.wait_ge(h_ready, UNITS * e + (u - 1))
                nc.scalar.activation(h_full[u % 2][:], pb(u % 2), ACT.Gelu,
                                     bias=part(later, LATER, "b1")[:, bass.ds(UNITS * e + u, 1)]).then_inc(gelu_done, 1)

            def pair_of_experts(n, is_first, is_last):
                for k in range(2):
                    e = 2 * n + k
                    for u in range(UNITS):
                        gelu(e, u)
                        if 2 <= u < 6 and not (is_last and k) and not (is_first and not k):
                            split_high(e + 1, n + k, 1 - k, u - 2)
                        if is_first and k == 0 and u == 5:
                            act.wait_ge(centred, 1)
                            nc.scalar.activation(gate[:], logits[:], ACT.Exp).then_inc(gate_exp, 1)
                        if is_first and k == 1 and u == 3:
                            act.wait_ge(gate_turned, 1)
                            nc.scalar.activation(gateT[:], pb(3)[0:E0, :].rearrange("e (t n) -> e t n", t=TC), ACT.Copy)\
                                .then_inc(gateT_ready, 1)

            transposed(3)
            act.wait_ge(xt1_ready, 3)
            act.wait_ge(xt0_ready, 3)
            nc.scalar.activation(x_hi[:], xnT[:], ACT.Copy).then_inc(xs_ready, 1)
            for q in range(4):
                split_high(1, 0, 1, q)
            for t in range(TC):
                if t:
                    act.wait_ge(ssq_ready, t)
                nc.scalar.activation(squares[:], xn[:, t, :], ACT.Square, accum_out=sumsq[:, t:t + 1]).then_inc(ssq_ready, 1)
            pair_of_experts(0, True, False)
            with act.Fori(1, E0 // 2 - 1) as n:
                pair_of_experts(n, False, False)
            pair_of_experts(E0 // 2 - 1, False, True)

            transposed(4)

            def weights2(p):
                k = p % 2
                act.wait_ge(max2_ready, p + 1)
                nc.scalar.activation(probs2[k][:], probs2[k][:], ACT.Exp, bias=stat2[:, p, 0:1], scale=1.0 / 16,
                                     accum_out=stat2[:, p, 1:2]).then_inc(exp2_done, 1)

            def right_half(p):
                act.wait_ge(turned2, 2 * p + 2)
                if p:
                    act.wait_ge(mixed_done, p)
                nc.scalar.activation(probsT2[:, KC // 2:KC, :], pb(5).rearrange("p (k n) -> p k n", n=P), ACT.Copy)\
                    .then_inc(right2_ready, 1)

            weights2(0)
            weights2(1)
            for p in range(TC):
                right_half(p)
                if p + 2 < TC:
                    weights2(p + 2)

            act.wait_ge(loaded["later"], 16)
            nc.scalar.activation(exp_a[:], part(later, LATER, "a_param"), ACT.Exp, scale=-1.0).then_inc(expa_ready, 1)
            transposed(5)
            act.wait_ge(pads_ready, 4)
            conv_w = part(later, LATER, "conv_w").rearrange("p (c k) -> p c k", c=CC)
            for m in range(CC):
                act.wait_ge(ag_done, m + 1)
                nc.scalar.activation(hidden[m // 2][:, m % 2, :], pb(2 + m), ACT.Identity, scale=conv_w[:, m, KER - 1:KER],
                                     bias=part(later, LATER, "conv_b")[:, m:m + 1]).then_inc(first_tap, 1)
                nc.scalar.activation(a_pad[:, m, :, KER - 1:], pb(2 + m).rearrange("p (b s) -> p b s", b=B), ACT.Copy)\
                    .then_inc(a_ready, 1)
            nc.scalar.activation(one_hot[:], ident, ACT.Copy).then_inc(one_hot_ready, 1)
            for m in range(CC):
                act.wait_ge(conv1_ready, m + 1)
                nc.scalar.activation(aT[:, m, :], hidden[m // 2][:, m % 2, :], ACT.Silu).then_inc(a_silu, 1)
                act.wait_ge(ag_done, CC + m + 1)
                nc.scalar.activation(gT[:, m, :], pb(2 + m), ACT.Silu).then_inc(g_ready, 1)
            act.wait_ge(low_done, 1)
            nc.scalar.activation(lowT[:], pb(7), ACT.Copy).then_inc(low_ready, 1)
            act.wait_ge(bc_done, 1)
            nc.scalar.activation(bc_hi[0:2 * NSTATE, :], pb(6)[0:2 * NSTATE, :], ACT.Copy).then_inc(bc_hi_ready, 1)
            for m in range(CC):
                act.wait_ge(relu_ready, m + 1)
                nc.scalar.activation(drive[:, m, :], pb(2 + m), ACT.Abs, bias=part(later, LATER, "d_param")[:, m:m + 1])\
                    .then_inc(abs_ready, 1)
                act.wait_ge(abs_ready, m + 1)
                nc.scalar.activation(drive[:, m, :], drive[:, m, :], ACT.Exp, scale=-1.0).then_inc(exp_soft, 1)
            act.wait_ge(exp_soft, CC)
            for m in range(CC):
                nc.scalar.activation(drive[:, m, :], drive[:, m, :], ACT.Ln, bias=ones[:, 0:1]).then_inc(soft_ready, 1)

            def decays(m, first_chunk):
                for g in range(GROUPS):
                    if first_chunk:
                        for s in range(GS):
                            act.wait_ge(Bbc_done, GS * g + s + 1)
                            nc.scalar.activation(Bbc[:, GS * g + s, :], pb(s), ACT.Copy).then_inc(Bbc_ready, 1)
                    if g == 0:
                        act.wait_ge(drive_ready, m + 1)
                    if g >= 2 or not first_chunk:
                        act.wait_ge(scanned, GROUPS * m + (g - 1))
                    row = delta[:, m, :] if first_chunk else delta[:, bass.ds(m, 1), :].rearrange("p c n -> p (c n)")
                    for s in range(GS):
                        last = nc.scalar.activation(
                            decay[g % 2][:, s, :].rearrange("p (b s) -> p b s", b=B)[:, :, 1:S],
                            row.rearrange("p (b s) -> p b s", b=B)[:, :, 1:S], ACT.Copy,
                            scale=exp_a[:, bass.ds(NSTATE * m + (GS * g + s), 1)])
                    last.then_inc(decay_ready, 1)

            act.wait_ge(expa_ready, 1)
            decays(0, True)
            with act.Fori(1, CC) as m:
                decays(m, False)

            transposed(6)
            act.wait_ge(centred1, 1)
            nc.scalar.activation(logits1[:], logits1[:], ACT.Exp).then_inc(gate1_exp, 1)

            def silu1(n):
                for k in range(FB):
                    act.wait_ge(gu_done, FB * n + (k + 1))
                    if not isinstance(n, int):
                        act.wait_ge(hid_ready, FB * n + (k - 2))
                    nc.scalar.activation(act_f[k][:], pb(2 * k), ACT.Silu).then_inc(silu1_ready, 1)

            silu1(0)
            with act.Fori(1, E1 // FB) as n:
                silu1(n)

        @block.vector
        def _(dve):
            order = Order(dve, dve_step)

            def layer_norm(k):
                for t in range(TC):
                    last = nc.vector.bn_stats(stats[:, t, :], X[:, t, :])
                order.step(last)
                for t in range(TC):
                    last = nc.vector.bn_aggr(moments[:, t, :], stats[:, t, :])
                order.step(last)
                nc.vector.tensor_scalar_add(vareps[:], moments[:, :, 1], EPS).then_inc(var_ready, 1)
                dve.wait_ge(rstd_ready, k)
                for t in range(TC):
                    last = nc.vector.tensor_scalar(xn[:, t, :], X[:, t, :], moments[:, t, 0:1], rstd[:, t:t + 1],
                                                   ALU.subtract, ALU.mult)
                last.then_inc(xn_ready, 1)

            def transposed(k):
                dve.wait_ge(xt_done, 2 * k)
                nc.vector.tensor_copy(xnT[:, 1, :], pb(1)).then_inc(xt1_ready, 1)

            dve.wait_ge(loaded["x"], 16)
            layer_norm(1)
            transposed(1)

            dve.wait_ge(loaded["rows"], 16)
            dve.wait_ge(xn_ready, 1)
            nc.vector.tensor_tensor(X[:], X[:], over(part(rows, ROWS, "bo"), TC, 1), ALU.add).then_inc(tile_added, 1)
            bq, bk, bv = part(first, FIRST, "bq"), part(first, FIRST, "bk"), part(rows, ROWS, "bv")
            dve.wait_ge(loaded["first"], 16)
            for g in range(STACKS):
                dve.wait_ge(q_hi_ready, g + 1)
                nc.vector.scalar_tensor_tensor(q_part[1][:, g, :], pb(Q_BANKS[g]), bq[:, g:g + 1], q_part[0][:, g, :].bitcast(F32),
                                               ALU.add, ALU.subtract).then_inc(q_lo_ready, 1)

            def key_piece(k_piece, c, half):
                cols = slice(half * 512, (half + 1) * 512)
                for g in range(2):
                    at, to = slice(64 * g, 64 * g + 64), slice(64 - 64 * g, 128 - 64 * g)
                    dve.wait_ge(k_hi_ready, 2 * k_piece + (g - 1))
                    last = nc.vector.scalar_tensor_tensor(
                        k_stack[to, DC * c + g, cols], pb(4)[at, :], bk[at, c:c + 1],
                        k_stack[at, DC * c + g, cols].bitcast(F32), ALU.add, ALU.subtract)
                last.then_inc(piece_taken, 1)

            def value_piece(piece, b, v):
                dve.wait_ge(proj_done, piece)
                if not (isinstance(b, int) and b == 0):
                    dve.wait_ge(quarter_done, 8 * b + (v - 3))
                nc.vector.tensor_tensor(V[:, 2 * v:2 * v + 2, :], pb(4).rearrange("p (k n) -> p k n", k=2), over(bv, 2, 1), ALU.add)\
                    .then_inc(piece_taken, 1)

            def invert_sums(b, c):
                dve.wait_ge(exp_done, 8 * b + PAIRS * (c + 1))
                if not (isinstance(b, int) and b == 0):
                    dve.wait_ge(diag_ready, DC * (b - 1) + (c + 1))
                nc.vector.reciprocal(inv_sums[c][:], sums[c][:]).then_inc(inverted, 1)

            def first_half(b, i):
                c, j = divmod(i, PAIRS)
                dve.wait_ge(t_done, 16 * b + 2 * i + 1)
                nc.vector.tensor_copy(probsT[c][:, 0:KC // 2, j, :], pb(5).rearrange("p (k n) -> p k n", n=P))\
                    .then_inc(pt0_ready, 1)

            def gather(b, par, c):
                dve.wait_ge(quarter_done, 8 * b + PAIRS * (c + 1))
                if not (isinstance(b, int) and b == 0 and c == 0):
                    dve.wait_ge(attn_ready, 2 * b + c)
                nc.vector.tensor_copy(own[:], pb(7)[:, 256:512].rearrange("p (h s) -> p h s", h=4)).then_inc(spread_taken, 1)
                dve.wait_ge(spread_taken, 2 * b + (c + 1))
                nc.vector.tensor_tensor(own[:], pb(7)[:, 0:256].rearrange("p (h s) -> p h s", h=4), own[:], ALU.mult)\
                    .then_inc(masked_ready, 1)
                dve.wait_ge(masked_ready, 2 * b + (c + 1))
                nc.vector.tensor_reduce(attn[:, c, par * S:(par + 1) * S], own[:].rearrange("p h s -> p s h"),
                                        AX.X, ALU.add).then_inc(attn_ready, 1)

            def add_tile(n):
                dve.wait_ge(out_done, n + 1)
                dve.wait_ge(tile_added, n + 1)
                to = X[:, n, :] if isinstance(n, int) else X[:, bass.ds(n, 1), :].rearrange("p t n -> p (t n)")
                nc.vector.tensor_tensor(to, to, pb(7)[:, 256:512], ALU.add).then_inc(tile_added, 1)

            def batch(b, par, last, tile=None):
                later_one = not (isinstance(b, int) and b == 0)
                for i in range(8):
                    if i in KEYS_AT:
                        key_piece(4 * b + 3 + KEYS_AT.index(i), 1, KEYS_AT.index(i))
                    elif i in VALUES_AT[1:]:
                        value_piece(piece_at(b, i, last), b, VALUES_AT.index(i))
                    elif i in NEXT_KEYS_AT and not last:
                        key_piece(4 * b + 5 + NEXT_KEYS_AT.index(i), 0, NEXT_KEYS_AT.index(i))
                    if i == 5 and tile is not None:
                        add_tile(tile)
                    if i == 4:
                        invert_sums(b, 0)
                    if i == 0 and later_one:
                        invert_sums(b - 1, 1)
                    dve.wait_ge(scores_done, 8 * b + (i + 1))
                    nc.vector.tensor_reduce(negmax_raw[i % 2][:], two(i % 2),
                                            AX.X, ALU.max, negate=True).then_inc(raw_max, 1)
                    dve.wait_ge(raw_max, 8 * b + (i + 1))
                    nc.vector.tensor_scalar(negmax[i % 2][:], negmax_raw[i % 2][:], 0.25, None, ALU.mult)\
                        .then_inc(max_ready, 1)
                    if i == VALUES_AT[0]:
                        value_piece(piece_at(b, i), b, 0)
                    if i == 0 and later_one:
                        gather(b - 1, 1 - par, 0)
                    if i == 4 and later_one:
                        gather(b - 1, 1 - par, 1)
                    if i >= 1:
                        first_half(b, i - 1)
                    elif later_one:
                        first_half(b - 1, 7)

            for half in range(2):
                key_piece(half + 1, 0, half)
            batch(0, 0, False)
            dve.wait_ge(s4_norm, 1)
            nc.vector.reciprocal(s4g[2][:], s4g[2][:]).then_inc(s4_norm, 1)
            with dve.Fori(0, B // 2 - 1) as n:
                batch(2 * n + 1, 1, False)
                batch(2 * n + 2, 0, False, n)
            batch(B - 1, 1, True)
            invert_sums(B - 1, 1)
            gather(B - 1, 1, 0)
            first_half(B - 1, 7)
            gather(B - 1, 1, 1)
            add_tile(TC - 1)
            dve.wait_ge(tile_added, TC + 1)
            dve.sem_inc(x_updated, 1)
            dve.wait_ge(x_updated, 1)
            layer_norm(2)
            transposed(2)
            dve.wait_ge(taps_ready, 1)
            dve.wait_ge(xt0_ready, 2)
            dve.wait_ge(xt1_ready, 2)
            for c in range(DC):
                order.step(nc.vector.tensor_scalar(conv[0][:, c, :], xnT[:, c, :], taps[:, 0, c:c + 1], None, ALU.mult))
                for l in range(1, B):
                    later_cols = conv[0][:, c, l * S:TOK]
                    ins = nc.vector.scalar_tensor_tensor(later_cols, xnT[:, c, 0:TOK - l * S], taps[:, l, c:c + 1],
                                                         later_cols, ALU.mult, ALU.add)
                    if l < B - 1:
                        order.step(ins)
                    else:
                        ins.then_inc(conv_ready, 1)
            for h in range(2):
                dve.wait_ge(back_done, h + 1)
                last = nc.vector.tensor_tensor(X[:, 2 * h:2 * h + 2, :], X[:, 2 * h:2 * h + 2, :],
                                               pb(2 + h).rearrange("p (t n) -> p t n", t=2), ALU.add)
            last.then_inc(x_updated, 1)

            def top(values, n, before, count, greater, equal, place_of):
                one, other = over(values, n, 3), over(values, n, 2)
                order.step(nc.vector.tensor_tensor(greater, other, one, ALU.is_gt))
                order.step(nc.vector.tensor_tensor(equal, other, one, ALU.is_equal))
                lower = over(part(table, TABLE, before), TC, 1)
                flat = equal.rearrange("p t a b -> p t (a b)")
                order.step(nc.vector.tensor_tensor(flat, flat, lower, ALU.mult))
                order.step(nc.vector.tensor_tensor(greater, greater, equal, ALU.add))
                order.step(nc.vector.tensor_reduce(place_of, greater, AX.X, ALU.add))
                order.step(nc.vector.tensor_scalar(place_of, place_of, float(count), None, ALU.is_lt))

            def router():
                dve.wait_ge(logits_done, 1)
                dve.wait_ge(ssq_ready, TC)
                rb = rank[:, 0, :]
                order.step(nc.vector.tensor_tensor(rb, pb(2)[:, TC * E0:(TC + 1) * E0], part(rows, ROWS, "rb"), ALU.add))
                for t in range(TC):
                    last = nc.vector.scalar_tensor_tensor(logits[:, t, :], pb(2)[:, t * E0:(t + 1) * E0], sumsq[:, t:t + 1], rb,
                                                          ALU.subtract, ALU.add)
                order.step(last)
                top(logits[:], E0, "before0", TOP0, above[:], tied[:], rank[:])
                order.step(nc.vector.tensor_reduce(best[:], logits[:], AX.X, ALU.max))
                nc.vector.tensor_tensor(logits[:], logits[:], over(best[:], E0, 2), ALU.subtract).then_inc(centred, 1)

            def router_end():
                dve.wait_ge(gate_exp, 1)
                order.step(nc.vector.tensor_tensor(gate[:], gate[:], rank[:], ALU.mult))
                order.step(nc.vector.tensor_reduce(best[:], gate[:], AX.X, ALU.add))
                order.step(nc.vector.reciprocal(best[:], best[:]))
                nc.vector.tensor_tensor(gate[:], gate[:], over(best[:], E0, 2), ALU.mult).then_inc(gate_ready, 1)
                dve.wait_ge(gate_ready, 1)

            def split_hidden(e, u):
                dve.wait_ge(gelu_done, UNITS * e + (u + 1))
                if not (isinstance(e, int) and e == 0 and u < 4):
                    dve.wait_ge(down_done, UNITS * e + (u - 3))
                nc.vector.tensor_copy(h_hi[u % 4][:], h_full[u % 2][:]).then_inc(h_hi_ready, 1)
                dve.wait_ge(h_hi_ready, UNITS * e + (u + 1))
                nc.vector.tensor_tensor(h_lo[u % 4][:], h_full[u % 2][:], h_hi[u % 4][:].bitcast(F32), ALU.subtract)\
                    .then_inc(h_ready, 1)

            def combine(e, k, is_first):
                dve.wait_ge(down_done, UNITS * (e + 1))
                if not is_first:
                    dve.wait_ge(combined, e)
                for t in range(TC):
                    y = pb(4 + 2 * k + t // 2)[:, (t % 2) * D:(t % 2 + 1) * D]
                    last = nc.vector.scalar_tensor_tensor(X[:, t, :], y, gate[:, t, bass.ds(e, 1)], X[:, t, :],
                                                          ALU.mult, ALU.add)
                last.then_inc(combined, 1)

            def pair_of_experts(n, is_first):
                for k in range(2):
                    e = 2 * n + k
                    for u in range(UNITS):
                        split_hidden(e, u)
                        if is_first and k == 0 and u == 3:
                            router()
                        if is_first and k == 0 and u == 6:
                            router_end()
                        if u == 3 and not (is_first and k == 0):
                            combine(e - 1, 1 - k, is_first and k == 1)
                        if is_first and k == 1 and u == 6:
                            dve.wait_ge(bias_done, 1)
                            dve.wait_ge(combined, 1)
                            order.step(nc.vector.tensor_tensor(
                                X[:], X[:], banks[:, 2:4, :].rearrange("p a (t n) -> p (a t) n", n=D), ALU.add))

            dve.wait_ge(x_updated, 2)
            layer_norm(3)
            transposed(3)
            dve.wait_ge(xt1_ready, 3)
            dve.wait_ge(xs_ready, 1)
            nc.vector.tensor_tensor(x_lo[:], xnT[:], x_hi[:].bitcast(F32), ALU.subtract).then_inc(xs_ready, 1)
            pair_of_experts(0, True)
            with dve.Fori(1, E0 // 2) as n:
                pair_of_experts(n, False)
            combine(E0 - 1, 1, False)
            dve.wait_ge(combined, E0)
            dve.sem_inc(x_updated, 1)

            dve.wait_ge(x_updated, 3)
            layer_norm(4)
            transposed(4)

            def greatest(p):
                k = p % 2
                dve.wait_ge(scores2_done, p + 1)
                dve.wait_ge(maskneg_ready, p + 1)
                if p >= 2:
                    dve.wait_ge(turned2, 2 * (p - 1))
                order.step(nc.vector.tensor_tensor(probs2[k][:], two(k), mask[p][:].bitcast(F32), ALU.add))
                order.step(nc.vector.tensor_reduce(stat2[:, p, 0:1], probs2[k][:], AX.X, ALU.max))
                nc.vector.tensor_scalar(stat2[:, p, 0:1], stat2[:, p, 0:1], -1.0 / 16, None, ALU.mult).then_inc(max2_ready, 1)

            def left_half(p):
                dve.wait_ge(turned2, 2 * p + 1)
                if p:
                    dve.wait_ge(mixed_done, p)
                nc.vector.tensor_copy(probsT2[:, 0:KC // 2, :], pb(4).rearrange("p (k n) -> p k n", n=P)).then_inc(left2_ready, 1)

            def normalise(p):
                mixed = xn[:, p, :]
                dve.wait_ge(exp2_done, p + 1)
                order.step(nc.vector.reciprocal(stat2[:, p, 1:2], stat2[:, p, 1:2]))
                dve.wait_ge(mixed_done, p + 1)
                nc.vector.tensor_scalar(mixed, pb(6)[:, 0:D], stat2[:, p, 1:2], None, ALU.mult).then_inc(mixed_taken, 1)
                dve.wait_ge(mixed_taken, p + 1)
                order.step(nc.vector.bn_stats(stats[:, p, :], mixed))
                order.step(nc.vector.bn_aggr(moments[:, p, :], stats[:, p, :]))
                nc.vector.tensor_scalar_add(stat2[:, p, 2:3], moments[:, p, 1:2], EPS).then_inc(var_ready, 1)
                dve.wait_ge(rstd_ready, 4 + p + 1)
                order.step(nc.vector.tensor_scalar(mixed, mixed, moments[:, p, 0:1], stat2[:, p, 3:4],
                                                   ALU.subtract, ALU.mult))
                order.step(nc.vector.tensor_tensor(mixed, mixed, part(rows, ROWS, "gamma"), ALU.mult))
                order.step(nc.vector.tensor_tensor(mixed, mixed, part(rows, ROWS, "beta"), ALU.add))
                order.mark(nc.vector.tensor_tensor(X[:, p, :], X[:, p, :], mixed, ALU.add))

            greatest(0)
            greatest(1)
            for p in range(TC):
                left_half(p)
                if p >= 1:
                    normalise(p - 1)
                if p + 2 < TC:
                    greatest(p + 2)
            normalise(TC - 1)
            order.settle()
            dve.sem_inc(x_updated, 1)

            dve.wait_ge(x_updated, 4)
            layer_norm(5 + TC)
            transposed(5)
            conv_w = part(later, LATER, "conv_w").rearrange("p (c k) -> p c k", c=CC)
            for m in range(CC):
                dve.wait_ge(first_tap, m + 1)
                dve.wait_ge(a_ready, m + 1)
                y = hidden[m // 2][:, m % 2, :].rearrange("p (b s) -> p b s", b=B)
                for k in range(KER - 1):
                    ins = nc.vector.scalar_tensor_tensor(y, a_pad[:, m, :, k:k + S], conv_w[:, m, k:k + 1], y, ALU.mult, ALU.add)
                    if k < KER - 2:
                        order.step(ins)
                    else:
                        ins.then_inc(conv1_ready, 1)
            d_param = part(later, LATER, "d_param")
            dve.wait_ge(bc_hi_ready, 1)
            nc.vector.tensor_tensor(bc_lo[0:2 * NSTATE, :], pb(6)[0:2 * NSTATE, :], bc_hi[0:2 * NSTATE, :].bitcast(F32),
                                    ALU.subtract).then_inc(bc_ready, 1)

            def step_parts(m):
                dve.wait_ge(step_done, m + 1)
                bias = d_param[:, m:m + 1]
                nc.vector.tensor_scalar(delta[:, m, :], pb(2 + m), bias, 0.0, ALU.add, ALU.max).then_inc(relu_ready, 1)

            def step_end(m):
                dve.wait_ge(soft_ready, m + 1)
                dve.wait_ge(relu_ready, m + 1)
                nc.vector.tensor_tensor(delta[:, m, :], delta[:, m, :], drive[:, m, :], ALU.add).then_inc(soft_taken, 1)
                dve.wait_ge(soft_taken, m + 1)
                dve.wait_ge(a_silu, m + 1)
                nc.vector.tensor_tensor(drive[:, m, :], delta[:, m, :], aT[:, m, :], ALU.mult).then_inc(drive_ready, 1)

            for m in range(CC):
                step_parts(m)
            for m in range(CC):
                step_end(m)

            def chunk(tile, m):
                return tile[:, m, :] if isinstance(m, int) else tile[:, bass.ds(m, 1), :].rearrange("p c n -> p (c n)")

            def gated(m, last=False):
                dve.wait_ge(y_ready, m + 1)
                if not isinstance(m, int) or m:
                    dve.wait_ge(gated_ready, 2 * m)
                nc.vector.scalar_tensor_tensor(acc[:], chunk(aT, m), d_param[:, bass.ds(m, 1)], pb(m + 2),
                                               ALU.mult, ALU.add).then_inc(gated_ready, 1)
                dve.wait_ge(gated_ready, 2 * m + 1)
                if last:
                    dve.wait_ge(projected, CC)
                nc.vector.tensor_tensor(gated_sum[:], acc[:], chunk(gT, m), ALU.mult).then_inc(gated_ready, 1)

            def states(m, first_chunk):
                for g in range(GROUPS):
                    if first_chunk:
                        for s in range(GS):
                            dve.wait_ge(Cbc_done, GS * g + s + 1)
                            nc.vector.tensor_copy(Cbc[:, GS * g + s, :], pb(6 + s)).then_inc(Cbc_ready, 1)
                    dve.wait_ge(decay_ready, GROUPS * m + (g + 1))
                    dve.wait_ge(inject_ready, GROUPS * m + (g + 1))
                    if g >= 2 or not first_chunk:
                        dve.wait_ge(shown_ready, GROUPS * m + (g - 1))
                    nc.vector.tensor_tensor_scan(hidden[g % 2][:].rearrange("p g n -> p (g n)"),
                                                 decay[g % 2][:].rearrange("p g n -> p (g n)"),
                                                 inject[g % 2][:].rearrange("p g n -> p (g n)"),
                                                 0.0, ALU.mult, ALU.add).then_inc(scanned, 1)
                    dve.wait_ge(scanned, GROUPS * m + (g + 1))
                    if first_chunk:
                        dve.wait_ge(Cbc_ready, GS * (g + 1))
                    if g >= 2 or not first_chunk:
                        dve.wait_ge(shown_used, GROUPS * m + (g - 1))
                    nc.vector.tensor_tensor(shown[g % 2][:], hidden[g % 2][:], Cbc[:, GS * g:GS * (g + 1), :], ALU.mult)\
                        .then_inc(shown_ready, 1)
                    if g == 2 and not first_chunk:
                        dve.wait_ge(projected, m)
                        gated(m - 1)

            dve.wait_ge(g_ready, CC)
            states(0, True)
            with dve.Fori(1, CC) as m:
                states(m, False)
            gated(CC - 1, True)
            for h in range(2):
                dve.wait_ge(out1_done, h + 1)
                last = nc.vector.tensor_copy(X[:, 2 * h:2 * h + 2, :], pb(6 + h).rearrange("p (t n) -> p t n", t=2))
            last.then_inc(x_updated, 1)

            dve.wait_ge(x_updated, 5)
            layer_norm(6 + TC)
            transposed(6)
            dve.wait_ge(logits1_done, 1)
            raw_logits = pb(6)[:, 0:TC * ROUTED1].rearrange("p (t e) -> p t e", t=TC)
            order.step(nc.vector.tensor_reduce(best1[:], raw_logits, AX.X, ALU.max))
            nc.vector.tensor_tensor(logits1[:], raw_logits, over(best1[:], ROUTED1, 2), ALU.subtract).then_inc(centred1, 1)
            nc.vector.memset(gate1[:], 1.0).then_inc(gate1_ready, 1)

            def route():
                dve.wait_ge(gate1_exp, 1)
                order.step(nc.vector.tensor_reduce(best1[:], logits1[:], AX.X, ALU.add))
                order.step(nc.vector.reciprocal(best1[:], best1[:]))
                order.step(nc.vector.tensor_tensor(logits1[:], logits1[:], over(best1[:], ROUTED1, 2), ALU.mult))
                top(logits1[:], ROUTED1, "before1", TOP1, above1[:], tied1[:], rank1[:])
                dve.wait_ge(gate1_ready, 1)
                nc.vector.tensor_tensor(gate1[:, :, 0:ROUTED1], logits1[:], rank1[:], ALU.mult).then_inc(gate1_ready, 1)
                dve.wait_ge(gate1_ready, 2)

            def hidden1(n, k):
                dve.wait_ge(silu1_ready, FB * n + (k + 1))
                if not isinstance(n, int):
                    dve.wait_ge(down1_done, FB * n + (k - 2))
                nc.vector.tensor_tensor(hid_f[k][:], act_f[k][:], pb(2 * k + 1), ALU.mult).then_inc(hid_ready, 1)

            def combine1(n, k):
                dve.wait_ge(down1_done, FB * n + (k + 1))
                if not (isinstance(n, int) and k == 0):
                    dve.wait_ge(combined1, FB * n + k)
                for t in range(TC):
                    y = pb(6 + t // 2)[:, (t % 2) * D:(t % 2 + 1) * D]
                    last = nc.vector.scalar_tensor_tensor(X[:, t, :], y, gate1[:, t, bass.ds(FB * n + k, 1)], X[:, t, :],
                                                          ALU.mult, ALU.add)
                last.then_inc(combined1, 1)

            def three_experts(n):
                hidden1(n, 0)
                hidden1(n, 1)
                if isinstance(n, int):
                    route()
                combine1(n, 0)
                hidden1(n, 2)
                combine1(n, 1)
                combine1(n, 2)

            three_experts(0)
            with dve.Fori(1, E1 // FB) as n:
                three_experts(n)
            dve.wait_ge(combined1, E1)
            dve.sem_inc(x_updated, 1)

        @block.tensor
        def _(pe):
            def mm(o, lhsT, rhs, start, stop):
                return nc.tensor.matmul(o, lhsT, rhs, start=start, stop=stop)

            def weights(tile, layout, name, parts):
                return part(tile, layout, name).rearrange("p (c n) -> p c n", c=parts)

            def transpose_tokens(k):
                pe.wait_ge(xn_ready, k)
                for c in range(DC):
                    for t in range(TC):
                        last = nc.tensor.transpose(pb(c)[:, t * P:(t + 1) * P], xn[:, t, c * P:(c + 1) * P], ident)
                    last.then_inc(xt_done, 1)

            pe.wait_ge(loaded["table"], 16)
            transpose_tokens(1)
            pe.wait_ge(loaded["first"], 16)
            wq = weights(first, FIRST, "wq", DC)
            pe.wait_ge(xt0_ready, 1)
            pe.wait_ge(xt1_ready, 1)
            for g in range(STACKS):
                for i in range(DC):
                    last = mm(pb(Q_BANKS[g]), wq[:, i, g * P:(g + 1) * P], xnT[:, i, :], i == 0, i == DC - 1)
                last.then_inc(q_done, 1)

            def three(o, a, b):
                passes = [(a[x][i], b[y][i]) for i in range(DC) for x, y in ((0, 0), (0, 1), (1, 0))]
                for n, (x, y) in enumerate(passes):
                    last = mm(o, x, y, n == 0, n == len(passes) - 1)
                return last

            def project_keys(piece, b, par, c, half):
                pe.wait_ge(ctx_lo_ready, DC * b + DC)
                if not (isinstance(piece, int) and piece == 1):
                    pe.wait_ge(piece_taken, piece - 1)
                w = [[w_kv[0][x][:, i, c * P:(c + 1) * P] for i in range(DC)] for x in range(2)]
                ctx = [[of[par][:, i, half * 512:(half + 1) * 512] for i in range(DC)] for of in (ctx_hi, ctx_lo)]
                three(pb(4), w, ctx).then_inc(proj_done, 1)

            def project_values(piece, b, par, v):
                pe.wait_ge(piece_taken, piece - 1)
                w = [[w_kv[1][x][:, i, :] for i in range(DC)] for x in range(2)]
                for kc in (2 * v, 2 * v + 1):
                    ctx = [[of[par][:, i, kc * P:(kc + 1) * P] for i in range(DC)] for of in (ctx_hi, ctx_lo)]
                    last = three(pb(4)[:, (kc % 2) * D:(kc % 2 + 1) * D], ctx, w)
                last.then_inc(proj_done, 1)

            def turn(b, i):
                pe.wait_ge(exp_done, 8 * b + (i + 1))
                for half in range(2):
                    if not (isinstance(b, int) and b == 0 and i == 0):
                        pe.wait_ge(pt1_ready if half else pt0_ready, 8 * b + i)
                    for k in range(KC // 2):
                        kc = half * (KC // 2) + k
                        last = nc.tensor.transpose(pb(5 + half)[:, k * P:(k + 1) * P],
                                                   probs[i % 2][:, kc * P:(kc + 1) * P], ident)
                    last.then_inc(t_done, 1)

            def weigh(b, c, q):
                pe.wait_ge(piece_taken, piece_at(b, VALUES_AT[q], isinstance(b, int) and b == B - 1))
                if q == 0:
                    pe.wait_ge(pt0_ready, 8 * b + PAIRS * (c + 1))
                    pe.wait_ge(pt1_ready, 8 * b + PAIRS * (c + 1))
                    pe.wait_ge(diag_ready, DC * b + (c + 1))
                    if not (isinstance(b, int) and b == 0 and c == 0):
                        pe.wait_ge(masked_ready, DC * b + c)
                    pick = weights(table, TABLE, "pick", 2)
                    for j in range(PAIRS):
                        g, of = divmod(j, 2)
                        mm(pb(7)[64 * g:64 * g + 64, 256 + of * P:256 + (of + 1) * P], pick[:, of, :], inv_diag[:, j, :], True, True)
                for kc in (2 * q, 2 * q + 1):
                    for g in range(2):
                        last = mm(pb(7)[64 * g:64 * g + 64, 0:256], V[:, kc, c * P + 64 * g:c * P + 64 * g + 64],
                                  probsT[c][:, kc, 2 * g:2 * g + 2, :], kc == 0, kc == KC - 1)
                last.then_inc(quarter_done, 1)

            def project_out(n):
                pe.wait_ge(attn_ready, 4 * n + 4)
                wo = weights(later, LATER, "wo", DC)
                for c in range(DC):
                    last = mm(pb(7)[:, 256:512], attn[:, c, :], wo[:, c, :], c == 0, c == DC - 1)
                last.then_inc(out_done, 1)

            def batch(b, par, last, tile=None):
                later_one = not (isinstance(b, int) and b == 0)
                for i in range(8):
                    g = i // 2
                    piece = piece_at(b, i, last)
                    if i in KEYS_AT:
                        project_keys(piece, b, par, 1, KEYS_AT.index(i))
                    elif i in VALUES_AT:
                        project_values(piece, b, par, VALUES_AT.index(i))
                    elif not last:
                        project_keys(piece, b + 1, 1 - par, 0, NEXT_KEYS_AT.index(i))
                    pe.wait_ge(heads_ready, STACKS * b + (g + 1))
                    pe.wait_ge(piece_taken, 8 * b + 2 if g < 2 else piece_at(b, KEYS_AT[1]))
                    if later_one or i >= 2:
                        pe.wait_ge(exp_done, 8 * b + (i - 1))
                    for half in range(2):
                        for n, q in enumerate(q_stack):
                            done = mm(pb(2 * (i % 2) + half), q[:, g, 2 * (i % 2):2 * (i % 2) + 2, :],
                                      k_stack[:, g, half * 512:(half + 1) * 512], n == 0, n == 1)
                    done.then_inc(scores_done, 1)
                    if i == 5 and tile is not None:
                        project_out(tile)
                    elif i == 0 and later_one:
                        weigh(b - 1, 0, 3)
                    elif 1 <= i < 5 and later_one:
                        weigh(b - 1, 1, i - 1)
                    elif i >= 5:
                        weigh(b, 0, i - 5)
                    if i >= 1:
                        turn(b, i - 1)
                    elif later_one:
                        turn(b - 1, 7)
                    if i == 5 and tile is not None:
                        pe.wait_ge(tile_added, tile + 2)
                        weigh(b, 0, 0)

            pe.wait_ge(w_lo_ready, 2)
            pe.wait_ge(loaded["later"], 16)
            for half in range(2):
                project_keys(half + 1, 0, 0, 0, half)
            batch(0, 0, False)
            with pe.Fori(0, B // 2 - 1) as n:
                batch(2 * n + 1, 1, False)
                batch(2 * n + 2, 0, False, n)
            batch(B - 1, 1, True)
            weigh(B - 1, 0, 3)
            turn(B - 1, 7)
            for q in range(4):
                weigh(B - 1, 1, q)
            project_out(TC - 1)
            transpose_tokens(2)
            for h in range(2):
                for t in (2 * h, 2 * h + 1):
                    for c in range(DC):
                        pe.wait_ge(silu_ready, c + 1)
                        last = nc.tensor.transpose(pb(2 + h)[:, (t % 2) * D + c * P:(t % 2) * D + (c + 1) * P],
                                                   conv[1][:, c, t * P:(t + 1) * P], ident)
                last.then_inc(back_done, 1)

            transpose_tokens(3)
            pe.wait_ge(xt0_ready, 3)
            pe.wait_ge(xt1_ready, 3)
            pe.wait_ge(xs_ready, 2)

            def up(e, k, u):
                if u == 0:
                    pe.wait_ge(lo_done, 4 * e + 2)
                if not (isinstance(e, int) and e == 0 and u < 2):
                    pe.wait_ge(gelu_done, UNITS * e + (u - 1))
                passes = []
                for c in range(DC):
                    cols = slice(c * F0 + u * P, c * F0 + (u + 1) * P)
                    passes += [(w_hi[k][:, cols], x_hi[:, c, :]), (w_hi[k][:, cols], x_lo[:, c, :]),
                               (w_lo[k][:, cols], x_hi[:, c, :])]
                for i, (w, x) in enumerate(passes):
                    last = mm(pb(u % 2), w, x, i == 0, i == len(passes) - 1)
                last.then_inc(up_done, 1)

            def down(e, k, u):
                pe.wait_ge(h_ready, UNITS * e + (u + 1))
                if u == 0:
                    pe.wait_ge(lo_done, 4 * e + 4)
                    if not (isinstance(e, int) and e < 2):
                        pe.wait_ge(combined, e - 1)
                cols = slice(EW // 2 + u * D, EW // 2 + (u + 1) * D)
                for t in range(TC):
                    tok = slice(t * P, (t + 1) * P)
                    o = pb(4 + 2 * k + t // 2)[:, (t % 2) * D:(t % 2 + 1) * D]
                    passes = [(h_hi[u % 4][:, tok], w_hi[k][:, cols]), (h_hi[u % 4][:, tok], w_lo[k][:, cols]),
                              (h_lo[u % 4][:, tok], w_hi[k][:, cols])]
                    for i, (h, w) in enumerate(passes):
                        last = mm(o, h, w, u == 0 and i == 0 and t % 2 == 0, u == UNITS - 1 and i == 2 and t % 2 == 1)
                last.then_inc(down_done, 1)

            def route():
                pe.wait_ge(keys_ready, 2)
                for t in range(TC):
                    for c in range(DC):
                        mm(pb(2)[:, t * E0:(t + 1) * E0], xnT[:, c, t * P:(t + 1) * P], key_sum[:, c, :], c == 0, c == DC - 1)
                for c in range(DC):
                    last = mm(pb(2)[:, TC * E0:(TC + 1) * E0], ones, key_sq[:, c, :], c == 0, c == DC - 1)
                last.then_inc(logits_done, 1)

            def pair_of_experts(n, is_first, is_last):
                for k in range(2):
                    e = 2 * n + k
                    for u in range(UNITS):
                        if u + 2 < UNITS:
                            up(e, k, u + 2)
                        elif not (is_last and k):
                            up(e + 1, 1 - k, u + 2 - UNITS)
                        down(e, k, u)
                        if is_first and k == 0 and u == 0:
                            route()
                        if is_first and k == 1 and u == 2:
                            pe.wait_ge(gate_ready, 1)
                            for t in range(TC):
                                last = nc.tensor.transpose(pb(3)[0:E0, t * P:(t + 1) * P], gate[:, t, :], ident)
                            last.then_inc(gate_turned, 1)
                        if is_first and k == 1 and u == 4:
                            pe.wait_ge(gateT_ready, 1)
                            pe.wait_ge(loaded["b2"], 16)
                            for t in range(TC):
                                last = mm(pb(2 + t // 2)[:, (t % 2) * D:(t % 2 + 1) * D], gateT[:, t, :], b2[:], True, True)
                            last.then_inc(bias_done, 1)

            up(0, 0, 0)
            up(0, 0, 1)
            pair_of_experts(0, True, False)
            with pe.Fori(1, E0 // 2 - 1) as n:
                pair_of_experts(n, False, False)
            pair_of_experts(E0 // 2 - 1, False, True)

            transpose_tokens(4)
            pe.wait_ge(xt0_ready, 4)
            pe.wait_ge(xt1_ready, 4)

            def score2(p):
                k = p % 2
                pe.wait_ge(ctxT2_loaded[p], 16)
                if p >= 2:
                    pe.wait_ge(max2_ready, p - 1)
                for half in range(2):
                    for c in range(DC):
                        for b in range(2):
                            last = mm(pb(2 * k + half)[64 * b:64 * b + 64, :], xnT[:, c, p * P + S * b:p * P + S * (b + 1)],
                                      ctxT2[p][:, b, c, half * 512:(half + 1) * 512], c == 0, c == DC - 1)
                last.then_inc(scores2_done, 1)

            def turn2(p):
                pe.wait_ge(exp2_done, p + 1)
                for half in range(2):
                    if p:
                        pe.wait_ge(right2_ready if half else left2_ready, p)
                    for j in range(KC // 2):
                        kc = half * (KC // 2) + j
                        last = nc.tensor.transpose(pb(4 + half)[:, j * P:(j + 1) * P], probs2[p % 2][:, kc * P:(kc + 1) * P], ident)
                    last.then_inc(turned2, 1)

            def mix2(p):
                pe.wait_ge(ctxN2_loaded[p], 16)
                pe.wait_ge(left2_ready, p + 1)
                pe.wait_ge(right2_ready, p + 1)
                if p:
                    pe.wait_ge(mixed_taken, p)
                for kc in range(KC):
                    for b in range(2):
                        last = mm(pb(6)[64 * b:64 * b + 64, 0:D], probsT2[:, kc, S * b:S * (b + 1)], ctxN2[p][:, b, kc, :],
                                  kc == 0, kc == KC - 1)
                last.then_inc(mixed_done, 1)

            score2(0)
            score2(1)
            turn2(0)
            for p in range(TC):
                if p + 2 < TC:
                    score2(p + 2)
                mix2(p)
                if p + 1 < TC:
                    turn2(p + 1)

            transpose_tokens(5)
            pe.wait_ge(xt0_ready, 5)
            pe.wait_ge(xt1_ready, 5)
            w_in = weights(later, LATER, "w_in", DC)
            for g in range(2):
                for m in range(CC):
                    if g:
                        pe.wait_ge(a_ready, m + 1)
                    for c in range(DC):
                        last = mm(pb(2 + m), w_in[:, c, g * DI + m * P:g * DI + (m + 1) * P], xnT[:, c, :], c == 0, c == DC - 1)
                    last.then_inc(ag_done, 1)
            w_sd1, w_sbc = weights(later, LATER, "w_sd1", CC), weights(later, LATER, "w_sbc", CC)
            for m in range(CC):
                pe.wait_ge(a_silu, m + 1)
                low_last = mm(pb(7), w_sd1[:, m, :], aT[:, m, :], m == 0, m == CC - 1)
                bc_last = mm(pb(6)[0:2 * NSTATE, :], w_sbc[:, m, :], aT[:, m, :], m == 0, m == CC - 1)
            low_last.then_inc(low_done, 1)
            bc_last.then_inc(bc_done, 1)
            pe.wait_ge(low_ready, 1)
            w_sd2 = part(later, LATER, "w_sd2")
            for m in range(CC):
                pe.wait_ge(g_ready, m + 1)
                mm(pb(2 + m), w_sd2[:, m * P:(m + 1) * P], lowT[:], True, True).then_inc(step_done, 1)
            pe.wait_ge(bc_ready, 1)
            pe.wait_ge(one_hot_ready, 1)

            def broadcast(g):
                for row, at, done, ready in ((0, 0, Bbc_done, Bbc_ready), (NSTATE, 6, Cbc_done, Cbc_ready)):
                    for s in range(GS):
                        if g:
                            pe.wait_ge(ready, GS * (g - 1) + s + 1)
                        r = row + GS * g + s
                        pick = one_hot[:, r:r + 1].broadcast_to([P, P])
                        mm(pb(at + s), pick, bc_hi[:], True, False)
                        mm(pb(at + s), pick, bc_lo[:], False, True).then_inc(done, 1)

            def sum_states(m, g):
                pe.wait_ge(shown_ready, GROUPS * m + (g + 1))
                for s in range(GS):
                    last = mm(pb(m + 2), ident, shown[g % 2][:, s, :], g == 0 and s == 0, g == GROUPS - 1 and s == GS - 1)
                last.then_inc(shown_used, 1)
                if g == GROUPS - 1:
                    pe.wait_ge(shown_used, GROUPS * (m + 1))
                    pe.sem_inc(y_ready, 1)

            w_out = weights(later, LATER, "w_out", CC).rearrange("p c n -> p (c n)")

            def project_out1(m, last):
                pe.wait_ge(gated_ready, 2 * m + 2)
                for t in range(TC):
                    done = mm(pb(6 + t // 2)[:, (t % 2) * D:(t % 2 + 1) * D], gated_sum[:, t * P:(t + 1) * P],
                              w_out[:, bass.ds(m * D, D)], False, last and t % 2 == 1)
                    if last and t % 2:
                        done.then_inc(out1_done, 1)
                if not last:
                    done.then_inc(projected, 1)

            broadcast(0)
            broadcast(1)
            for g in range(GROUPS):
                if g + 2 < GROUPS:
                    broadcast(g + 2)
                sum_states(0, g)
            pe.wait_ge(Cbc_ready, NSTATE)
            for t in range(TC):
                last = mm(pb(6 + t // 2)[:, (t % 2) * D:(t % 2 + 1) * D], ident, X[:, t, :], t % 2 == 0, False)
            last.then_inc(projected, 1)
            with pe.Fori(1, CC) as m:
                for g in range(GROUPS):
                    sum_states(m, g)
                    if g == 3:
                        project_out1(m - 1, False)
            project_out1(CC - 1, True)

            transpose_tokens(6)
            pe.wait_ge(xt0_ready, 6)
            pe.wait_ge(xt1_ready, 6)
            gate_w = weights(later, LATER, "gate_w", DC)
            for t in range(TC):
                for c in range(DC):
                    last = mm(pb(6)[:, t * ROUTED1:(t + 1) * ROUTED1], xnT[:, c, t * P:(t + 1) * P], gate_w[:, c, :],
                              c == 0, c == DC - 1)
            last.then_inc(logits1_done, 1)

            def gate_up(n, k):
                pe.wait_ge(wf_loaded[k], 16 * n + 16)
                if not isinstance(n, int):
                    pe.wait_ge(hid_ready, FB * n + (k - 2))
                for g in range(2):
                    for c in range(DC):
                        last = mm(pb(2 * k + g), wf[k][:, (g * DC + c) * P:(g * DC + c + 1) * P], xnT[:, c, :], c == 0, c == DC - 1)
                last.then_inc(gu_done, 1)

            def down1(n, k):
                pe.wait_ge(hid_ready, FB * n + (k + 1))
                if isinstance(n, int) and k == 0:
                    pe.wait_ge(centred1, 1)
                else:
                    pe.wait_ge(combined1, FB * n + k)
                for t in range(TC):
                    last = mm(pb(6 + t // 2)[:, (t % 2) * D:(t % 2 + 1) * D], hid_f[k][:, t * P:(t + 1) * P],
                              wf[k][:, 2 * D:3 * D], True, True)
                last.then_inc(down1_done, 1)

            def three_experts(n):
                gate_up(n, 0)
                gate_up(n, 1)
                down1(n, 0)
                gate_up(n, 2)
                down1(n, 1)
                down1(n, 2)

            three_experts(0)
            with pe.Fori(1, E1 // FB) as n:
                three_experts(n)


def _tables():
    t = np.zeros((P, TABLE_W), np.float32)

    def put(name, value):
        a, b = TABLE[name]
        t[:, a:b] = np.asarray(value, np.float64).reshape(P, b - a) if np.ndim(value) > 1 else value

    p = np.arange(P)
    put("ident", np.eye(P))
    pick = p[None, None, :64] // DH == 2 * np.arange(2)[None, :, None] + p[:, None, None] // S
    put("pick", pick)
    put("quad", p[:, None] % 64 // DH == np.arange(4))
    for name, n in (("before0", E0), ("before1", ROUTED1)):
        put(name, (np.arange(n)[None, :] < np.arange(n)[:, None]).ravel())
    omega = np.exp(-2j * np.pi * np.arange(MODES) / B)
    omega[MODES - 1] = -1.0
    put("ar", (2 * (1 - omega)).real)
    put("ai", (2 * (1 - omega)).imag)
    put("cr", (1 + omega).real)
    put("ci", (1 + omega).imag)
    often = np.array([1, 2, 2, 2, 1]) * 2 / B
    turn = 2 * np.pi * np.outer(np.arange(B), np.arange(MODES)) / B
    put("alpha", (often * np.cos(turn)).ravel())
    beta = -often * np.sin(turn)
    beta[:, [0, MODES - 1]] = 0
    put("beta", beta.ravel())
    put("ones", np.ones(P))
    put("minus_half", np.full(TC, -0.5))
    put("minus_one", np.full(DC * MODES, -1.0))
    return t


def _layouts(x, ctx_1024, mask_BxSxS2_ik1, **w):
    g = {k: np.asarray(v) for k, v in w.items()}

    def rows_in(m):
        m = m.reshape(m.shape[0] // P, P, -1)
        return np.ascontiguousarray(m.transpose(1, 0, 2)).reshape(P, -1)

    def weight(name):
        return rows_in(g[name].T)

    def side(layout, values):
        return np.ascontiguousarray(np.concatenate([values[n].reshape(P, -1) for n in layout], axis=1))

    out = {"x": np.asarray(x).reshape(TOK, D)}
    ctx = np.asarray(ctx_1024)
    out["ctxT"] = np.ascontiguousarray(ctx.transpose(0, 2, 1).reshape(B, DC, P, KEYS).transpose(0, 2, 1, 3))
    out["ctxN"] = np.ascontiguousarray(ctx.reshape(B, KC, P, D).transpose(0, 2, 1, 3))
    out["mask"] = np.asarray(mask_BxSxS2_ik1).reshape(TOK, KEYS)
    out["first"] = side(FIRST, {
        "wq": weight("L0_xattn_w_q").reshape(P, DC, STACKS, 1, 64).repeat(2, axis=3), "wk": weight("L0_xattn_w_k"), "wv": weight("L0_xattn_w_v"),
        "bq": g["L0_xattn_b_q"].reshape(STACKS, 1, 64).repeat(2, axis=1).reshape(STACKS, P).T, "bk": rows_in(g["L0_xattn_b_k"])})
    out["table"] = _tables()
    b1 = g["L0_ffn_b1"].reshape(E0, FC, P).transpose(2, 0, 1)
    sbc = np.concatenate([g["L1_attn_W_sB"], g["L1_attn_W_sC"]], axis=0)
    out["later"] = side(LATER, {
        "wo": weight("L0_xattn_w_o"), "log_dt": rows_in(g["L0_attn_log_dt"]), "inv_w": rows_in(g["L0_attn_inv_w_real"]),
        "w_im": rows_in(g["L0_attn_w_imaginary"]), "B": rows_in(g["L0_attn_B"]), "P": rows_in(g["L0_attn_P"][0]),
        "C": rows_in(g["L0_attn_C"]), "D": rows_in(g["L0_attn_D"]), "keys": weight("L0_ffn_keys"),
        "rw": weight("L0_ffn_rw"), "b1": np.ascontiguousarray(b1), "w_in": weight("L1_attn_W_in"),
        "w_sbc": rows_in(sbc.T), "w_sd1": weight("L1_attn_W_sD1"), "w_sd2": weight("L1_attn_W_sD2"),
        "conv_w": rows_in(g["L1_attn_conv_w"]), "conv_b": rows_in(g["L1_attn_conv_b"]),
        "a_param": rows_in(g["L1_attn_A_param"]), "d_param": rows_in(g["L1_attn_D_param"]),
        "w_out": weight("L1_attn_W_out"), "gate_w": weight("L1_ffn_gate_w")})
    row = np.concatenate([g["L0_xattn_b_v"], g["L0_xattn_b_o"], g["L1_xattn_gamma"], g["L1_xattn_beta"], g["L0_ffn_rb"]])
    out["rows"] = np.ascontiguousarray(np.broadcast_to(row, (P, ROWS_W)))
    out["b2"] = g["L0_ffn_b2"]
    w1 = g["L0_ffn_w1"].transpose(0, 2, 1).reshape(E0, DC, P, F0).transpose(0, 2, 1, 3).reshape(E0, P, -1)
    w2 = g["L0_ffn_w2"].transpose(0, 2, 1).reshape(E0, FC, P, D).transpose(0, 2, 1, 3).reshape(E0, P, -1)
    out["w0"] = np.ascontiguousarray(np.concatenate([w1, w2], axis=2))
    up = np.stack([np.concatenate([g["L1_ffn_wg"], g["L1_ffn_sg"][None]]),
                   np.concatenate([g["L1_ffn_wu"], g["L1_ffn_su"][None]])], axis=1)
    up = up.transpose(0, 3, 1, 2).reshape(E1, DC, P, 2, P).transpose(0, 2, 3, 1, 4).reshape(E1, P, -1)
    down = np.concatenate([g["L1_ffn_wd"], g["L1_ffn_sd"][None]]).transpose(0, 2, 1)
    out["w1"] = np.ascontiguousarray(np.concatenate([up, down], axis=2))
    return out


def kernel(**inputs):
    import concourse.bacc as bacc
    from concourse.bass_utils import run_bass_kernel_spmd

    arrays = _layouts(**inputs)
    nc = bacc.Bacc("TRN2", target_bir_lowering=False, num_devices=1)
    drams = {n: nc.dram_tensor(f"in_{n}", a.shape, mybir.dt.from_np(a.dtype), kind="ExternalInput").ap()
             for n, a in arrays.items()}
    out = nc.dram_tensor("out", (TOK, D), F32, kind="ExternalOutput").ap()
    build(nc, drams, out)
    r = run_bass_kernel_spmd(nc, [{f"in_{n}": a for n, a in arrays.items()}], core_ids=[0])
    return r.results[0]["out"].reshape(B, S, D)
```

```python
from contextlib import ExitStack

import concourse.bass as bass
import numpy as np
from concourse import mybir

F32 = mybir.dt.float32
F32R = mybir.dt.float32r
I32 = mybir.dt.int32
ACT = mybir.ActivationFunctionType
ALU = mybir.AluOpType
AX = mybir.AxisListType

P = 128
B, S, D = 8, 64, 256
KEYS = 1024
TOK = B * S
TC = TOK // P
DC = D // P
KC = KEYS // P
HEADS, DH = 16, 16
HPC = HEADS // DC
PAIRS, PAIR_W = HPC // 2, 2 * DH
EPS = 1e-5
NSTATE, MODES = 16, 5
E0, TOP0, F0 = 16, 4, 1024
FC = F0 // P
E1, TOP1 = 9, 2
ROUTED1 = E1 - 1
DI, DISCR, KER = 512, 128, 4
CC = DI // P
NEG = -9000000000000000.0
EW = 2 * DC * F0
QW = EW // 4
UNITS = FC
GS = 2
GROUPS = NSTATE // GS
FB = 3
LAYERS = 6
Q_BANKS, FIRST_BANKS = (2, 3, 5, 6), (4, 7)
KEYS_AT, VALUES_AT, NEXT_KEYS_AT = (0, 2), (1, 3, 5, 7), (4, 6)
G_BANKS, EARLY_B, EARLY_C = (3, 4, 5, 0), 4, 3
EARLY_IN = 1
X_BANKS, X1_BANKS = (6, 7), (4, 5)
STACKS = D // 64
STAGE_AT, PHASE_AT, PLAN_END = 51 * 1024, 83 * 1024, 207 * 1024


def columns(widths):
    at, out = 0, {}
    for name, width in widths:
        out[name] = (at, at + width)
        at += width
    return out, at


FIRST, FIRST_W = columns([("wq", DC * 2 * D), ("bq", STACKS), ("wk", DC * D), ("bk", DC), ("wv", DC * D)])
TABLE, TABLE_W = columns([
    ("ident", P), ("quad", 4), ("pick", PAIR_W), ("before0", E0 * E0),
    ("before1", ROUTED1 * ROUTED1), ("ar", MODES), ("ai", MODES), ("cr", MODES), ("ci", MODES),
    ("alpha", B * MODES), ("beta", B * MODES), ("ones", P), ("minus_half", TC), ("minus_one", DC * MODES)])
LATER, LATER_W = columns([
    ("wo", DC * D), ("log_dt", DC), ("inv_w", DC * NSTATE), ("w_im", DC * NSTATE), ("B", DC * NSTATE * 2),
    ("P", DC * NSTATE * 2), ("C", DC * NSTATE * 2), ("D", DC), ("keys", DC * E0), ("rw", DC * E0),
    ("b1", E0 * FC), ("w_in", DC * 2 * DI), ("w_sbc", CC * 2 * NSTATE), ("w_sd1", CC * DISCR), ("w_sd2", DI),
    ("conv_w", CC * KER), ("conv_b", CC), ("a_param", CC * NSTATE), ("d_param", CC), ("w_out", CC * D),
    ("gate_w", DC * ROUTED1)])
ROWS, ROWS_W = columns([("bv", D), ("bo", D), ("gamma", D), ("beta", D), ("rb", E0)])


def part(tile, layout, name):
    a, b = layout[name]
    return tile[:, a:b]


class Order:

    def __init__(self, eng, sem):
        self.eng, self.sem, self.count = eng, sem, 0

    def mark(self, ins):
        self.count += 1
        ins.then_inc(self.sem, 1)

    def settle(self):
        self.eng.wait_ge(self.sem, self.count)

    def step(self, ins):
        self.mark(ins)
        self.settle()


def over(ap, n, axis):
    ap = ap.unsqueeze(axis)
    shape = list(ap.shape)
    shape[axis] = n
    return ap.broadcast_to(shape)


def build(nc, d, out):
    ctx = ExitStack()
    with ctx:
        names = set()

        def sem(name):
            assert name not in names
            names.add(name)
            return ctx.enter_context(nc.semaphore(name))

        base = -(-nc.sbuf_base // 64) * 64
        place = {"common": base, "stage": base + STAGE_AT, "phase": base + PHASE_AT}
        ends = {"common": place["stage"], "stage": place["phase"], "phase": base + PLAN_END}

        def sb(region, name, shape, dt=F32):
            width = int(np.prod(shape[1:])) * 4
            at = place[region]
            place[region] = at + -(-width // 64) * 64
            assert place[region] <= ends[region], (name, region, place[region] - ends[region])
            return nc.alloc_sbuf_tensor_at(name, shape, dt, offset=at)

        first = sb("common", "first", [P, FIRST_W])
        table = sb("common", "table", [P, TABLE_W])
        later = sb("common", "later", [P, LATER_W])
        rows = sb("common", "rows", [P, ROWS_W])
        b2 = sb("common", "b2", [E0, D])
        X = sb("common", "X", [P, TC, D])
        xn = sb("common", "xn", [P, TC, D])
        xnT = sb("common", "xnT", [P, DC, TOK])
        stats = sb("common", "stats", [P, TC, 6])
        moments = sb("common", "moments", [P, TC, 2])
        vareps = sb("common", "vareps", [P, TC])
        rstd = sb("common", "rstd", [P, TC])
        taps = sb("common", "taps", [P, B, DC])
        key_sum = sb("common", "key_sum", [P, DC, E0])
        key_sq = sb("common", "key_sq", [P, DC, E0])
        stat2 = sb("common", "stat2", [P, TC, 4])
        exp_a = sb("common", "exp_a", [P, CC * NSTATE])

        ident = part(table, TABLE, "ident")
        ones = part(table, TABLE, "ones")

        raw = [sb("stage", f"raw{k}", [P, EW]) for k in range(2)]

        place["stage"] = base + STAGE_AT
        ctx_hi, ctx_lo = [], []
        for k in range(2):
            ctx_hi.append(sb("stage", f"ctx_hi{k}", [P, DC, KEYS], F32R))
            ctx_lo.append(sb("stage", f"ctx_lo{k}", [P, DC, KEYS], F32R))
        top = place["phase"]
        ctx_raw = sb("phase", "ctx_raw", [P, DC, KEYS])
        w_kv = [[sb("phase", f"w_{n}_{part_of}", [P, DC, D], F32R) for part_of in ("hi", "lo")] for n in "kv"]
        k_stack = sb("phase", "k_stack", [P, STACKS, KEYS], F32R)
        V = sb("phase", "V", [P, KC, D])
        probs = [sb("phase", f"probs{k}", [P, KEYS]) for k in range(2)]
        probsT = [sb("phase", f"probsT{k}", [P, KC, PAIRS, P]) for k in range(DC)]
        q_part = [sb("phase", f"q_{n}", [P, STACKS, TOK], F32R) for n in ("hi", "lo")]
        q_stack = [sb("phase", f"q_stack_{n}", [P, STACKS, 4, S], F32R) for n in ("hi", "lo")]
        negmax_raw = [sb("phase", f"negmax_raw{k}", [P, 1]) for k in range(2)]
        negmax = [sb("phase", f"negmax{k}", [P, 1]) for k in range(2)]
        sums = [sb("phase", f"sums{k}", [P, PAIRS]) for k in range(DC)]
        inv_sums = [sb("phase", f"inv_sums{k}", [P, PAIRS]) for k in range(DC)]
        inv_diag = sb("phase", "inv_diag", [P, PAIRS, P])
        own = sb("phase", "own", [P, 2, S])
        attn = sb("phase", "attn", [P, DC, P])
        s4 = {n: sb("phase", "s4_" + n, [P, DC * NSTATE]) for n in ("wr", "wi", "ew")}
        s4v = sb("phase", "s4_v", [P, 7, DC * NSTATE])
        s4t = sb("phase", "s4_t", [P, DC * NSTATE])
        s4g = [sb("phase", f"s4_g{k}", [P, MODES, DC * NSTATE]) for k in range(6)]
        s4p = sb("phase", "s4_p", [P, 8, MODES * DC, NSTATE])
        s4s = sb("phase", "s4_s", [P, 14, MODES, DC])
        s4dt = sb("phase", "s4_dt", [P, DC])
        s4l = [sb("phase", f"s4_l{k}", [P, B, DC, MODES]) for k in range(2)]

        place["phase"] = top
        conv = [sb("phase", f"conv{k}", [P, DC, TOK]) for k in range(2)]
        w_hi, w_lo = [], []
        for k in range(2):
            w_hi.append(sb("phase", f"w_hi{k}", [P, EW], F32R))
            w_lo.append(sb("phase", f"w_lo{k}", [P, EW], F32R))
        x_hi = sb("phase", "x_hi", [P, DC, TOK], F32R)
        x_lo = sb("phase", "x_lo", [P, DC, TOK], F32R)
        h_full = [sb("phase", f"h_full{k}", [P, TOK]) for k in range(2)]
        h_hi = [sb("phase", f"h_hi{k}", [P, TOK], F32R) for k in range(4)]
        h_lo = [sb("phase", f"h_lo{k}", [P, TOK], F32R) for k in range(4)]
        logits = sb("phase", "logits", [P, TC, E0])
        squares = sb("phase", "squares", [P, D])
        sumsq = sb("phase", "sumsq", [P, TC])
        above = sb("phase", "above", [P, TC, E0, E0])
        tied = sb("phase", "tied", [P, TC, E0, E0])
        rank = sb("phase", "rank", [P, TC, E0])
        best = sb("phase", "best", [P, TC])
        gate = sb("phase", "gate", [P, TC, E0])
        gateT = sb("phase", "gateT", [E0, TC, P])

        place["phase"] = top
        place["stage"] = base + STAGE_AT
        mask = [sb("phase", f"mask{k}", [P, KEYS], I32) for k in range(2)]
        ctxT2, ctxN2 = [], []
        for p in range(TC):
            ctxT2.append(sb("phase" if p else "stage", f"ctxT2{p}", [P, 2, DC, KEYS]))
            ctxN2.append(sb("phase" if p else "stage", f"ctxN2{p}", [P, 2, KC, D]))
        probs2 = [sb("phase", f"probs2{k}", [P, KEYS]) for k in range(2)]
        probsT2 = sb("phase", "probsT2", [P, KC, P])
        mask += [sb("phase", f"mask{p}", [P, KEYS], I32) for p in range(2, TC)]

        place["phase"] = top
        place["stage"] = base + STAGE_AT
        Bbc = sb("phase", "Bbc", [P, NSTATE, TOK])
        Cbc = sb("phase", "Cbc", [P, NSTATE, TOK])
        a_pad = sb("phase", "a_pad", [P, CC, B, S + KER - 1])
        aT = sb("phase", "aT", [P, CC, TOK])
        gT = sb("phase", "gT", [P, CC, TOK])
        delta = sb("phase", "delta", [P, CC, TOK])
        drive = sb("phase", "drive", [P, CC, TOK])
        hidden = [sb("phase", f"hidden{k}", [P, GS, TOK]) for k in range(2)]
        gated_sum = sb("phase", "gated_sum", [P, TOK])
        bc = sb("stage", "bc", [4 * NSTATE, TOK], F32R)
        two_hot = sb("stage", "two_hot", [4 * NSTATE, 2 * NSTATE], F32R)
        lowT = sb("stage", "lowT", [P, TOK])
        acc = lowT
        decay = [sb("stage", f"decay{k}", [P, GS, TOK]) for k in range(2)]
        inject = [sb("stage", f"inject{k}", [P, GS, TOK]) for k in range(2)]
        shown = [sb("stage", f"shown{k}", [P, GS, TOK]) for k in range(2)]

        wf = [sb("phase", f"wf{k}", [P, 3 * D]) for k in range(FB)]
        place["phase"] = top
        f_hi = [sb("phase", f"f_hi{k}", [P, 3 * D], F32R) for k in range(FB)]
        f_lo = [sb("phase", f"f_lo{k}", [P, 3 * D], F32R) for k in range(FB)]
        x1_hi = sb("phase", "x1_hi", [P, DC, TOK], F32R)
        x1_lo = sb("phase", "x1_lo", [P, DC, TOK], F32R)
        act_f = [sb("phase", f"act_f{k}", [P, TOK]) for k in range(FB)]
        hid_f = [sb("phase", f"hid_f{k}", [P, TOK]) for k in range(FB)]
        hid_hi = [sb("phase", f"hid_hi{k}", [P, TOK], F32R) for k in range(FB)]
        hid_lo = [sb("phase", f"hid_lo{k}", [P, TOK], F32R) for k in range(FB)]
        logits1 = sb("phase", "logits1", [P, TC, ROUTED1])
        above1 = sb("phase", "above1", [P, TC, ROUTED1, ROUTED1])
        tied1 = sb("phase", "tied1", [P, TC, ROUTED1, ROUTED1])
        rank1 = sb("phase", "rank1", [P, TC, ROUTED1])
        best1 = sb("phase", "best1", [P, TC])
        gate1 = sb("phase", "gate1", [P, TC, E1])

        banks = ctx.enter_context(nc.psum_tensor("banks", [P, 8, 512], F32))

        def pb(i):
            return banks[:, i, :] if isinstance(i, int) else banks[:, bass.ds(i, 1), :].rearrange("p a n -> p (a n)")

        def two(i):
            return banks[:, 2 * i:2 * i + 2, :].rearrange("p a n -> p (a n)")

        loaded = {n: sem("loaded_" + n) for n in ("x", "first", "table", "later", "rows", "b2")}
        ctx_loaded = sem("ctx_loaded")
        raw_loaded = [sem(f"raw_loaded{k}") for k in range(2)]
        stored = sem("stored")
        dve_step, pool_step = sem("dve_step"), sem("pool_step")
        stats_ready, moments_ready, var_ready, rstd_ready, xn_ready = (
            sem(n) for n in ("stats_ready", "moments_ready", "var_ready", "rstd_ready", "xn_ready"))
        pair_var_ready, pair_rstd_ready = sem("pair_var_ready"), sem("pair_rstd_ready")
        xt_done, xt0_ready, xt1_ready = sem("xt_done"), sem("xt0_ready"), sem("xt1_ready")
        q_done, q_hi_ready, q_lo_ready, heads_ready = sem("q_done"), sem("q_hi_ready"), sem("q_lo_ready"), sem("heads_ready")
        w_hi_ready, w_lo_ready, ctx_hi_ready, ctx_lo_ready = (
            sem(n) for n in ("w_hi_ready", "w_lo_ready", "ctx_hi_ready", "ctx_lo_ready"))
        proj_done, k_hi_ready, piece_taken = sem("proj_done"), sem("k_hi_ready"), sem("piece_taken")
        scores_done, raw_max, max_ready, exp_done = sem("scores_done"), sem("raw_max"), sem("max_ready"), sem("exp_done")
        t_done, pt0_ready, pt1_ready = sem("t_done"), sem("pt0_ready"), sem("pt1_ready")
        quarter_done, masked_ready, attn_ready = sem("quarter_done"), sem("masked_ready"), sem("attn_ready")
        inverted, diag_ready, spread_taken, tile_added = (
            sem(n) for n in ("inverted", "diag_ready", "spread_taken", "tile_added"))
        out_done, x_updated = sem("out_done"), sem("x_updated")
        s4_norm = sem("s4_norm")
        s4_exp, taps_ready = sem("s4_exp"), sem("taps_ready")
        conv_ready, silu_ready, back_done = sem("conv_ready"), sem("silu_ready"), sem("back_done")

        hi_done, lo_done, x_hi_ready, x_lo_ready = sem("hi_done"), sem("lo_done"), sem("x_hi_ready"), sem("x_lo_ready")
        keys_ready, logits_done, ssq_ready = sem("keys_ready"), sem("logits_done"), sem("ssq_ready")
        centred, gate_exp, gate_ready = sem("centred"), sem("gate_exp"), sem("gate_ready")
        gate_turned, gateT_ready, bias_done = (sem(n) for n in ("gate_turned", "gateT_ready", "bias_done"))
        up_done, gelu_done, h_hi_ready, h_ready = sem("up_done"), sem("gelu_done"), sem("h_hi_ready"), sem("h_ready")
        down_done, combined = sem("down_done"), sem("combined")
        ctxT2_loaded = [sem(f"ctxT2_loaded{p}") for p in range(TC)]
        ctxN2_loaded = [sem(f"ctxN2_loaded{p}") for p in range(TC)]
        mask_loaded = [sem(f"mask_loaded{p}") for p in range(TC)]
        maskneg_ready, scores2_done, max2_ready, exp2_done = (
            sem(n) for n in ("maskneg_ready", "scores2_done", "max2_ready", "exp2_done"))
        turned2, left2_ready, right2_ready, mixed_done = (sem(n) for n in ("turned2", "left2_ready", "right2_ready", "mixed_done"))
        mixed_taken = sem("mixed_taken")
        early_turned, early_ready = sem("early_turned"), sem("early_ready")
        expa_ready, pads_ready, ag_done, a_ready, g_ready = (sem(n) for n in ("expa_ready", "pads_ready", "ag_done", "a_ready", "g_ready"))
        conv1_ready, a_silu, bc_done, bc_ready = (sem(n) for n in ("conv1_ready", "a_silu", "bc_done", "bc_ready"))
        low_done, low_ready, step_done, abs_ready, soft_ready, drive_ready = (
            sem(n) for n in ("low_done", "low_ready", "step_done", "abs_ready", "soft_ready", "drive_ready"))
        soft_taken, relu_ready, inject_free, step_taken = (
            sem(n) for n in ("soft_taken", "relu_ready", "inject_free", "step_taken"))
        Bbc_done, Cbc_done = (sem(n) for n in ("Bbc_done", "Cbc_done"))
        Bbc_ready = [sem(f"Bbc{s}_ready") for s in range(GS)]
        Cbc_ready = [sem(f"Cbc{s}_ready") for s in range(GS)]
        decay_ready, inject_ready, scanned, shown_ready, shown_used, y_ready, gated_ready = (
            sem(n) for n in ("decay_ready", "inject_ready", "scanned", "shown_ready", "shown_used", "y_ready", "gated_ready"))
        gates_done = sem("gates_done")
        bc_hi_ready, two_hot_ready, first_tap, exp_soft, projected = (
            sem(n) for n in ("bc_hi_ready", "two_hot_ready", "first_tap", "exp_soft", "projected"))
        out1_done = sem("out1_done")
        wf_loaded = [sem(f"wf_loaded{k}") for k in range(FB)]
        logits1_done, centred1, gate1_exp, gate1_ready = (sem(n) for n in ("logits1_done", "centred1", "gate1_exp", "gate1_ready"))
        f_hi_ready, f_lo_ready, x1_hi_ready, x1_lo_ready, gu_done, gu_free, silu1_ready, hid_ready = (
            sem(n) for n in ("f_hi_ready", "f_lo_ready", "x1_hi_ready", "x1_lo_ready", "gu_done", "gu_free", "silu1_ready", "hid_ready"))
        hid_hi_ready, hid_lo_ready, down1_done, combined1 = (
            sem(n) for n in ("hid_hi_ready", "hid_lo_ready", "down1_done", "combined1"))

        def norm_of(k, t):
            return TC * (k - 1) + t + 1

        def piece_at(b, step, last=False):
            return 8 * b + (3 + step - sum(last and step > at for at in NEXT_KEYS_AT))

        block = ctx.enter_context(nc.Block())

        @block.sync
        def _(sp):
            sp.dma_start(X[:], d["x"].rearrange("(c p) n -> p c n", p=P)).then_inc(loaded["x"], 16)
            sp.dma_start(table[:], d["table"]).then_inc(loaded["table"], 16)
            sp.dma_start(first[:], d["first"]).then_inc(loaded["first"], 16)
            sp.dma_start(ctx_raw[:], d["ctxT"][0]).then_inc(ctx_loaded, 16)
            sp.dma_start(rows[:], d["rows"]).then_inc(loaded["rows"], 16)
            sp.dma_start(later[:], d["later"]).then_inc(loaded["later"], 16)
            sp.dma_start(b2[:], d["b2"]).then_inc(loaded["b2"], 16)
            with sp.Fori(0, B - 1) as n:
                sp.wait_ge(ctx_lo_ready, DC * n + DC)
                sp.dma_start(ctx_raw[:], d["ctxT"][bass.ds(n + 1, 1)].rearrange("a p c n -> p (a c) n")).then_inc(ctx_loaded, 16)
            for k, pieces in enumerate((piece_at(B - 2, VALUES_AT[-1]), 8 * B)):
                sp.wait_ge(proj_done, pieces)
                sp.dma_start(raw[k][:], d["w0"][k]).then_inc(raw_loaded[k], 16)
            sp.wait_ge(x_updated, 2)
            for m in range(2):
                sp.dma_start(mask[m][:], d["mask"][m * P:(m + 1) * P]).then_inc(mask_loaded[m], 16)
            with sp.Fori(0, E0 // 2 - 1) as n:
                for k in range(2):
                    sp.wait_ge(lo_done, 8 * n + 4 * (k + 1))
                    sp.dma_start(raw[k][:], d["w0"][bass.ds(2 * n + (2 + k), 1)].rearrange("a p n -> p (a n)"))\
                        .then_inc(raw_loaded[k], 16)
            for p in range(TC):
                if p == 0:
                    sp.wait_ge(lo_done, 4 * E0)
                elif p == 1:
                    sp.wait_ge(down_done, UNITS * (E0 - 1))
                elif p == 2:
                    sp.wait_ge(x_updated, 3)
                    for m in (2, 3):
                        sp.dma_start(mask[m][:], d["mask"][m * P:(m + 1) * P]).then_inc(mask_loaded[m], 16)
                sp.dma_start(ctxT2[p][:], d["ctxT"][2 * p:2 * p + 2].rearrange("b p c n -> p b c n"))\
                    .then_inc(ctxT2_loaded[p], 16)
                sp.dma_start(ctxN2[p][:], d["ctxN"][2 * p:2 * p + 2].rearrange("b p k n -> p b k n"))\
                    .then_inc(ctxN2_loaded[p], 16)
            sp.wait_ge(x_updated, 4)
            for k in range(FB):
                sp.dma_start(wf[k][:], d["w1"][k]).then_inc(wf_loaded[k], 16)
            with sp.Fori(0, E1 // FB - 1) as n:
                for k in range(FB):
                    sp.wait_ge(f_lo_ready, FB * n + (k + 1))
                    sp.dma_start(wf[k][:], d["w1"][bass.ds(FB * n + (FB + k), 1)].rearrange("a p n -> p (a n)"))\
                        .then_inc(wf_loaded[k], 16)
            sp.wait_ge(x_updated, LAYERS)
            sp.dma_start(out.rearrange("(c p) n -> p c n", p=P), X[:]).then_inc(stored, 16)
            sp.wait_ge(stored, 16)

        @block.gpsimd
        def _(pool):
            order = Order(pool, pool_step)

            def rstd_of(k, t):
                pool.wait_ge(var_ready, norm_of(k, t))
                nc.gpsimd.tensor_tensor(rstd[:, t:t + 1], vareps[:, t:t + 1], part(table, TABLE, "minus_half")[:, 0:1], ALU.pow)\
                    .then_inc(rstd_ready, 1)

            def split_heads(b):
                for g in range(STACKS):
                    pool.wait_ge(q_lo_ready, g + 1)
                    if not (isinstance(b, int) and b == 0):
                        pool.wait_ge(scores_done, 8 * b + (2 * g - 6))
                    for q, to in zip(q_part, q_stack):
                        last = nc.gpsimd.tensor_tensor(
                            to[:, g], over(q[:, g, bass.ds(b * S, S)], 4, 1).bitcast(F32), over(part(table, TABLE, "quad"), S, 2),
                            ALU.mult)
                    last.then_inc(heads_ready, 1)

            def diagonals(b, c):
                pool.wait_ge(inverted, DC * b + (c + 1))
                if not (isinstance(b, int) and b == 0 and c == 0):
                    pool.wait_ge(quarter_done, 8 * b + (PAIRS * c - 3))
                nc.gpsimd.tensor_tensor(inv_diag[:], over(ident, PAIRS, 1), over(inv_sums[c][:], P, 2), ALU.mult)\
                    .then_inc(diag_ready, 1)

            def context_low(b, k):
                for c in range(DC):
                    pool.wait_ge(ctx_hi_ready, DC * b + (c + 1))
                    nc.gpsimd.tensor_tensor(ctx_lo[k][:, c, :], ctx_raw[:, c, :], ctx_hi[k][:, c, :].bitcast(F32), ALU.subtract)\
                        .then_inc(ctx_lo_ready, 1)

            def filter_taps():
                N, MN = DC * NSTATE, [P, MODES, DC * NSTATE]
                mul, add, sub = ALU.mult, ALU.add, ALU.subtract

                def tt(o, a, b, op):
                    order.step(nc.gpsimd.tensor_tensor(o, a, b, op))

                def modes(name):
                    return over(part(table, TABLE, name), N, 2)

                def poles(ap):
                    return over(ap, MODES, 1)

                def by_state(ap):
                    return over(ap, NSTATE, 2)

                pool.wait_ge(s4_exp, 2)
                pool.wait_ge(loaded["later"], 16)
                w3 = {n: s4[n][:].rearrange("p (c n) -> p c n", c=DC) for n in s4}
                im3 = part(later, LATER, "w_im").rearrange("p (c n) -> p c n", c=DC)
                tt(w3["wr"], w3["ew"], by_state(s4dt[:]), mul)
                tt(w3["wi"], im3, by_state(s4dt[:]), mul)
                wr, wi = poles(s4["wr"][:]), poles(s4["wi"][:])
                g = [x[:] for x in s4g]
                tt(g[0], wr, modes("cr"), mul)
                tt(g[1], wi, modes("ci"), mul)
                tt(g[0], g[0], g[1], add)
                tt(g[0], g[0], modes("ar"), add)
                tt(g[1], wr, modes("ci"), mul)
                tt(g[2], wi, modes("cr"), mul)
                tt(g[1], g[1], g[2], sub)
                tt(g[1], g[1], modes("ai"), add)
                tt(g[2], g[0], g[0], mul)
                tt(g[3], g[1], g[1], mul)
                tt(g[2], g[2], g[3], add)
                pool.sem_inc(s4_norm, 1)
                yield
                pool.wait_ge(s4_norm, 2)
                tt(g[3], g[0], g[2], mul)
                tt(g[4], g[1], g[2], mul)
                gr, gi = g[3], g[4]
                yield
                pair = {n: part(later, LATER, n).rearrange("p (n two) -> p n two", two=2) for n in ("B", "C", "P")}
                re = {n: pair[n][:, :, 0] for n in pair}
                im = {n: pair[n][:, :, 1] for n in pair}
                t = s4t[:]

                def both(o, a, b, e, f, op):
                    tt(o, a, b, mul)
                    tt(t, e, f, mul)
                    tt(o, o, t, op)

                both(s4v[:, 0], re["B"], re["C"], im["B"], im["C"], sub)
                both(s4v[:, 1], re["B"], im["C"], im["B"], re["C"], add)
                both(s4v[:, 2], re["B"], re["P"], im["B"], im["P"], add)
                both(s4v[:, 3], im["B"], re["P"], re["B"], im["P"], sub)
                both(s4v[:, 4], re["P"], re["C"], im["P"], im["C"], sub)
                both(s4v[:, 5], re["P"], im["C"], im["P"], re["C"], add)
                both(s4v[:, 6], re["P"], re["P"], im["P"], im["P"], add)
                yield
                prod = [s4p[:, k].rearrange("p (m c) n -> p m (c n)", m=MODES) for k in range(8)]
                for k in range(3):
                    if k:
                        yield
                    vr, vi = poles(s4v[:, 2 * k]), poles(s4v[:, 2 * k + 1])
                    tt(prod[2 * k], vr, gr, mul)
                    tt(g[5], vi, gi, mul)
                    tt(prod[2 * k], prod[2 * k], g[5], add)
                    tt(prod[2 * k + 1], vi, gr, mul)
                    tt(g[5], vr, gi, mul)
                    tt(prod[2 * k + 1], prod[2 * k + 1], g[5], sub)
                tt(prod[6], poles(s4v[:, 6]), gr, mul)
                tt(prod[7], poles(s4v[:, 6]), gi, mul)
                yield
                flat = s4p[:].rearrange("p k m n -> p (k m) n")
                n = NSTATE // 2
                while n:
                    tt(flat[:, :, 0:n], flat[:, :, 0:n], flat[:, :, n:2 * n], add)
                    n //= 2
                Z = [s4s[:, k] for k in range(14)]
                for k in range(8):
                    tt(Z[k], s4p[:, k, :, 0].rearrange("p (m c) -> p m c", m=MODES), over(s4dt[:], MODES, 1), mul)
                yield
                cr, ci = (over(part(table, TABLE, n), DC, 2) for n in ("cr", "ci"))
                dr, di, tr, ti, u0, u1 = Z[8:14]
                tt(dr, cr, Z[6], mul)
                tt(u0, ci, Z[7], mul)
                tt(dr, dr, u0, add)
                order.step(nc.gpsimd.tensor_scalar_add(dr, dr, 1.0))
                tt(di, ci, Z[6], mul)
                tt(u0, cr, Z[7], mul)
                tt(di, di, u0, sub)
                tt(u0, Z[2], Z[4], mul)
                tt(u1, Z[3], Z[5], mul)
                tt(u0, u0, u1, sub)
                tt(u1, Z[2], Z[5], mul)
                tt(tr, Z[3], Z[4], mul)
                tt(u1, u1, tr, add)
                tt(tr, cr, u0, mul)
                tt(ti, ci, u1, mul)
                tt(tr, tr, ti, sub)
                tt(ti, cr, u1, mul)
                tt(u0, ci, u0, mul)
                tt(ti, ti, u0, add)
                yield
                tt(u0, dr, dr, mul)
                tt(u1, di, di, mul)
                tt(u0, u0, u1, add)
                one = part(table, TABLE, "minus_one").rearrange("p (m c) -> p m c", m=MODES)
                tt(u0, u0, one, ALU.pow)
                tt(u1, tr, dr, mul)
                tt(Z[2], ti, di, mul)
                tt(u1, u1, Z[2], add)
                tt(u1, u1, u0, mul)
                tt(Z[0], Z[0], u1, sub)
                tt(u1, ti, dr, mul)
                tt(Z[2], tr, di, mul)
                tt(u1, u1, Z[2], sub)
                tt(u1, u1, u0, mul)
                tt(Z[1], Z[1], u1, sub)
                yield
                for name, k in (("alpha", 0), ("beta", 1)):
                    for c in range(DC):
                        tt(s4l[k][:, :, c, :], over(Z[k][:, :, c], B, 1),
                           part(table, TABLE, name).rearrange("p (l m) -> p l m", l=B), mul)
                tt(s4l[0][:], s4l[0][:], s4l[1][:], add)
                for m in range(1, MODES):
                    tt(s4l[0][:, :, :, 0], s4l[0][:, :, :, 0], s4l[0][:, :, :, m], add)
                order.step(nc.gpsimd.tensor_copy(taps[:], s4l[0][:, :, :, 0]))
                nc.gpsimd.tensor_tensor(taps[:, 0, :], taps[:, 0, :], part(later, LATER, "D"), add).then_inc(taps_ready, 1)

            pool.wait_ge(loaded["table"], 16)
            for t in range(TC):
                rstd_of(1, t)
            for j, n in enumerate(("wk", "wv")):
                pool.wait_ge(w_hi_ready, j + 1)
                nc.gpsimd.tensor_tensor(w_kv[j][1][:], part(first, FIRST, n).rearrange("p (c n) -> p c n", c=DC),
                                        w_kv[j][0][:].bitcast(F32), ALU.subtract).then_inc(w_lo_ready, 1)
            context_low(0, 0)
            split_heads(0)
            def split_low(e, k):
                for q in range(4):
                    cols = slice(q * QW, (q + 1) * QW)
                    pool.wait_ge(hi_done, 4 * e + (q + 1))
                    nc.gpsimd.tensor_tensor(w_lo[k][:, cols], raw[k][:, cols], w_hi[k][:, cols].bitcast(F32), ALU.subtract)\
                        .then_inc(lo_done, 1)

            taps_parts = filter_taps()
            next(taps_parts)
            context_low(1, 1)
            diagonals(0, 0)
            split_heads(1)
            next(taps_parts)
            diagonals(0, 1)
            next(taps_parts)
            context_low(2, 0)
            diagonals(1, 0)
            split_heads(2)
            next(taps_parts)
            with pool.Fori(1, B // 2 - 1) as n:
                for k in range(2):
                    diagonals(2 * n + (k - 1), 1)
                    context_low(2 * n + (k + 1), 1 - k)
                    diagonals(2 * n + k, 0)
                    split_heads(2 * n + (k + 1))
            diagonals(B - 3, 1)
            next(taps_parts)
            context_low(B - 1, 1)
            diagonals(B - 2, 0)
            split_heads(B - 1)
            next(taps_parts)
            diagonals(B - 2, 1)
            next(taps_parts)
            for t in range(TC - 1):
                rstd_of(2, t)
            diagonals(B - 1, 0)
            next(taps_parts)
            diagonals(B - 1, 1)
            for _ in taps_parts:
                pass
            rstd_of(2, TC - 1)
            split_low(0, 0)
            for t in range(TC):
                rstd_of(3, t)

            keys3 = part(later, LATER, "keys").rearrange("p (c e) -> p c e", c=DC)
            rw3 = part(later, LATER, "rw").rearrange("p (c e) -> p c e", c=DC)
            order.step(nc.gpsimd.tensor_tensor(key_sum[:], keys3, keys3, ALU.add))
            nc.gpsimd.tensor_tensor(key_sum[:], key_sum[:], rw3, ALU.add).then_inc(keys_ready, 1)
            order.step(nc.gpsimd.tensor_tensor(key_sq[:], keys3, keys3, ALU.mult))
            nc.gpsimd.tensor_scalar(key_sq[:], key_sq[:], -1.0, 0.0, ALU.mult, ALU.add).then_inc(keys_ready, 1)

            split_low(1, 1)
            with pool.Fori(0, E0 // 2 - 1) as n:
                for k in range(2):
                    split_low(2 * n + (2 + k), k)

            def mask_term(p):
                pool.wait_ge(mask_loaded[p], 16)
                nc.gpsimd.tensor_scalar(mask[p][:].bitcast(F32), mask[p][:], 0, NEG * 16, ALU.is_equal, ALU.mult)\
                    .then_inc(maskneg_ready, 1)

            def rstd_of_pair(p):
                pool.wait_ge(pair_var_ready, p + 1)
                nc.gpsimd.tensor_tensor(stat2[:, p, 3:4], stat2[:, p, 2:3], part(table, TABLE, "minus_half")[:, 0:1], ALU.pow)\
                    .then_inc(pair_rstd_ready, 1)

            mask_term(0)
            mask_term(1)
            for t in range(TC):
                rstd_of(4, t)
            mask_term(2)
            mask_term(3)
            for p in range(TC):
                rstd_of_pair(p)
                rstd_of(5, p)

            pool.wait_ge(x_updated, 4)
            nc.gpsimd.memset(a_pad[:, :, :, 0:KER - 1], 0.0).then_inc(pads_ready, 1)
            for k in range(2):
                last = nc.gpsimd.memset(decay[k][:].rearrange("p g (b s) -> p (g b) s", s=S)[:, :, 0:1], 0.0)
            last.then_inc(pads_ready, 1)

            def chunk_of(tile, m):
                return tile[:].rearrange("p c n -> p (c n)")[:, bass.ds(m * TOK, TOK)]

            def injected(m, first_chunk, last=False):
                for g in range(GROUPS):
                    if first_chunk:
                        for ready in Bbc_ready:
                            pool.wait_ge(ready, g + 1)
                        pool.wait_ge(drive_ready, 1)
                    if g >= 2 or not first_chunk:
                        pool.wait_ge(scanned, GROUPS * m + (g - 1))
                        pool.sem_inc(inject_free, 1)
                    nc.gpsimd.tensor_tensor(inject[g % 2][:], Bbc[:, GS * g:GS * (g + 1), :],
                                            over(chunk_of(drive, m), GS, 1), ALU.mult).then_inc(inject_ready, 1)
                    if g == GROUPS // 2 and not last:
                        step_end(m + 1)

            def step_end(m):
                pool.wait_ge(soft_ready, CC)
                pool.wait_ge(relu_ready, CC)
                nc.gpsimd.tensor_tensor(chunk_of(delta, m), chunk_of(delta, m), chunk_of(drive, m), ALU.add).then_inc(soft_taken, 1)
                pool.wait_ge(soft_taken, m + 1)
                pool.sem_inc(step_taken, 1)
                nc.gpsimd.tensor_tensor(chunk_of(drive, m), chunk_of(delta, m), chunk_of(aT, m), ALU.mult).then_inc(drive_ready, 1)
                pool.wait_ge(drive_ready, m + 1)
                pool.sem_inc(step_taken, 1)

            pool.wait_ge(a_silu, CC)
            injected(0, True)
            with pool.Fori(1, CC - 1) as m:
                injected(m, False)
            injected(CC - 1, False, True)

            def split_low1(n):
                for k in range(FB):
                    pool.wait_ge(f_hi_ready, FB * n + (k + 1))
                    nc.gpsimd.tensor_tensor(f_lo[k][:], wf[k][:], f_hi[k][:].bitcast(F32), ALU.subtract).then_inc(f_lo_ready, 1)

            for t in range(TC):
                rstd_of(6, t)
            split_low1(0)
            with pool.Fori(1, E1 // FB) as n:
                split_low1(n)

        @block.scalar
        def _(act):
            def transposed(k):
                act.wait_ge(xt_done, 2 * k - 1)
                nc.scalar.activation(xnT[:, 0, :], pb(0), ACT.Copy).then_inc(xt0_ready, 1)

            def token_high(k, in_banks, to, ready, low_ready):
                for c in range(DC):
                    act.wait_ge(xt_done, 2 * k - 1 + c)
                    nc.scalar.activation(to[:, c, :], pb(in_banks[c]), ACT.Copy).then_inc(ready, 1)
                act.wait_ge(low_ready, 1)
                nc.scalar.activation(xnT[:, 0, :], pb(in_banks[0]), ACT.Copy).then_inc(xt0_ready, 1)

            def context_high(b, k):
                act.wait_ge(ctx_loaded, 16 * b + 16)
                for c in range(DC):
                    nc.scalar.activation(ctx_hi[k][:, c, :], ctx_raw[:, c, :], ACT.Copy).then_inc(ctx_hi_ready, 1)

            def key_piece(piece, c, half, bank=4):
                act.wait_ge(proj_done, piece)
                for g in range(2):
                    at = slice(64 * g, 64 * g + 64)
                    nc.scalar.activation(k_stack[at, DC * c + g, half * 512:(half + 1) * 512], pb(bank)[at, :], ACT.Identity,
                                         bias=part(first, FIRST, "bk")[at, c:c + 1]).then_inc(k_hi_ready, 1)

            def batch(b, par, last):
                for i in range(8):
                    if i in KEYS_AT:
                        key_piece(piece_at(b, i), 1, KEYS_AT.index(i))
                    if i in NEXT_KEYS_AT and not last:
                        key_piece(piece_at(b, i), 0, NEXT_KEYS_AT.index(i))
                    act.wait_ge(max_ready, 8 * b + (i + 1))
                    if i >= 2 or not (isinstance(b, int) and b == 0):
                        act.wait_ge(t_done, 16 * b + 2 * (i - 1))
                    nc.scalar.activation(probs[i % 2][:], two(i % 2), ACT.Exp, bias=negmax[i % 2][:], scale=0.25,
                                         accum_out=sums[i // PAIRS][:, i % PAIRS:i % PAIRS + 1]).then_inc(exp_done, 1)
                    if i >= 1:
                        second_half(b, i - 1)
                    elif not (isinstance(b, int) and b == 0):
                        second_half(b - 1, 7)
                    if i == 1 and not last:
                        context_high(b + 1, 1 - par)

            def second_half(b, i):
                c, j = divmod(i, PAIRS)
                act.wait_ge(t_done, 16 * b + 2 * i + 2)
                nc.scalar.activation(probsT[c][:, KC // 2:KC, j, :], pb(6).rearrange("p (k n) -> p k n", n=P),
                                     ACT.Copy).then_inc(pt1_ready, 1)

            act.wait_ge(loaded["first"], 16)
            for j, n in enumerate(("wk", "wv")):
                nc.scalar.activation(w_kv[j][0][:], part(first, FIRST, n).rearrange("p (c n) -> p c n", c=DC), ACT.Copy)\
                    .then_inc(w_hi_ready, 1)
            transposed(1)
            context_high(0, 0)
            for g in range(STACKS):
                act.wait_ge(q_done, g + 1)
                nc.scalar.activation(q_part[0][:, g, :], pb(Q_BANKS[g]), ACT.Identity, bias=part(first, FIRST, "bq")[:, g:g + 1])\
                    .then_inc(q_hi_ready, 1)
            for half in range(2):
                key_piece(half + 1, 0, half, FIRST_BANKS[half])
            act.wait_ge(loaded["later"], 16)
            nc.scalar.activation(s4dt[:], part(later, LATER, "log_dt"), ACT.Exp).then_inc(s4_exp, 1)
            nc.scalar.activation(s4["ew"][:], part(later, LATER, "inv_w"), ACT.Exp).then_inc(s4_exp, 1)
            batch(0, 0, False)
            with act.Fori(0, B // 2 - 1) as n:
                for k in range(2):
                    batch(2 * n + (1 + k), 1 - k, False)
            batch(B - 1, 1, True)
            second_half(B - 1, 7)
            def split_high(e, half_e, k, q):
                if q == 0:
                    act.wait_ge(raw_loaded[k], 16 * half_e + 16)
                    if not (isinstance(e, int) and e < 2):
                        act.wait_ge(down_done, UNITS * (e - 1))
                cols = slice(q * QW, (q + 1) * QW)
                nc.scalar.activation(w_hi[k][:, cols], raw[k][:, cols], ACT.Copy).then_inc(hi_done, 1)

            act.wait_ge(out_done, TC)
            for q in range(4):
                split_high(0, 0, 0, q)
            transposed(2)
            for c in range(DC):
                act.wait_ge(conv_ready, c + 1)
                nc.scalar.activation(conv[1][:, c, :], conv[0][:, c, :], ACT.Silu).then_inc(silu_ready, 1)

            def gelu(e, u):
                act.wait_ge(up_done, UNITS * e + (u + 1))
                if not (isinstance(e, int) and e == 0 and u < 2):
                    act.wait_ge(h_hi_ready, UNITS * e + (u - 1))
                    act.wait_ge(h_ready, UNITS * e + (u - 1))
                nc.scalar.activation(h_full[u % 2][:], pb(u % 2), ACT.Gelu,
                                     bias=part(later, LATER, "b1")[:, bass.ds(UNITS * e + u, 1)]).then_inc(gelu_done, 1)

            def pair_of_experts(n, is_first, is_last):
                for k in range(2):
                    e = 2 * n + k
                    for u in range(UNITS):
                        gelu(e, u)
                        if 2 <= u < 6 and not (is_last and k):
                            split_high(e + 1, n + k, 1 - k, u - 2)
                        if is_first and k == 0 and u == 0:
                            for t in range(TC):
                                if t:
                                    act.wait_ge(ssq_ready, t)
                                nc.scalar.activation(squares[:], xn[:, t, :], ACT.Square, accum_out=sumsq[:, t:t + 1])\
                                    .then_inc(ssq_ready, 1)
                        if is_first and k == 1 and u == 0:
                            act.wait_ge(centred, 1)
                            nc.scalar.activation(gate[:], logits[:], ACT.Exp).then_inc(gate_exp, 1)
                        if is_first and k == 1 and u == 4:
                            act.wait_ge(gate_turned, 1)
                            nc.scalar.activation(gateT[:], pb(3)[0:E0, :].rearrange("e (t n) -> e t n", t=TC), ACT.Copy)\
                                .then_inc(gateT_ready, 1)

            token_high(3, X_BANKS, x_hi, x_hi_ready, x_lo_ready)
            pair_of_experts(0, True, False)
            with act.Fori(1, E0 // 2 - 1) as n:
                pair_of_experts(n, False, False)
            pair_of_experts(E0 // 2 - 1, False, True)

            act.wait_ge(early_turned, 1)
            nc.scalar.activation(xnT[:, :, 0:P], pb(7)[:, 0:DC * P].rearrange("p (c n) -> p c n", c=DC), ACT.Copy).then_inc(early_ready, 1)
            act.wait_ge(xt_done, 7)
            nc.scalar.activation(xnT[:, 0, P:TOK], pb(4)[:, P:TOK], ACT.Copy).then_inc(xt0_ready, 1)

            def weights2(p):
                k = p % 2
                act.wait_ge(max2_ready, p + 1)
                nc.scalar.activation(probs2[k][:], probs2[k][:], ACT.Exp, bias=stat2[:, p, 0:1], scale=1.0 / 16,
                                     accum_out=stat2[:, p, 1:2]).then_inc(exp2_done, 1)

            def right_half(p):
                act.wait_ge(turned2, 2 * p + 2)
                if p:
                    act.wait_ge(mixed_done, p)
                nc.scalar.activation(probsT2[:, KC // 2:KC, :], pb(5).rearrange("p (k n) -> p k n", n=P), ACT.Copy)\
                    .then_inc(right2_ready, 1)

            weights2(0)
            weights2(1)
            for p in range(TC):
                right_half(p)
                if p + 2 < TC:
                    weights2(p + 2)

            early = slice(0, TOK - P)
            act.wait_ge(early_turned, 2)
            for c in range(DC):
                nc.scalar.activation(xnT[:, c, early], pb(c)[:, early], ACT.Copy).then_inc(early_ready, 1)
            act.wait_ge(xt_done, 9)
            nc.scalar.activation(xnT[:, 0, TOK - P:TOK], pb(0)[:, TOK - P:TOK], ACT.Copy).then_inc(xt0_ready, 1)
            act.wait_ge(pads_ready, 2)

            def silu_a(m):
                act.wait_ge(conv1_ready, m + 1)
                nc.scalar.activation(aT[:, m, :], hidden[m // 2][:, m % 2, :], ACT.Silu).then_inc(a_silu, 1)

            conv_w = part(later, LATER, "conv_w").rearrange("p (c k) -> p c k", c=CC)
            for m in range(CC):
                act.wait_ge(ag_done, m + 1)
                nc.scalar.activation(hidden[m // 2][:, m % 2, :], pb(2 + m), ACT.Identity, scale=conv_w[:, m, KER - 1:KER],
                                     bias=part(later, LATER, "conv_b")[:, m:m + 1]).then_inc(first_tap, 1)
                nc.scalar.activation(a_pad[:, m, :, KER - 1:], pb(2 + m).rearrange("p (b s) -> p b s", b=B), ACT.Copy)\
                    .then_inc(a_ready, 1)
                if m >= 2:
                    silu_a(m - 2)
            for m in range(CC - 2, CC):
                silu_a(m)
            nc.scalar.activation(exp_a[:], part(later, LATER, "a_param"), ACT.Exp, scale=-1.0).then_inc(expa_ready, 1)
            act.wait_ge(low_done, 1)
            nc.scalar.activation(lowT[:], pb(7), ACT.Copy).then_inc(low_ready, 1)
            def exp_of_step(m):
                act.wait_ge(abs_ready, m + 1)
                nc.scalar.activation(drive[:, m, :], drive[:, m, :], ACT.Exp, scale=-1.0).then_inc(exp_soft, 1)

            for m in range(CC):
                act.wait_ge(step_done, m + 1)
                nc.scalar.activation(drive[:, m, :], pb(2 + m), ACT.Abs, bias=part(later, LATER, "d_param")[:, m:m + 1])\
                    .then_inc(abs_ready, 1)
                if m:
                    exp_of_step(m - 1)
            exp_of_step(CC - 1)
            act.wait_ge(bc_done, 1)
            nc.scalar.activation(bc[0:2 * NSTATE, :], pb(6)[0:2 * NSTATE, :], ACT.Copy).then_inc(bc_hi_ready, 1)
            act.wait_ge(exp_soft, CC)
            for m in range(CC):
                nc.scalar.activation(drive[:, m, :], drive[:, m, :], ACT.Ln, bias=ones[:, 0:1]).then_inc(soft_ready, 1)

            def rows_of_b(g):
                for s in range(GS):
                    act.wait_ge(Bbc_done, GS * g + s + 1)
                    nc.scalar.activation(Bbc[:, GS * g + s, :], pb(s), ACT.Copy).then_inc(Bbc_ready[s], 1)

            def decays(m, first_chunk):
                for g in range(GROUPS):
                    if g == 0:
                        act.wait_ge(drive_ready, m + 1)
                    if g >= 2 or not first_chunk:
                        act.wait_ge(scanned, GROUPS * m + (g - 1))
                    row = delta[:, m, :] if first_chunk else delta[:, bass.ds(m, 1), :].rearrange("p c n -> p (c n)")
                    for s in range(GS):
                        last = nc.scalar.activation(
                            decay[g % 2][:, s, :].rearrange("p (b s) -> p b s", b=B)[:, :, 1:S],
                            row.rearrange("p (b s) -> p b s", b=B)[:, :, 1:S], ACT.Copy,
                            scale=exp_a[:, bass.ds(NSTATE * m + (GS * g + s), 1)])
                    last.then_inc(decay_ready, 1)
                    if first_chunk and g == 0:
                        for early in range(2, EARLY_B):
                            rows_of_b(early)
                    if first_chunk and EARLY_C <= g + 1 < GROUPS:
                        act.wait_ge(Cbc_done, GS * (g + 1) + 2)
                        nc.scalar.activation(Cbc[:, GS * (g + 1) + 1, :], pb(7), ACT.Copy).then_inc(Cbc_ready[1], 1)
                    if first_chunk and g and g + EARLY_B - 1 < GROUPS:
                        rows_of_b(g + EARLY_B - 1)
                    if first_chunk and g > GROUPS - CC:
                        silu_g(g - (GROUPS - CC + 1))

            def silu_g(m):
                act.wait_ge(gates_done, m + 1)
                nc.scalar.activation(gT[:, m, :], pb(G_BANKS[m]), ACT.Silu).then_inc(g_ready, 1)

            act.wait_ge(expa_ready, 1)
            rows_of_b(1)
            decays(0, True)
            silu_g(CC - 1)
            with act.Fori(1, CC) as m:
                decays(m, False)

            def split_high1(n, k, in_loop=True):
                act.wait_ge(wf_loaded[k], 16 * n + 16)
                if in_loop:
                    act.wait_ge(down1_done, FB * n + (k + 1))
                nc.scalar.activation(f_hi[k][:], wf[k][:], ACT.Copy).then_inc(f_hi_ready, 1)

            act.wait_ge(x_updated, 5)
            for k in range(2):
                split_high1(0, k, False)
            token_high(6, X1_BANKS, x1_hi, x1_hi_ready, x1_lo_ready)

            def expert1(n, k, last=False):
                act.wait_ge(gu_done, FB * n + (k + 1))
                act.wait_ge(gu_free, FB * n + (k + 1))
                nc.scalar.activation(act_f[k][:], pb(2 * k), ACT.Silu).then_inc(silu1_ready, 1)
                if k == 0:
                    split_high1(n, 2)
                elif not last:
                    split_high1(n + 1, k - 1)
                act.wait_ge(hid_ready, FB * n + (k + 1))
                nc.scalar.activation(hid_hi[k][:], hid_f[k][:], ACT.Copy).then_inc(hid_hi_ready, 1)

            expert1(0, 0)
            act.wait_ge(centred1, 1)
            nc.scalar.activation(logits1[:], logits1[:], ACT.Exp).then_inc(gate1_exp, 1)
            with act.Fori(0, E1 // FB - 1) as n:
                for k in range(1, FB):
                    expert1(n, k)
                expert1(n + 1, 0)
            for k in range(1, FB):
                expert1(E1 // FB - 1, k, True)

        @block.vector
        def _(dve):
            order = Order(dve, dve_step)

            def norm_stats(k, t):
                nc.vector.bn_stats(stats[:, t, :], X[:, t, :]).then_inc(stats_ready, 1)

            def norm_moments(k, t):
                dve.wait_ge(stats_ready, norm_of(k, t))
                nc.vector.bn_aggr(moments[:, t, :], stats[:, t, :]).then_inc(moments_ready, 1)

            def norm_variance(k, t):
                dve.wait_ge(moments_ready, norm_of(k, t))
                nc.vector.tensor_scalar_add(vareps[:, t:t + 1], moments[:, t, 1:2], EPS).then_inc(var_ready, 1)

            def norm_tile(k, t):
                dve.wait_ge(rstd_ready, norm_of(k, t))
                nc.vector.tensor_scalar(xn[:, t, :], X[:, t, :], moments[:, t, 0:1], rstd[:, t:t + 1],
                                        ALU.subtract, ALU.mult).then_inc(xn_ready, 1)

            def layer_norm(k):
                for i in range(TC + 3):
                    for stage, do in enumerate((norm_stats, norm_moments, norm_variance, norm_tile)):
                        if 0 <= i - stage < TC:
                            do(k, i - stage)

            def norm_begin(k, t):
                norm_stats(k, t)
                norm_moments(k, t)
                norm_variance(k, t)

            def transposed(k):
                dve.wait_ge(xt_done, 2 * k)
                nc.vector.tensor_copy(xnT[:, 1, :], pb(1)).then_inc(xt1_ready, 1)

            def token_low(k, in_banks, high, high_ready, to, ready):
                for c in range(DC):
                    dve.wait_ge(high_ready, c + 1)
                    nc.vector.tensor_tensor(to[:, c, :], pb(in_banks[c]), high[:, c, :].bitcast(F32), ALU.subtract).then_inc(ready, 1)
                nc.vector.tensor_copy(xnT[:, 1, :], pb(in_banks[1])).then_inc(xt1_ready, 1)

            dve.wait_ge(loaded["x"], 16)
            layer_norm(1)
            transposed(1)

            dve.wait_ge(loaded["rows"], 16)
            dve.wait_ge(xn_ready, norm_of(1, TC - 1))
            nc.vector.tensor_tensor(X[:], X[:], over(part(rows, ROWS, "bo"), TC, 1), ALU.add).then_inc(tile_added, 1)
            bq, bk, bv = part(first, FIRST, "bq"), part(first, FIRST, "bk"), part(rows, ROWS, "bv")
            dve.wait_ge(loaded["first"], 16)
            for g in range(STACKS):
                dve.wait_ge(q_hi_ready, g + 1)
                nc.vector.scalar_tensor_tensor(q_part[1][:, g, :], pb(Q_BANKS[g]), bq[:, g:g + 1], q_part[0][:, g, :].bitcast(F32),
                                               ALU.add, ALU.subtract).then_inc(q_lo_ready, 1)

            def key_piece(k_piece, c, half, bank=4):
                cols = slice(half * 512, (half + 1) * 512)
                for g in range(2):
                    at, to = slice(64 * g, 64 * g + 64), slice(64 - 64 * g, 128 - 64 * g)
                    dve.wait_ge(k_hi_ready, 2 * k_piece + (g - 1))
                    last = nc.vector.scalar_tensor_tensor(
                        k_stack[to, DC * c + g, cols], pb(bank)[at, :], bk[at, c:c + 1],
                        k_stack[at, DC * c + g, cols].bitcast(F32), ALU.add, ALU.subtract)
                last.then_inc(piece_taken, 1)

            def value_piece(piece, b, v):
                dve.wait_ge(proj_done, piece)
                if not (isinstance(b, int) and b == 0):
                    dve.wait_ge(quarter_done, 8 * b + (v - 3))
                nc.vector.tensor_tensor(V[:, 2 * v:2 * v + 2, :], pb(4).rearrange("p (k n) -> p k n", k=2), over(bv, 2, 1), ALU.add)\
                    .then_inc(piece_taken, 1)

            def invert_sums(b, c):
                dve.wait_ge(exp_done, 8 * b + PAIRS * (c + 1))
                if not (isinstance(b, int) and b == 0):
                    dve.wait_ge(diag_ready, DC * (b - 1) + (c + 1))
                nc.vector.reciprocal(inv_sums[c][:], sums[c][:]).then_inc(inverted, 1)

            def first_half(b, i):
                c, j = divmod(i, PAIRS)
                dve.wait_ge(t_done, 16 * b + 2 * i + 1)
                nc.vector.tensor_copy(probsT[c][:, 0:KC // 2, j, :], pb(5).rearrange("p (k n) -> p k n", n=P))\
                    .then_inc(pt0_ready, 1)

            def gather(b, par, c):
                dve.wait_ge(quarter_done, 8 * b + PAIRS * (c + 1))
                if not (isinstance(b, int) and b == 0 and c == 0):
                    dve.wait_ge(attn_ready, 2 * b + c)
                nc.vector.tensor_copy(own[:], pb(7)[:, P:2 * P].rearrange("p (h s) -> p h s", h=2)).then_inc(spread_taken, 1)
                dve.wait_ge(spread_taken, 2 * b + (c + 1))
                nc.vector.tensor_tensor(own[:], pb(7)[:, 0:P].rearrange("p (h s) -> p h s", h=2), own[:], ALU.mult)\
                    .then_inc(masked_ready, 1)
                dve.wait_ge(masked_ready, 2 * b + (c + 1))
                nc.vector.tensor_reduce(attn[:, c, par * S:(par + 1) * S], own[:].rearrange("p h s -> p s h"),
                                        AX.X, ALU.add).then_inc(attn_ready, 1)

            def add_tile(n):
                dve.wait_ge(out_done, n + 1)
                dve.wait_ge(tile_added, n + 1)
                to = X[:, n, :] if isinstance(n, int) else X[:, bass.ds(n, 1), :].rearrange("p t n -> p (t n)")
                nc.vector.tensor_tensor(to, to, pb(7)[:, 256:512], ALU.add).then_inc(tile_added, 1)

            def batch(b, par, last, tile=None):
                later_one = not (isinstance(b, int) and b == 0)
                for i in range(8):
                    dve.wait_ge(scores_done, 8 * b + (i + 1))
                    nc.vector.tensor_reduce(negmax_raw[i % 2][:], two(i % 2),
                                            AX.X, ALU.max, negate=True).then_inc(raw_max, 1)
                    dve.wait_ge(raw_max, 8 * b + (i + 1))
                    nc.vector.tensor_scalar(negmax[i % 2][:], negmax_raw[i % 2][:], 0.25, None, ALU.mult)\
                        .then_inc(max_ready, 1)
                    if i in KEYS_AT:
                        key_piece(4 * b + 3 + KEYS_AT.index(i), 1, KEYS_AT.index(i))
                    elif i in VALUES_AT:
                        value_piece(piece_at(b, i, last), b, VALUES_AT.index(i))
                    elif i in NEXT_KEYS_AT and not last:
                        key_piece(4 * b + 5 + NEXT_KEYS_AT.index(i), 0, NEXT_KEYS_AT.index(i))
                    if i == 5 and tile is not None:
                        add_tile(tile)
                    if i == 4:
                        invert_sums(b, 0)
                    if i == 0 and later_one:
                        invert_sums(b - 1, 1)
                    if i == 0 and later_one:
                        gather(b - 1, 1 - par, 0)
                    if i == 4 and later_one:
                        gather(b - 1, 1 - par, 1)
                    if i >= 1:
                        first_half(b, i - 1)
                    elif later_one:
                        first_half(b - 1, 7)
                    if last and 1 <= i < TC:
                        dve.wait_ge(tile_added, i + 1)
                        norm_begin(2, i - 1)
                    if last and 5 <= i < TC + 4:
                        norm_tile(2, i - 5)

            for half in range(2):
                key_piece(half + 1, 0, half, FIRST_BANKS[half])
            batch(0, 0, False)
            dve.wait_ge(s4_norm, 1)
            nc.vector.reciprocal(s4g[2][:], s4g[2][:]).then_inc(s4_norm, 1)
            with dve.Fori(0, B // 2 - 1) as n:
                batch(2 * n + 1, 1, False)
                batch(2 * n + 2, 0, False, n)
            batch(B - 1, 1, True)
            invert_sums(B - 1, 1)
            gather(B - 1, 1, 0)
            first_half(B - 1, 7)
            gather(B - 1, 1, 1)
            add_tile(TC - 1)
            dve.wait_ge(tile_added, TC + 1)
            dve.sem_inc(x_updated, 1)
            dve.wait_ge(x_updated, 1)
            norm_begin(2, TC - 1)
            norm_tile(2, TC - 1)
            transposed(2)
            dve.wait_ge(taps_ready, 1)
            dve.wait_ge(xt0_ready, 2)
            dve.wait_ge(xt1_ready, 2)
            for c in range(DC):
                order.step(nc.vector.tensor_scalar(conv[0][:, c, :], xnT[:, c, :], taps[:, 0, c:c + 1], None, ALU.mult))
                for l in range(1, B):
                    later_cols = conv[0][:, c, l * S:TOK]
                    ins = nc.vector.scalar_tensor_tensor(later_cols, xnT[:, c, 0:TOK - l * S], taps[:, l, c:c + 1],
                                                         later_cols, ALU.mult, ALU.add)
                    if l < B - 1:
                        order.step(ins)
                    else:
                        ins.then_inc(conv_ready, 1)
            for h in range(2):
                dve.wait_ge(back_done, h + 1)
                last = nc.vector.tensor_tensor(X[:, 2 * h:2 * h + 2, :], X[:, 2 * h:2 * h + 2, :],
                                               pb(2 + h).rearrange("p (t n) -> p t n", t=2), ALU.add)
            last.then_inc(x_updated, 1)

            def top(values, n, before, count, greater, equal, place_of):
                one, other = over(values, n, 3), over(values, n, 2)
                order.step(nc.vector.tensor_tensor(greater, other, one, ALU.is_gt))
                yield
                order.step(nc.vector.tensor_tensor(equal, other, one, ALU.is_equal))
                yield
                lower = over(part(table, TABLE, before), TC, 1)
                flat = equal.rearrange("p t a b -> p t (a b)")
                order.step(nc.vector.tensor_tensor(flat, flat, lower, ALU.mult))
                yield
                order.step(nc.vector.tensor_tensor(greater, greater, equal, ALU.add))
                yield
                order.step(nc.vector.tensor_reduce(place_of, greater, AX.X, ALU.add))
                order.step(nc.vector.tensor_scalar(place_of, place_of, float(count), None, ALU.is_lt))

            def router():
                dve.wait_ge(logits_done, 1)
                dve.wait_ge(ssq_ready, TC)
                rb = rank[:, 0, :]
                order.step(nc.vector.tensor_tensor(rb, pb(2)[:, TC * E0:(TC + 1) * E0], part(rows, ROWS, "rb"), ALU.add))
                for t in range(TC):
                    last = nc.vector.scalar_tensor_tensor(logits[:, t, :], pb(2)[:, t * E0:(t + 1) * E0], sumsq[:, t:t + 1], rb,
                                                          ALU.subtract, ALU.add)
                order.step(last)
                yield from top(logits[:], E0, "before0", TOP0, above[:], tied[:], rank[:])
                order.step(nc.vector.tensor_reduce(best[:], logits[:], AX.X, ALU.max))
                nc.vector.tensor_tensor(logits[:], logits[:], over(best[:], E0, 2), ALU.subtract).then_inc(centred, 1)
                yield

            def router_end():
                dve.wait_ge(gate_exp, 1)
                order.step(nc.vector.tensor_tensor(gate[:], gate[:], rank[:], ALU.mult))
                order.step(nc.vector.tensor_reduce(best[:], gate[:], AX.X, ALU.add))
                order.step(nc.vector.reciprocal(best[:], best[:]))
                nc.vector.tensor_tensor(gate[:], gate[:], over(best[:], E0, 2), ALU.mult).then_inc(gate_ready, 1)
                dve.wait_ge(gate_ready, 1)

            def split_hidden(e, u):
                dve.wait_ge(gelu_done, UNITS * e + (u + 1))
                if not (isinstance(e, int) and e == 0 and u < 4):
                    dve.wait_ge(down_done, UNITS * e + (u - 3))
                nc.vector.tensor_copy(h_hi[u % 4][:], h_full[u % 2][:]).then_inc(h_hi_ready, 1)
                dve.wait_ge(h_hi_ready, UNITS * e + (u + 1))
                nc.vector.tensor_tensor(h_lo[u % 4][:], h_full[u % 2][:], h_hi[u % 4][:].bitcast(F32), ALU.subtract)\
                    .then_inc(h_ready, 1)

            def combine(e, k, is_first):
                dve.wait_ge(down_done, UNITS * (e + 1))
                if not is_first:
                    dve.wait_ge(combined, e)
                for t in range(TC):
                    y = pb(4 + 2 * k + t // 2)[:, (t % 2) * D:(t % 2 + 1) * D]
                    last = nc.vector.scalar_tensor_tensor(X[:, t, :], y, gate[:, t, bass.ds(e, 1)], X[:, t, :],
                                                          ALU.mult, ALU.add)
                last.then_inc(combined, 1)

            def pair_of_experts(n, is_first):
                for k in range(2):
                    e = 2 * n + k
                    for u in range(UNITS):
                        split_hidden(e, u)
                        if is_first and k == 0 and 2 <= u < 7:
                            next(router_parts)
                        if is_first and k == 1 and u == 1:
                            router_end()
                        if u == 3 and not (is_first and k == 0):
                            combine(e - 1, 1 - k, is_first and k == 1)
                        if is_first and k == 1 and u == 7:
                            dve.wait_ge(bias_done, 1)
                            dve.wait_ge(combined, 1)
                            order.step(nc.vector.tensor_tensor(
                                X[:], X[:], banks[:, 2:4, :].rearrange("p a (t n) -> p (a t) n", n=D), ALU.add))

            dve.wait_ge(x_updated, 2)
            layer_norm(3)
            token_low(3, X_BANKS, x_hi, x_hi_ready, x_lo, x_lo_ready)
            router_parts = router()
            pair_of_experts(0, True)
            with dve.Fori(1, E0 // 2) as n:
                pair_of_experts(n, False)
            combine(E0 - 1, 1, False)
            dve.wait_ge(combined, E0)
            dve.sem_inc(x_updated, 1)

            dve.wait_ge(x_updated, 3)
            layer_norm(4)
            dve.wait_ge(xt_done, 8)
            nc.vector.tensor_copy(xnT[:, 1, P:TOK], pb(5)[:, P:TOK]).then_inc(xt1_ready, 1)

            def greatest(p):
                k = p % 2
                dve.wait_ge(scores2_done, p + 1)
                dve.wait_ge(maskneg_ready, p + 1)
                if p >= 2:
                    dve.wait_ge(turned2, 2 * (p - 1))
                order.step(nc.vector.tensor_tensor(probs2[k][:], two(k), mask[p][:].bitcast(F32), ALU.add))
                order.step(nc.vector.tensor_reduce(stat2[:, p, 0:1], probs2[k][:], AX.X, ALU.max))
                nc.vector.tensor_scalar(stat2[:, p, 0:1], stat2[:, p, 0:1], -1.0 / 16, None, ALU.mult).then_inc(max2_ready, 1)

            def left_half(p):
                dve.wait_ge(turned2, 2 * p + 1)
                if p:
                    dve.wait_ge(mixed_done, p)
                nc.vector.tensor_copy(probsT2[:, 0:KC // 2, :], pb(4).rearrange("p (k n) -> p k n", n=P)).then_inc(left2_ready, 1)

            def normalise(p):
                dve.wait_ge(exp2_done, p + 1)
                order.step(nc.vector.tensor_scalar(stat2[:, p, 1:2], stat2[:, p, 1:2], stat2[:, p, 1:2], EPS, ALU.mult, ALU.mult))
                raw, scaled = pb(6 + p % 2)[:, 0:D], xn[:, p, :]
                dve.wait_ge(mixed_done, p + 1)
                order.step(nc.vector.bn_stats(stats[:, p, :], raw))
                order.step(nc.vector.bn_aggr(moments[:, p, :], stats[:, p, :]))
                nc.vector.tensor_tensor(stat2[:, p, 2:3], moments[:, p, 1:2], stat2[:, p, 1:2], ALU.add).then_inc(pair_var_ready, 1)
                nc.vector.scalar_tensor_tensor(scaled, raw, moments[:, p, 0:1], part(rows, ROWS, "gamma"),
                                               ALU.subtract, ALU.mult).then_inc(mixed_taken, 1)
                dve.wait_ge(mixed_taken, p + 1)
                dve.wait_ge(pair_rstd_ready, p + 1)
                order.mark(nc.vector.scalar_tensor_tensor(X[:, p, :], scaled, stat2[:, p, 3:4], X[:, p, :], ALU.mult, ALU.add))

            order.step(nc.vector.tensor_tensor(X[:], X[:], over(part(rows, ROWS, "beta"), TC, 1), ALU.add))
            greatest(0)
            greatest(1)
            for p in range(TC):
                left_half(p)
                if p >= 1:
                    normalise(p - 1)
                if p + 2 < TC:
                    greatest(p + 2)
                if p >= 1:
                    order.settle()
                    norm_begin(5, p - 1)
                    norm_tile(5, p - 1)
            normalise(TC - 1)
            order.settle()
            dve.sem_inc(x_updated, 1)
            norm_begin(5, TC - 1)
            norm_tile(5, TC - 1)

            dve.wait_ge(xt_done, 10)
            nc.vector.tensor_copy(xnT[:, 1, TOK - P:TOK], pb(1)[:, TOK - P:TOK]).then_inc(xt1_ready, 1)
            conv_w = part(later, LATER, "conv_w").rearrange("p (c k) -> p c k", c=CC)
            for m in range(CC):
                dve.wait_ge(first_tap, m + 1)
                dve.wait_ge(a_ready, m + 1)
                y = hidden[m // 2][:, m % 2, :].rearrange("p (b s) -> p b s", b=B)
                for k in range(KER - 1):
                    ins = nc.vector.scalar_tensor_tensor(y, a_pad[:, m, :, k:k + S], conv_w[:, m, k:k + 1], y, ALU.mult, ALU.add)
                    if k < KER - 2:
                        order.step(ins)
                    else:
                        ins.then_inc(conv1_ready, 1)
            nc.vector.tensor_tensor(two_hot[:], ident[0:4 * NSTATE, 0:2 * NSTATE], ident[0:4 * NSTATE, 2 * NSTATE:4 * NSTATE],
                                    ALU.add).then_inc(two_hot_ready, 1)
            d_param = part(later, LATER, "d_param")
            def step_part(m):
                dve.wait_ge(abs_ready, m + 1)
                nc.vector.tensor_scalar(delta[:, m, :], pb(2 + m), d_param[:, m:m + 1], 0.0, ALU.add, ALU.max).then_inc(relu_ready, 1)

            def first_step_end(m):
                dve.wait_ge(soft_ready, m + 1)
                dve.wait_ge(relu_ready, m + 1)
                nc.vector.tensor_tensor(delta[:, m, :], delta[:, m, :], drive[:, m, :], ALU.add).then_inc(soft_taken, 1)
                dve.wait_ge(soft_taken, m + 1)
                dve.wait_ge(a_silu, m + 1)
                nc.vector.tensor_tensor(drive[:, m, :], delta[:, m, :], aT[:, m, :], ALU.mult).then_inc(drive_ready, 1)

            def rows_of_c(g):
                for s in range(GS if g < EARLY_C else 1):
                    dve.wait_ge(Cbc_done, GS * g + s + 1)
                    nc.vector.tensor_copy(Cbc[:, GS * g + s, :], pb(6 + s)).then_inc(Cbc_ready[s], 1)

            for m in range(CC):
                step_part(m)
            dve.wait_ge(bc_hi_ready, 1)
            nc.vector.tensor_tensor(bc[2 * NSTATE:4 * NSTATE, :], pb(6)[0:2 * NSTATE, :], bc[0:2 * NSTATE, :].bitcast(F32),
                                    ALU.subtract).then_inc(bc_ready, 1)
            first_step_end(0)
            for s in range(GS):
                dve.wait_ge(Bbc_done, s + 1)
                nc.vector.tensor_copy(Bbc[:, s, :], pb(s)).then_inc(Bbc_ready[s], 1)
            for g in range(EARLY_C):
                rows_of_c(g)

            def chunk(tile, m):
                return tile[:, m, :] if isinstance(m, int) else tile[:, bass.ds(m, 1), :].rearrange("p c n -> p (c n)")

            def gated(m, last=False):
                dve.wait_ge(y_ready, m + 1)
                if not isinstance(m, int) or m:
                    dve.wait_ge(gated_ready, 2 * m)
                nc.vector.scalar_tensor_tensor(acc[:], chunk(aT, m), d_param[:, bass.ds(m, 1)], pb(m + 2),
                                               ALU.mult, ALU.add).then_inc(gated_ready, 1)
                dve.wait_ge(gated_ready, 2 * m + 1)
                if last:
                    dve.wait_ge(projected, CC)
                dve.wait_ge(g_ready, m + 1)
                nc.vector.tensor_tensor(gated_sum[:], acc[:], chunk(gT, m), ALU.mult).then_inc(gated_ready, 1)

            def states(m, first_chunk):
                for g in range(GROUPS):
                    dve.wait_ge(decay_ready, GROUPS * m + (g + 1))
                    dve.wait_ge(inject_ready, GROUPS * m + (g + 1))
                    if g >= 2 or not first_chunk:
                        dve.wait_ge(shown_ready, GROUPS * m + (g - 1))
                    nc.vector.tensor_tensor_scan(hidden[g % 2][:].rearrange("p g n -> p (g n)"),
                                                 decay[g % 2][:].rearrange("p g n -> p (g n)"),
                                                 inject[g % 2][:].rearrange("p g n -> p (g n)"),
                                                 0.0, ALU.mult, ALU.add).then_inc(scanned, 1)
                    dve.wait_ge(scanned, GROUPS * m + (g + 1))
                    if first_chunk:
                        for ready in Cbc_ready:
                            dve.wait_ge(ready, g + 1)
                    if g >= 2 or not first_chunk:
                        dve.wait_ge(shown_used, GROUPS * m + (g - 1))
                    nc.vector.tensor_tensor(shown[g % 2][:], hidden[g % 2][:], Cbc[:, GS * g:GS * (g + 1), :], ALU.mult)\
                        .then_inc(shown_ready, 1)
                    if first_chunk and EARLY_C <= g + 2 < GROUPS:
                        rows_of_c(g + 2)
                    if g == 2 and not first_chunk:
                        dve.wait_ge(projected, m)
                        gated(m - 1)

            states(0, True)
            with dve.Fori(1, CC) as m:
                states(m, False)
            gated(CC - 1, True)
            for h in range(2):
                dve.wait_ge(out1_done, h + 1)
                last = nc.vector.tensor_copy(X[:, 2 * h:2 * h + 2, :], pb(6 + h).rearrange("p (t n) -> p t n", t=2))
            last.then_inc(x_updated, 1)

            dve.wait_ge(x_updated, 5)
            layer_norm(6)
            dve.sem_inc(gu_free, FB)
            token_low(6, X1_BANKS, x1_hi, x1_hi_ready, x1_lo, x1_lo_ready)

            def centre_logits():
                dve.wait_ge(logits1_done, 1)
                raw_logits = pb(6)[:, 0:TC * ROUTED1].rearrange("p (t e) -> p t e", t=TC)
                order.step(nc.vector.tensor_reduce(best1[:], raw_logits, AX.X, ALU.max))
                nc.vector.tensor_tensor(logits1[:], raw_logits, over(best1[:], ROUTED1, 2), ALU.subtract).then_inc(centred1, 1)
                nc.vector.memset(gate1[:], 1.0).then_inc(gate1_ready, 1)

            def route():
                dve.wait_ge(gate1_exp, 1)
                order.step(nc.vector.tensor_reduce(best1[:], logits1[:], AX.X, ALU.add))
                order.step(nc.vector.reciprocal(best1[:], best1[:]))
                order.step(nc.vector.tensor_tensor(logits1[:], logits1[:], over(best1[:], ROUTED1, 2), ALU.mult))
                yield from top(logits1[:], ROUTED1, "before1", TOP1, above1[:], tied1[:], rank1[:])
                dve.wait_ge(gate1_ready, 1)
                nc.vector.tensor_tensor(gate1[:, :, 0:ROUTED1], logits1[:], rank1[:], ALU.mult).then_inc(gate1_ready, 1)
                dve.wait_ge(gate1_ready, 2)

            def hidden1(n, k):
                dve.wait_ge(silu1_ready, FB * n + (k + 1))
                dve.wait_ge(down1_done, FB * n + (k + 1))
                nc.vector.tensor_tensor(hid_f[k][:], act_f[k][:], pb(2 * k + 1), ALU.mult).then_inc(hid_ready, 1)
                dve.wait_ge(hid_ready, FB * n + (k + 1))
                dve.sem_inc(gu_free, 1)

            def hidden1_low(n, k):
                dve.wait_ge(hid_hi_ready, FB * n + (k + 1))
                nc.vector.tensor_tensor(hid_lo[k][:], hid_f[k][:], hid_hi[k][:].bitcast(F32), ALU.subtract).then_inc(hid_lo_ready, 1)

            def combine1(n, k):
                dve.wait_ge(down1_done, FB * n + (FB + k + 1))
                dve.wait_ge(combined1, FB * n + (k + 1))
                for t in range(TC):
                    y = pb(6 + t // 2)[:, (t % 2) * D:(t % 2 + 1) * D]
                    last = nc.vector.scalar_tensor_tensor(X[:, t, :], y, gate1[:, t, bass.ds(FB * n + k, 1)], X[:, t, :],
                                                          ALU.mult, ALU.add)
                last.then_inc(combined1, 1)

            def after(n, k):
                return (n, k + 1) if k + 1 < FB else (n + 1, 0)

            def expert1(n, k, last=False):
                hidden1_low(n, k)
                if not last:
                    hidden1(*after(n, k))
                combine1(n, k)

            hidden1(0, 0)
            centre_logits()
            dve.wait_ge(centred1, 1)
            dve.sem_inc(combined1, 1)
            hidden1_low(0, 0)
            route_parts = route()
            next(route_parts)
            hidden1(0, 1)
            for _ in route_parts:
                pass
            combine1(0, 0)
            with dve.Fori(0, E1 // FB - 1) as n:
                for k in range(1, FB + 1):
                    expert1(*after(n, k - 1))
            for k in range(1, FB):
                expert1(E1 // FB - 1, k, k == FB - 1)
            dve.wait_ge(combined1, E1 + 1)
            dve.sem_inc(x_updated, 1)

        @block.tensor
        def _(pe):
            def mm(o, lhsT, rhs, start, stop):
                return nc.tensor.matmul(o, lhsT, rhs, start=start, stop=stop)

            def weights(tile, layout, name, parts):
                return part(tile, layout, name).rearrange("p (c n) -> p c n", c=parts)

            def transpose_tokens(k, tiles=range(TC), in_banks=(0, 1)):
                for t in tiles:
                    pe.wait_ge(xn_ready, norm_of(k, t))
                    for c in range(DC):
                        done = nc.tensor.transpose(pb(in_banks[c])[:, t * P:(t + 1) * P], xn[:, t, c * P:(c + 1) * P], ident)
                        if k == 5 and t == TC - 2 and c == DC - 1:
                            done.then_inc(early_turned, 1)
                        if t == TC - 1:
                            done.then_inc(xt_done, 1)

            pe.wait_ge(loaded["table"], 16)
            transpose_tokens(1)
            pe.wait_ge(loaded["first"], 16)
            wq = weights(first, FIRST, "wq", DC)
            pe.wait_ge(xt0_ready, 1)
            pe.wait_ge(xt1_ready, 1)
            for g in range(STACKS):
                for i in range(DC):
                    last = mm(pb(Q_BANKS[g]), wq[:, i, g * P:(g + 1) * P], xnT[:, i, :], i == 0, i == DC - 1)
                last.then_inc(q_done, 1)

            def three(o, a, b):
                passes = [(a[x][i], b[y][i]) for i in range(DC) for x, y in ((0, 0), (0, 1), (1, 0))]
                for n, (x, y) in enumerate(passes):
                    last = mm(o, x, y, n == 0, n == len(passes) - 1)
                return last

            def project_keys(piece, b, par, c, half, bank=4):
                pe.wait_ge(ctx_lo_ready, DC * b + DC)
                if not isinstance(piece, int) or piece > 2:
                    pe.wait_ge(piece_taken, 1 if isinstance(piece, int) and piece == 3 else piece - 1)
                w = [[w_kv[0][x][:, i, c * P:(c + 1) * P] for i in range(DC)] for x in range(2)]
                ctx = [[of[par][:, i, half * 512:(half + 1) * 512] for i in range(DC)] for of in (ctx_hi, ctx_lo)]
                three(pb(bank), w, ctx).then_inc(proj_done, 1)

            def project_values(piece, b, par, v):
                pe.wait_ge(piece_taken, piece - 1)
                w = [[w_kv[1][x][:, i, :] for i in range(DC)] for x in range(2)]
                for kc in (2 * v, 2 * v + 1):
                    ctx = [[of[par][:, i, kc * P:(kc + 1) * P] for i in range(DC)] for of in (ctx_hi, ctx_lo)]
                    last = three(pb(4)[:, (kc % 2) * D:(kc % 2 + 1) * D], ctx, w)
                last.then_inc(proj_done, 1)

            def turn(b, i):
                pe.wait_ge(exp_done, 8 * b + (i + 1))
                for half in range(2):
                    if not (isinstance(b, int) and b == 0 and i == 0):
                        pe.wait_ge(pt1_ready if half else pt0_ready, 8 * b + i)
                    for k in range(KC // 2):
                        kc = half * (KC // 2) + k
                        last = nc.tensor.transpose(pb(5 + half)[:, k * P:(k + 1) * P],
                                                   probs[i % 2][:, kc * P:(kc + 1) * P], ident)
                    last.then_inc(t_done, 1)

            def weigh(b, c, q):
                pe.wait_ge(piece_taken, piece_at(b, VALUES_AT[q], isinstance(b, int) and b == B - 1))
                if q == 0:
                    pe.wait_ge(pt0_ready, 8 * b + PAIRS * (c + 1))
                    pe.wait_ge(pt1_ready, 8 * b + PAIRS * (c + 1))
                    pe.wait_ge(diag_ready, DC * b + (c + 1))
                    if not (isinstance(b, int) and b == 0 and c == 0):
                        pe.wait_ge(masked_ready, DC * b + c)
                    for j in range(PAIRS):
                        mm(pb(7)[PAIR_W * j:PAIR_W * (j + 1), P:2 * P], part(table, TABLE, "pick"), inv_diag[:, j, :], True, True)
                for kc in (2 * q, 2 * q + 1):
                    for j in range(PAIRS):
                        at = c * P + PAIR_W * j
                        last = mm(pb(7)[PAIR_W * j:PAIR_W * (j + 1), 0:P], V[:, kc, at:at + PAIR_W],
                                  probsT[c][:, kc, j, :], kc == 0, kc == KC - 1)
                last.then_inc(quarter_done, 1)

            def project_out(n):
                pe.wait_ge(attn_ready, 4 * n + 4)
                wo = weights(later, LATER, "wo", DC)
                for c in range(DC):
                    last = mm(pb(7)[:, 256:512], attn[:, c, :], wo[:, c, :], c == 0, c == DC - 1)
                last.then_inc(out_done, 1)

            def project_piece(b, par, i, last):
                piece = piece_at(b, i, last)
                if i in KEYS_AT:
                    project_keys(piece, b, par, 1, KEYS_AT.index(i))
                elif i in VALUES_AT:
                    project_values(piece, b, par, VALUES_AT.index(i))
                elif not last:
                    project_keys(piece, b + 1, 1 - par, 0, NEXT_KEYS_AT.index(i))

            def batch(b, par, last, tile=None):
                later_one = not (isinstance(b, int) and b == 0)
                for i in range(8):
                    g = i // 2
                    if not later_one and i == 0:
                        project_piece(b, par, i, last)
                    pe.wait_ge(heads_ready, STACKS * b + (g + 1))
                    if g >= 2:
                        pe.wait_ge(piece_taken, piece_at(b, KEYS_AT[1]))
                    else:
                        pe.wait_ge(piece_taken, piece_at(b - 1, NEXT_KEYS_AT[1]) if later_one else 2)
                    if later_one or i >= 2:
                        pe.wait_ge(exp_done, 8 * b + (i - 1))
                    for half in range(2):
                        for n, q in enumerate(q_stack):
                            done = mm(pb(2 * (i % 2) + half), q[:, g, 2 * (i % 2):2 * (i % 2) + 2, :],
                                      k_stack[:, g, half * 512:(half + 1) * 512], n == 0, n == 1)
                    done.then_inc(scores_done, 1)
                    if later_one or i:
                        project_piece(b, par, i, last)
                    if i == 5 and tile is not None:
                        project_out(tile)
                    elif i == 0 and later_one:
                        weigh(b - 1, 0, 3)
                    elif 1 <= i < 5 and later_one:
                        weigh(b - 1, 1, i - 1)
                    elif i >= 5:
                        weigh(b, 0, i - 5)
                    if i >= 1:
                        turn(b, i - 1)
                    elif later_one:
                        turn(b - 1, 7)
                    if i == 5 and tile is not None:
                        pe.wait_ge(tile_added, tile + 2)
                        weigh(b, 0, 0)

            pe.wait_ge(w_lo_ready, 2)
            for half in range(2):
                project_keys(half + 1, 0, 0, 0, half, FIRST_BANKS[half])
            batch(0, 0, False)
            pe.wait_ge(loaded["later"], 16)
            with pe.Fori(0, B // 2 - 1) as n:
                batch(2 * n + 1, 1, False)
                batch(2 * n + 2, 0, False, n)
            batch(B - 1, 1, True)
            weigh(B - 1, 0, 3)
            turn(B - 1, 7)
            for q in range(4):
                weigh(B - 1, 1, q)
            transpose_tokens(2, range(TC - 1))
            project_out(TC - 1)
            transpose_tokens(2, [TC - 1])
            for h in range(2):
                for t in (2 * h, 2 * h + 1):
                    for c in range(DC):
                        pe.wait_ge(silu_ready, c + 1)
                        last = nc.tensor.transpose(pb(2 + h)[:, (t % 2) * D + c * P:(t % 2) * D + (c + 1) * P],
                                                   conv[1][:, c, t * P:(t + 1) * P], ident)
                last.then_inc(back_done, 1)

            transpose_tokens(3, in_banks=X_BANKS)
            pe.wait_ge(x_lo_ready, DC)

            def up(e, k, u):
                if u == 0:
                    pe.wait_ge(lo_done, 4 * e + 2)
                if not (isinstance(e, int) and e == 0 and u < 2):
                    pe.wait_ge(gelu_done, UNITS * e + (u - 1))
                passes = []
                for c in range(DC):
                    cols = slice(c * F0 + u * P, c * F0 + (u + 1) * P)
                    passes += [(w_hi[k][:, cols], x_hi[:, c, :]), (w_hi[k][:, cols], x_lo[:, c, :]),
                               (w_lo[k][:, cols], x_hi[:, c, :])]
                for i, (w, x) in enumerate(passes):
                    last = mm(pb(u % 2), w, x, i == 0, i == len(passes) - 1)
                last.then_inc(up_done, 1)

            def down(e, k, u):
                pe.wait_ge(h_ready, UNITS * e + (u + 1))
                if u == 0:
                    pe.wait_ge(lo_done, 4 * e + 4)
                    if not (isinstance(e, int) and e < 2):
                        pe.wait_ge(combined, e - 1)
                cols = slice(EW // 2 + u * D, EW // 2 + (u + 1) * D)
                for t in range(TC):
                    tok = slice(t * P, (t + 1) * P)
                    o = pb(4 + 2 * k + t // 2)[:, (t % 2) * D:(t % 2 + 1) * D]
                    passes = [(h_hi[u % 4][:, tok], w_hi[k][:, cols]), (h_hi[u % 4][:, tok], w_lo[k][:, cols]),
                              (h_lo[u % 4][:, tok], w_hi[k][:, cols])]
                    for i, (h, w) in enumerate(passes):
                        last = mm(o, h, w, u == 0 and i == 0 and t % 2 == 0, u == UNITS - 1 and i == 2 and t % 2 == 1)
                last.then_inc(down_done, 1)

            def route():
                pe.wait_ge(keys_ready, 2)
                pe.wait_ge(xt0_ready, 3)
                pe.wait_ge(xt1_ready, 3)
                for t in range(TC):
                    for c in range(DC):
                        mm(pb(2)[:, t * E0:(t + 1) * E0], xnT[:, c, t * P:(t + 1) * P], key_sum[:, c, :], c == 0, c == DC - 1)
                for c in range(DC):
                    last = mm(pb(2)[:, TC * E0:(TC + 1) * E0], ones, key_sq[:, c, :], c == 0, c == DC - 1)
                last.then_inc(logits_done, 1)

            def pair_of_experts(n, is_first, is_last):
                for k in range(2):
                    e = 2 * n + k
                    for u in range(UNITS):
                        if u + 2 < UNITS:
                            up(e, k, u + 2)
                        elif not (is_last and k):
                            up(e + 1, 1 - k, u + 2 - UNITS)
                        down(e, k, u)
                        if is_first and k == 0 and u == 0:
                            route()
                        if is_first and k == 1 and u == 2:
                            pe.wait_ge(gate_ready, 1)
                            for t in range(TC):
                                last = nc.tensor.transpose(pb(3)[0:E0, t * P:(t + 1) * P], gate[:, t, :], ident)
                            last.then_inc(gate_turned, 1)
                        if is_first and k == 1 and u == 5:
                            pe.wait_ge(gateT_ready, 1)
                            pe.wait_ge(loaded["b2"], 16)
                            for t in range(TC):
                                last = mm(pb(2 + t // 2)[:, (t % 2) * D:(t % 2 + 1) * D], gateT[:, t, :], b2[:], True, True)
                            last.then_inc(bias_done, 1)

            up(0, 0, 0)
            up(0, 0, 1)
            pair_of_experts(0, True, False)
            with pe.Fori(1, E0 // 2 - 1) as n:
                pair_of_experts(n, False, False)
            pair_of_experts(E0 // 2 - 1, False, True)

            pe.wait_ge(xn_ready, norm_of(4, 0))
            for c in range(DC):
                last = nc.tensor.transpose(pb(7)[:, c * P:(c + 1) * P], xn[:, 0, c * P:(c + 1) * P], ident)
            last.then_inc(early_turned, 1)
            pe.wait_ge(early_ready, 1)

            def score2(p):
                k = p % 2
                pe.wait_ge(ctxT2_loaded[p], 16)
                if p >= 2:
                    pe.wait_ge(max2_ready, p - 1)
                if p == 1:
                    pe.wait_ge(xt0_ready, 4)
                    pe.wait_ge(xt1_ready, 4)
                for half in range(2):
                    if p == 0 and half:
                        transpose_tokens(4, range(1, TC), (4, 5))
                    for c in range(DC):
                        for b in range(2):
                            last = mm(pb(2 * k + half)[64 * b:64 * b + 64, :], xnT[:, c, p * P + S * b:p * P + S * (b + 1)],
                                      ctxT2[p][:, b, c, half * 512:(half + 1) * 512], c == 0, c == DC - 1)
                last.then_inc(scores2_done, 1)

            def turn2(p):
                pe.wait_ge(exp2_done, p + 1)
                for half in range(2):
                    if p:
                        pe.wait_ge(right2_ready if half else left2_ready, p)
                    for j in range(KC // 2):
                        kc = half * (KC // 2) + j
                        last = nc.tensor.transpose(pb(4 + half)[:, j * P:(j + 1) * P], probs2[p % 2][:, kc * P:(kc + 1) * P], ident)
                    last.then_inc(turned2, 1)

            def mix2(p):
                pe.wait_ge(ctxN2_loaded[p], 16)
                pe.wait_ge(left2_ready, p + 1)
                pe.wait_ge(right2_ready, p + 1)
                if p >= 2:
                    pe.wait_ge(mixed_taken, p - 1)
                for kc in range(KC):
                    for b in range(2):
                        last = mm(pb(6 + p % 2)[64 * b:64 * b + 64, 0:D], probsT2[:, kc, S * b:S * (b + 1)], ctxN2[p][:, b, kc, :],
                                  kc == 0, kc == KC - 1)
                last.then_inc(mixed_done, 1)

            score2(0)
            score2(1)
            turn2(0)
            for p in range(TC):
                if p + 2 < TC:
                    score2(p + 2)
                mix2(p)
                if p + 1 < TC:
                    turn2(p + 1)

            w_in = weights(later, LATER, "w_in", DC)

            def project_in(o, m, cols=slice(0, TOK)):
                for c in range(DC):
                    last = mm(o[:, cols], w_in[:, c, m * P:(m + 1) * P], xnT[:, c, cols], c == 0, c == DC - 1)
                return last

            transpose_tokens(5, range(TC - 1))
            pe.wait_ge(early_ready, 1 + DC)
            for m in range(EARLY_IN):
                project_in(pb(2 + m), m, slice(0, TOK - P))
            transpose_tokens(5, [TC - 1])
            pe.wait_ge(xt0_ready, 5)
            pe.wait_ge(xt1_ready, 5)
            for m in range(CC):
                project_in(pb(2 + m), m, slice(TOK - P if m < EARLY_IN else 0, TOK)).then_inc(ag_done, 1)
            w_sd1, w_sbc = weights(later, LATER, "w_sd1", CC), weights(later, LATER, "w_sbc", CC)

            def project_low(m):
                pe.wait_ge(a_silu, m + 1)
                return mm(pb(7), w_sd1[:, m, :], aT[:, m, :], m == 0, m == CC - 1)

            def project_bc(m):
                return mm(pb(6)[0:2 * NSTATE, :], w_sbc[:, m, :], aT[:, m, :], m == 0, m == CC - 1)

            project_low(0)
            project_bc(0)
            project_low(1)
            project_low(2)
            project_bc(1)
            project_low(3).then_inc(low_done, 1)
            project_bc(2)
            pe.wait_ge(low_ready, 1)
            w_sd2 = part(later, LATER, "w_sd2")
            for m in range(CC):
                pe.wait_ge(a_ready, m + 1)
                mm(pb(2 + m), w_sd2[:, m * P:(m + 1) * P], lowT[:], True, True).then_inc(step_done, 1)
            project_bc(3).then_inc(bc_done, 1)

            def project_gate(m):
                if G_BANKS[m] >= 2:
                    pe.wait_ge(relu_ready, G_BANKS[m] - 1)
                else:
                    pe.wait_ge(Bbc_ready[G_BANKS[m]], GROUPS)
                project_in(pb(G_BANKS[m]), CC + m).then_inc(gates_done, 1)

            for m in range(CC - 1):
                project_gate(m)
            pe.wait_ge(bc_ready, 1)
            pe.wait_ge(two_hot_ready, 1)

            def broadcast(row, o):
                return mm(o, two_hot[:, row:row + 1].broadcast_to([4 * NSTATE, P]), bc[:], True, True)

            def broadcast_b(g):
                for s in range(GS):
                    if g:
                        pe.wait_ge(Bbc_ready[s], g)
                    broadcast(GS * g + s, pb(s)).then_inc(Bbc_done, 1)

            def broadcast_c(g):
                for s in range(GS):
                    if g:
                        pe.wait_ge(Cbc_ready[s], g)
                    broadcast(NSTATE + GS * g + s, pb(6 + s)).then_inc(Cbc_done, 1)

            def sum_states(m, g):
                pe.wait_ge(shown_ready, GROUPS * m + (g + 1))
                for s in range(GS):
                    last = mm(pb(m + 2), ident, shown[g % 2][:, s, :], g == 0 and s == 0, g == GROUPS - 1 and s == GS - 1)
                last.then_inc(shown_used, 1)
                if g == GROUPS - 1:
                    pe.wait_ge(shown_used, GROUPS * (m + 1))
                    pe.sem_inc(y_ready, 1)

            w_out = weights(later, LATER, "w_out", CC).rearrange("p c n -> p (c n)")

            def project_out1(m, last):
                pe.wait_ge(gated_ready, 2 * m + 2)
                for t in range(TC):
                    done = mm(pb(6 + t // 2)[:, (t % 2) * D:(t % 2 + 1) * D], gated_sum[:, t * P:(t + 1) * P],
                              w_out[:, bass.ds(m * D, D)], False, last and t % 2 == 1)
                    if last and t % 2:
                        done.then_inc(out1_done, 1)
                if not last:
                    done.then_inc(projected, 1)

            for g in range(EARLY_B):
                broadcast_b(g)
                if g < EARLY_C:
                    broadcast_c(g)
            for g in range(GROUPS):
                if g + EARLY_B < GROUPS:
                    broadcast_b(g + EARLY_B)
                if g == GROUPS - EARLY_B + 1:
                    project_gate(CC - 1)
                if g + EARLY_C < GROUPS:
                    broadcast_c(g + EARLY_C)
                sum_states(0, g)
            for ready in Cbc_ready:
                pe.wait_ge(ready, GROUPS)
            for t in range(TC):
                last = mm(pb(6 + t // 2)[:, (t % 2) * D:(t % 2 + 1) * D], ident, X[:, t, :], t % 2 == 0, False)
            last.then_inc(projected, 1)
            with pe.Fori(1, CC) as m:
                for g in range(GROUPS):
                    sum_states(m, g)
                    if g == 3:
                        project_out1(m - 1, False)
            project_out1(CC - 1, True)

            transpose_tokens(6, in_banks=X1_BANKS)

            def gate_up(n, k):
                pe.wait_ge(f_lo_ready, FB * n + (k + 1))
                pe.wait_ge(gu_free, FB * n + (k + 1))
                for g in range(2):
                    w = [[of[k][:, (g * DC + c) * P:(g * DC + c + 1) * P] for c in range(DC)] for of in (f_hi, f_lo)]
                    last = three(pb(2 * k + g), w, [[of[:, c, :] for c in range(DC)] for of in (x1_hi, x1_lo)])
                last.then_inc(gu_done, 1)

            def down1(n, k):
                pe.wait_ge(hid_lo_ready, FB * n + (k + 1))
                pe.wait_ge(combined1, FB * n + (k + 1))
                for t in range(TC):
                    tok = slice(t * P, (t + 1) * P)
                    hi, lo, w_hi_, w_lo_ = hid_hi[k][:, tok], hid_lo[k][:, tok], f_hi[k][:, 2 * D:3 * D], f_lo[k][:, 2 * D:3 * D]
                    for i, (h, w) in enumerate(((hi, w_hi_), (hi, w_lo_), (lo, w_hi_))):
                        last = mm(pb(6 + t // 2)[:, (t % 2) * D:(t % 2 + 1) * D], h, w, i == 0, i == 2)
                last.then_inc(down1_done, 1)

            def three_experts(n, last):
                for k in range(FB):
                    if k + 1 < FB:
                        gate_up(n, k + 1)
                    elif not last:
                        gate_up(n + 1, 0)
                    down1(n, k)

            pe.sem_inc(down1_done, FB)
            pe.wait_ge(x1_lo_ready, DC)
            gate_up(0, 0)
            pe.wait_ge(xt0_ready, 6)
            pe.wait_ge(xt1_ready, 6)
            gate_w = weights(later, LATER, "gate_w", DC)
            for t in range(TC):
                for c in range(DC):
                    last = mm(pb(6)[:, t * ROUTED1:(t + 1) * ROUTED1], xnT[:, c, t * P:(t + 1) * P], gate_w[:, c, :],
                              c == 0, c == DC - 1)
            last.then_inc(logits1_done, 1)
            with pe.Fori(0, E1 // FB - 1) as n:
                three_experts(n, False)
            three_experts(E1 // FB - 1, True)


def _tables():
    t = np.zeros((P, TABLE_W), np.float32)

    def put(name, value):
        a, b = TABLE[name]
        t[:, a:b] = np.asarray(value, np.float64).reshape(P, b - a) if np.ndim(value) > 1 else value

    p = np.arange(P)
    put("ident", np.eye(P))
    pick = p[None, :PAIR_W] // DH == p[:, None] // S
    put("pick", pick)
    put("quad", p[:, None] % 64 // DH == np.arange(4))
    for name, n in (("before0", E0), ("before1", ROUTED1)):
        put(name, (np.arange(n)[None, :] < np.arange(n)[:, None]).ravel())
    omega = np.exp(-2j * np.pi * np.arange(MODES) / B)
    omega[MODES - 1] = -1.0
    put("ar", (2 * (1 - omega)).real)
    put("ai", (2 * (1 - omega)).imag)
    put("cr", (1 + omega).real)
    put("ci", (1 + omega).imag)
    often = np.array([1, 2, 2, 2, 1]) * 2 / B
    turn = 2 * np.pi * np.outer(np.arange(B), np.arange(MODES)) / B
    put("alpha", (often * np.cos(turn)).ravel())
    beta = -often * np.sin(turn)
    beta[:, [0, MODES - 1]] = 0
    put("beta", beta.ravel())
    put("ones", np.ones(P))
    put("minus_half", np.full(TC, -0.5))
    put("minus_one", np.full(DC * MODES, -1.0))
    return t


def _layouts(x, ctx_1024, mask_BxSxS2_ik1, **w):
    g = {k: np.asarray(v) for k, v in w.items()}

    def rows_in(m):
        m = m.reshape(m.shape[0] // P, P, -1)
        return np.ascontiguousarray(m.transpose(1, 0, 2)).reshape(P, -1)

    def weight(name):
        return rows_in(g[name].T)

    def side(layout, values):
        return np.ascontiguousarray(np.concatenate([values[n].reshape(P, -1) for n in layout], axis=1))

    out = {"x": np.asarray(x).reshape(TOK, D)}
    ctx = np.asarray(ctx_1024)
    out["ctxT"] = np.ascontiguousarray(ctx.transpose(0, 2, 1).reshape(B, DC, P, KEYS).transpose(0, 2, 1, 3))
    out["ctxN"] = np.ascontiguousarray(ctx.reshape(B, KC, P, D).transpose(0, 2, 1, 3))
    out["mask"] = np.asarray(mask_BxSxS2_ik1).reshape(TOK, KEYS)
    out["first"] = side(FIRST, {
        "wq": weight("L0_xattn_w_q").reshape(P, DC, STACKS, 1, 64).repeat(2, axis=3), "wk": weight("L0_xattn_w_k"), "wv": weight("L0_xattn_w_v"),
        "bq": g["L0_xattn_b_q"].reshape(STACKS, 1, 64).repeat(2, axis=1).reshape(STACKS, P).T, "bk": rows_in(g["L0_xattn_b_k"])})
    out["table"] = _tables()
    b1 = g["L0_ffn_b1"].reshape(E0, FC, P).transpose(2, 0, 1)
    sbc = np.concatenate([g["L1_attn_W_sB"], g["L1_attn_W_sC"]], axis=0)
    out["later"] = side(LATER, {
        "wo": weight("L0_xattn_w_o"), "log_dt": rows_in(g["L0_attn_log_dt"]), "inv_w": rows_in(g["L0_attn_inv_w_real"]),
        "w_im": rows_in(g["L0_attn_w_imaginary"]), "B": rows_in(g["L0_attn_B"]), "P": rows_in(g["L0_attn_P"][0]),
        "C": rows_in(g["L0_attn_C"]), "D": rows_in(g["L0_attn_D"]), "keys": weight("L0_ffn_keys"),
        "rw": weight("L0_ffn_rw"), "b1": np.ascontiguousarray(b1), "w_in": weight("L1_attn_W_in"),
        "w_sbc": rows_in(sbc.T), "w_sd1": weight("L1_attn_W_sD1"), "w_sd2": weight("L1_attn_W_sD2"),
        "conv_w": rows_in(g["L1_attn_conv_w"]), "conv_b": rows_in(g["L1_attn_conv_b"]),
        "a_param": rows_in(g["L1_attn_A_param"]), "d_param": rows_in(g["L1_attn_D_param"]),
        "w_out": weight("L1_attn_W_out"), "gate_w": weight("L1_ffn_gate_w")})
    row = np.concatenate([g["L0_xattn_b_v"], g["L0_xattn_b_o"], g["L1_xattn_gamma"], g["L1_xattn_beta"], g["L0_ffn_rb"]])
    out["rows"] = np.ascontiguousarray(np.broadcast_to(row, (P, ROWS_W)))
    out["b2"] = g["L0_ffn_b2"]
    w1 = g["L0_ffn_w1"].transpose(0, 2, 1).reshape(E0, DC, P, F0).transpose(0, 2, 1, 3).reshape(E0, P, -1)
    w2 = g["L0_ffn_w2"].transpose(0, 2, 1).reshape(E0, FC, P, D).transpose(0, 2, 1, 3).reshape(E0, P, -1)
    out["w0"] = np.ascontiguousarray(np.concatenate([w1, w2], axis=2))
    up = np.stack([np.concatenate([g["L1_ffn_wg"], g["L1_ffn_sg"][None]]),
                   np.concatenate([g["L1_ffn_wu"], g["L1_ffn_su"][None]])], axis=1)
    up = up.transpose(0, 3, 1, 2).reshape(E1, DC, P, 2, P).transpose(0, 2, 3, 1, 4).reshape(E1, P, -1)
    down = np.concatenate([g["L1_ffn_wd"], g["L1_ffn_sd"][None]]).transpose(0, 2, 1)
    out["w1"] = np.ascontiguousarray(np.concatenate([up, down], axis=2))
    return out


def kernel(**inputs):
    import concourse.bacc as bacc
    from concourse.bass_utils import run_bass_kernel_spmd

    arrays = _layouts(**inputs)
    nc = bacc.Bacc("TRN2", target_bir_lowering=False, num_devices=1)
    drams = {n: nc.dram_tensor(f"in_{n}", a.shape, mybir.dt.from_np(a.dtype), kind="ExternalInput").ap()
             for n, a in arrays.items()}
    out = nc.dram_tensor("out", (TOK, D), F32, kind="ExternalOutput").ap()
    build(nc, drams, out)
    r = run_bass_kernel_spmd(nc, [{f"in_{n}": a for n, a in arrays.items()}], core_ids=[0])
    return r.results[0]["out"].reshape(B, S, D)
```
